# Optimizing a Trainium2 kernel written in Bass

```python
import numpy as np
import jax
import jax.numpy as jnp

def _softmax(x, axis=-1):
    return jax.nn.softmax(x, axis=axis)

def _gelu(x):
    return jax.nn.gelu(x, approximate=True)

def _silu(x):
    return jax.nn.silu(x)

def _sigmoid(x):
    return jax.nn.sigmoid(x)

def _layernorm(x, axis=-1, eps=1e-05):
    m = jnp.mean(x, axis=axis, keepdims=True)
    v = jnp.var(x, axis=axis, keepdims=True)
    return (x - m) / jnp.sqrt(v + eps)

def _scatter_add(tgt, idx, src, axis=0):
    return tgt.at[idx].add(src)

def _segment_sum(src, seg, n):
    return jax.ops.segment_sum(src, seg, n)
kernel_name = 'mk_xattn_ffn_d2_seqx_r8_e28665'

def setup_inputs(seed: int=0):
    np.random.seed(seed)
    _w = jnp.asarray

    def _rec_inputs():
        import jax
        import jax.numpy as jnp
        _rk = jax.random.key(seed)
        x = -0.000125 + 0.9999 * jax.random.normal(jax.random.fold_in(_rk, 1), (8, 256, 256), jnp.float32)
        _lenS = 256 - jax.random.randint(jax.random.fold_in(_rk, 7), (8,), 0, max(1, 256 // 4) + 1, jnp.int32)
        _lenS2 = 64 - jax.random.randint(jax.random.fold_in(_rk, 8), (8,), 0, max(1, 64 // 4) + 1, jnp.int32)
        _ctx_2048P = jax.random.normal(jax.random.fold_in(_rk, 11), (8, 16, 256), jnp.float32)
        _ctx_2048c = jax.random.dirichlet(jax.random.fold_in(_rk, 511), 0.3 * jnp.ones((16,), jnp.float32), (8, 64))
        _ctx_2048t = jnp.einsum('bsk,bkd->bsd', _ctx_2048c, _ctx_2048P)
        _ctx_2048t = _ctx_2048t * jax.lax.rsqrt(jnp.mean(jnp.square(_ctx_2048t)) + 1e-12) * 0.953939
        ctx_2048 = -0.000514642 + 1.00011 * (_ctx_2048t + 0.3 * jax.random.normal(jax.random.fold_in(_rk, 611), (8, 64, 256), jnp.float32))
        _validS = jnp.arange(256)[None, :] < _lenS[:, None]
        _validS2 = jnp.arange(64)[None, :] < _lenS2[:, None]
        _causal = jnp.tril(jnp.ones((256, 256), dtype=bool))
        mask_BxS2_bk0 = jnp.logical_not(jnp.broadcast_to(_validS2[:, :], (8, 64)))
        return (x, ctx_2048, mask_BxS2_bk0)
    x, ctx_2048, mask_BxS2_bk0 = _rec_inputs()

    def _L0_xattn_setup():
        import jax, jax.numpy as jnp
        import numpy as np
        key = jax.random.key(seed)
        k1, k2, k3 = jax.random.split(key, 3)
        B, S, D, M = (8, 256, 256, 128)
        hidden_states = jax.random.normal(k1, (B, S, D), dtype=jnp.float32)
        memory_tokens = jax.random.normal(k2, (B, M, D), dtype=jnp.float32)
        memory_mask = jax.random.randint(k3, (B, M), 0, 2).astype(jnp.bool_)
        return {'hidden_states': hidden_states, 'memory_tokens': memory_tokens, 'memory_mask': memory_mask}
    _L0_xattn_all = _L0_xattn_setup()
    _L0_xattn_in = {k: v for k, v in _L0_xattn_all.items() if k in ()}
    del _L0_xattn_all

    def _L0_ffn_setup():
        import jax, jax.numpy as jnp
        import numpy as np
        BLOCK_SIZE = 32
        FP4_GRID = jnp.array([0.0, 0.5, 1.0, 1.5, 2.0, 3.0, 4.0, 6.0], dtype=jnp.float32)
        FP4_MIDS = jnp.array([0.25, 0.75, 1.25, 1.75, 2.5, 3.5, 5.0], dtype=jnp.float32)

        def quantize_to_mxfp4(w, block_size=BLOCK_SIZE):
            K, N = w.shape
            wb = w.reshape(K // block_size, block_size, N)
            amax = jnp.max(jnp.abs(wb), axis=1, keepdims=True)
            exp = jnp.floor(jnp.log2(jnp.maximum(amax, 1e-30))) - 2.0
            scales = jnp.exp2(exp)
            x = wb / scales
            idx = jnp.digitize(jnp.abs(x), FP4_MIDS)
            q = jnp.sign(x) * FP4_GRID[idx]
            return (q, scales)

        def mxfp4_matmul(inputs, q, scales, block_size=BLOCK_SIZE):
            K = inputs.shape[-1]
            N = q.shape[-1]
            w = (q * scales).reshape(K, N)
            return inputs @ w
        key = jax.random.key(seed)
        ks = jax.random.split(key, 3)
        B, S, D, F = (4, 256, 256, 1024)
        inputs = jax.random.normal(ks[0], (B, S, D), dtype=jnp.float32)
        up_kernel = jax.random.normal(ks[1], (D, F), dtype=jnp.float32) * (1.0 / np.sqrt(D))
        down_kernel = jax.random.normal(ks[2], (F, D), dtype=jnp.float32) * (1.0 / np.sqrt(F))
        up_bias = jnp.zeros((F,), dtype=jnp.float32)
        down_bias = jnp.zeros((D,), dtype=jnp.float32)
        return {'inputs': inputs, 'up_kernel': up_kernel, 'up_bias': up_bias, 'down_kernel': down_kernel, 'down_bias': down_bias}
    _L0_ffn_all = _L0_ffn_setup()
    _L0_ffn_in = {k: v for k, v in _L0_ffn_all.items() if k in ('up_kernel', 'up_bias', 'down_kernel', 'down_bias')}
    del _L0_ffn_all

    def _L1_xattn_setup():
        import jax, jax.numpy as jnp
        import numpy as np
        HIDDEN = 256
        NUM_HEADS = 16
        NUM_KV_HEADS = 4
        HEAD_DIM = 128
        ROPE_THETA = 10000.0
        EPS = 1e-06

        def rms_norm(x, w, eps=EPS):
            var = jnp.mean(jnp.square(x), axis=-1, keepdims=True)
            return x * jax.lax.rsqrt(var + eps) * w

        def rope_cache(L, head_dim, theta, dtype):
            inv_freq = 1.0 / theta ** (jnp.arange(0, head_dim, 2, dtype=jnp.float32) / head_dim)
            t = jnp.arange(L, dtype=jnp.float32)
            freqs = jnp.outer(t, inv_freq)
            emb = jnp.concatenate([freqs, freqs], -1)
            cos = jnp.cos(emb).astype(dtype)[None, :, None, :]
            sin = jnp.sin(emb).astype(dtype)[None, :, None, :]
            return (cos, sin)

        def rotate_half(x):
            x1, x2 = jnp.split(x, 2, axis=-1)
            return jnp.concatenate([-x2, x1], axis=-1)
        key = jax.random.key(seed)
        ks = jax.random.split(key, 10)
        B, L, T = (2, 256, 64)
        q_out = NUM_HEADS * HEAD_DIM
        kv_out = NUM_KV_HEADS * HEAD_DIM
        s = lambda fan_in: 1.0 / np.sqrt(fan_in)
        return {'x': jax.random.normal(ks[0], (B, L, HIDDEN), jnp.float32), 'h_ctx_kv': jax.random.normal(ks[1], (B, T, HIDDEN), jnp.float32), 'wq': jax.random.normal(ks[2], (HIDDEN, q_out), jnp.float32) * s(HIDDEN), 'wk': jax.random.normal(ks[3], (HIDDEN, kv_out), jnp.float32) * s(HIDDEN), 'wv': jax.random.normal(ks[4], (HIDDEN, kv_out), jnp.float32) * s(HIDDEN), 'wo': jax.random.normal(ks[5], (q_out, HIDDEN), jnp.float32) * s(q_out), 'wk_ctx': jax.random.normal(ks[6], (HIDDEN, kv_out), jnp.float32) * s(HIDDEN), 'wv_ctx': jax.random.normal(ks[7], (HIDDEN, kv_out), jnp.float32) * s(HIDDEN), 'q_norm_w': jnp.ones((HEAD_DIM,), jnp.float32), 'k_norm_w': jnp.ones((HEAD_DIM,), jnp.float32)}
    _L1_xattn_all = _L1_xattn_setup()
    _L1_xattn_in = {k: v for k, v in _L1_xattn_all.items() if k in ('wq', 'wk', 'wv', 'wo', 'wk_ctx', 'wv_ctx', 'q_norm_w', 'k_norm_w')}
    del _L1_xattn_all

    def _L1_ffn_setup():
        import jax, jax.numpy as jnp
        import numpy as np
        TURBO_BLOCK_SIZE = 64
        TURBO_MSE_BITS = 5
        QMAX = 2 ** (TURBO_MSE_BITS - 1) - 1
        SHRINKS = np.linspace(0.4, 1.0, 16)

        def mse_quant_dequant(w):
            O, I = w.shape
            wb = w.reshape(O, I // TURBO_BLOCK_SIZE, TURBO_BLOCK_SIZE)
            amax = jnp.max(jnp.abs(wb), axis=-1, keepdims=True)
            base = jnp.maximum(amax, 1e-08) / QMAX
            best_err = jnp.full(amax.shape, jnp.inf, dtype=w.dtype)
            best_scale = base
            for s in SHRINKS:
                scale = base * jnp.asarray(s, dtype=w.dtype)
                deq = jnp.clip(jnp.round(wb / scale), -QMAX, QMAX) * scale
                err = jnp.sum((deq - wb) ** 2, axis=-1, keepdims=True)
                upd = err < best_err
                best_err = jnp.where(upd, err, best_err)
                best_scale = jnp.where(upd, scale, best_scale)
            deq = jnp.clip(jnp.round(wb / best_scale), -QMAX, QMAX) * best_scale
            return deq.reshape(O, I)

        def turbo_linear(x, w):
            wq = w + jax.lax.stop_gradient(mse_quant_dequant(w) - w)
            return x @ wq.T
        key = jax.random.key(seed)
        k1, k2, k3 = jax.random.split(key, 3)
        dim, mlp_mult = (256, 4)
        hidden = mlp_mult * dim
        x = jax.random.normal(k1, (4, 256, dim), dtype=jnp.float32)
        w_fc = jax.random.normal(k2, (hidden, dim), dtype=jnp.float32) * 0.02
        w_proj = jax.random.normal(k3, (dim, hidden), dtype=jnp.float32) * 0.02
        return {'x': x, 'w_fc': w_fc, 'w_proj': w_proj}
    _L1_ffn_all = _L1_ffn_setup()
    _L1_ffn_in = {k: v for k, v in _L1_ffn_all.items() if k in ('w_fc', 'w_proj')}
    del _L1_ffn_all
    return {'x': x, 'ctx_2048': ctx_2048, 'mask_BxS2_bk0': mask_BxS2_bk0, 'L0_ffn_up_kernel': _L0_ffn_in['up_kernel'], 'L0_ffn_up_bias': _L0_ffn_in['up_bias'], 'L0_ffn_down_kernel': _L0_ffn_in['down_kernel'], 'L0_ffn_down_bias': _L0_ffn_in['down_bias'], 'L1_xattn_wq': _L1_xattn_in['wq'], 'L1_xattn_wk': _L1_xattn_in['wk'], 'L1_xattn_wv': _L1_xattn_in['wv'], 'L1_xattn_wo': _L1_xattn_in['wo'], 'L1_xattn_wk_ctx': _L1_xattn_in['wk_ctx'], 'L1_xattn_wv_ctx': _L1_xattn_in['wv_ctx'], 'L1_xattn_q_norm_w': _L1_xattn_in['q_norm_w'], 'L1_xattn_k_norm_w': _L1_xattn_in['k_norm_w'], 'L1_ffn_w_fc': _L1_ffn_in['w_fc'], 'L1_ffn_w_proj': _L1_ffn_in['w_proj']}

def reference(x, ctx_2048, mask_BxS2_bk0, L0_ffn_up_kernel, L0_ffn_up_bias, L0_ffn_down_kernel, L0_ffn_down_bias, L1_xattn_wq, L1_xattn_wk, L1_xattn_wv, L1_xattn_wo, L1_xattn_wk_ctx, L1_xattn_wv_ctx, L1_xattn_q_norm_w, L1_xattn_k_norm_w, L1_ffn_w_fc, L1_ffn_w_proj):
    import jax
    import jax.numpy as jnp

    def _L0_xattn_ref(hidden_states, memory_tokens, memory_mask):
        import jax, jax.numpy as jnp
        import numpy as np
        B, S, D = hidden_states.shape
        scale = 1.0 / jnp.sqrt(jnp.asarray(D, hidden_states.dtype))
        scores = jnp.einsum('bsd,bmd->bsm', hidden_states, memory_tokens) * scale
        neg_inf = jnp.asarray(-1e+30, scores.dtype)
        scores = jnp.where(memory_mask[:, None, :], scores, neg_inf)
        attn = jax.nn.softmax(scores, axis=-1)
        readout = jnp.einsum('bsm,bmd->bsd', attn, memory_tokens)
        valid_b = jnp.any(memory_mask, axis=-1)
        out = jnp.where(valid_b[:, None, None], readout, jnp.zeros_like(readout))
        return out

    def _L0_ffn_ref(inputs, up_kernel, up_bias, down_kernel, down_bias):
        import jax, jax.numpy as jnp
        import numpy as np
        BLOCK_SIZE = 32
        FP4_GRID = jnp.array([0.0, 0.5, 1.0, 1.5, 2.0, 3.0, 4.0, 6.0], dtype=jnp.float32)
        FP4_MIDS = jnp.array([0.25, 0.75, 1.25, 1.75, 2.5, 3.5, 5.0], dtype=jnp.float32)

        def quantize_to_mxfp4(w, block_size=BLOCK_SIZE):
            K, N = w.shape
            wb = w.reshape(K // block_size, block_size, N)
            amax = jnp.max(jnp.abs(wb), axis=1, keepdims=True)
            exp = jnp.floor(jnp.log2(jnp.maximum(amax, 1e-30))) - 2.0
            scales = jnp.exp2(exp)
            x = wb / scales
            idx = jnp.digitize(jnp.abs(x), FP4_MIDS)
            q = jnp.sign(x) * FP4_GRID[idx]
            return (q, scales)

        def mxfp4_matmul(inputs, q, scales, block_size=BLOCK_SIZE):
            K = inputs.shape[-1]
            N = q.shape[-1]
            w = (q * scales).reshape(K, N)
            return inputs @ w
        q_up, s_up = quantize_to_mxfp4(up_kernel, BLOCK_SIZE)
        x = mxfp4_matmul(inputs, q_up, s_up, BLOCK_SIZE) + up_bias
        x = jax.nn.gelu(x)
        q_dn, s_dn = quantize_to_mxfp4(down_kernel, BLOCK_SIZE)
        x = mxfp4_matmul(x, q_dn, s_dn, BLOCK_SIZE) + down_bias
        return x

    def _L1_xattn_ref(x, h_ctx_kv, wq, wk, wv, wo, wk_ctx, wv_ctx, q_norm_w, k_norm_w):
        import jax, jax.numpy as jnp
        import numpy as np
        HIDDEN = 256
        NUM_HEADS = 16
        NUM_KV_HEADS = 4
        HEAD_DIM = 128
        ROPE_THETA = 10000.0
        EPS = 1e-06

        def rms_norm(x, w, eps=EPS):
            var = jnp.mean(jnp.square(x), axis=-1, keepdims=True)
            return x * jax.lax.rsqrt(var + eps) * w

        def rope_cache(L, head_dim, theta, dtype):
            inv_freq = 1.0 / theta ** (jnp.arange(0, head_dim, 2, dtype=jnp.float32) / head_dim)
            t = jnp.arange(L, dtype=jnp.float32)
            freqs = jnp.outer(t, inv_freq)
            emb = jnp.concatenate([freqs, freqs], -1)
            cos = jnp.cos(emb).astype(dtype)[None, :, None, :]
            sin = jnp.sin(emb).astype(dtype)[None, :, None, :]
            return (cos, sin)

        def rotate_half(x):
            x1, x2 = jnp.split(x, 2, axis=-1)
            return jnp.concatenate([-x2, x1], axis=-1)
        B, L, _ = x.shape
        T = h_ctx_kv.shape[1]
        rep = NUM_HEADS // NUM_KV_HEADS
        q = (x @ wq).reshape(B, L, NUM_HEADS, HEAD_DIM)
        k = (x @ wk).reshape(B, L, NUM_KV_HEADS, HEAD_DIM)
        v = (x @ wv).reshape(B, L, NUM_KV_HEADS, HEAD_DIM)
        q = rms_norm(q, q_norm_w)
        k = rms_norm(k, k_norm_w)
        k_ctx = (h_ctx_kv @ wk_ctx).reshape(B, T, NUM_KV_HEADS, HEAD_DIM)
        v_ctx = (h_ctx_kv @ wv_ctx).reshape(B, T, NUM_KV_HEADS, HEAD_DIM)
        k_ctx = rms_norm(k_ctx, k_norm_w)
        cos, sin = rope_cache(L, HEAD_DIM, ROPE_THETA, x.dtype)
        q = q * cos + rotate_half(q) * sin
        k = k * cos + rotate_half(k) * sin
        k_full = jnp.concatenate([k_ctx, k], axis=1)
        v_full = jnp.concatenate([v_ctx, v], axis=1)
        k_full = jnp.repeat(k_full, rep, axis=2)
        v_full = jnpp_repeat = jnp.repeat(v_full, rep, axis=2)
        i = jnp.arange(L)[:, None]
        j = jnp.arange(L)[None, :]
        causal = jnp.where(j > i, -jnp.inf, 0.0).astype(x.dtype)
        mask = jnp.concatenate([jnp.zeros((L, T), x.dtype), causal], axis=1)
        scale = 1.0 / np.sqrt(HEAD_DIM)
        scores = jnp.einsum('blhd,bmhd->bhlm', q, k_full) * scale + mask
        probs = jax.nn.softmax(scores, axis=-1)
        out = jnp.einsum('bhlm,bmhd->blhd', probs, v_full)
        out = out.reshape(B, L, NUM_HEADS * HEAD_DIM)
        return out @ wo

    def _L1_ffn_ref(x, w_fc, w_proj):
        import jax, jax.numpy as jnp
        import numpy as np
        TURBO_BLOCK_SIZE = 64
        TURBO_MSE_BITS = 5
        QMAX = 2 ** (TURBO_MSE_BITS - 1) - 1
        SHRINKS = np.linspace(0.4, 1.0, 16)

        def mse_quant_dequant(w):
            O, I = w.shape
            wb = w.reshape(O, I // TURBO_BLOCK_SIZE, TURBO_BLOCK_SIZE)
            amax = jnp.max(jnp.abs(wb), axis=-1, keepdims=True)
            base = jnp.maximum(amax, 1e-08) / QMAX
            best_err = jnp.full(amax.shape, jnp.inf, dtype=w.dtype)
            best_scale = base
            for s in SHRINKS:
                scale = base * jnp.asarray(s, dtype=w.dtype)
                deq = jnp.clip(jnp.round(wb / scale), -QMAX, QMAX) * scale
                err = jnp.sum((deq - wb) ** 2, axis=-1, keepdims=True)
                upd = err < best_err
                best_err = jnp.where(upd, err, best_err)
                best_scale = jnp.where(upd, scale, best_scale)
            deq = jnp.clip(jnp.round(wb / best_scale), -QMAX, QMAX) * best_scale
            return deq.reshape(O, I)

        def turbo_linear(x, w):
            wq = w + jax.lax.stop_gradient(mse_quant_dequant(w) - w)
            return x @ wq.T
        h = jnp.maximum(turbo_linear(x, w_fc), 0.0)
        return turbo_linear(h * h, w_proj)
    x = x + _L0_xattn_ref(_layernorm(x, axis=-1), ctx_2048, mask_BxS2_bk0)
    x = x + _L0_ffn_ref(_layernorm(x, axis=-1), L0_ffn_up_kernel, L0_ffn_up_bias, L0_ffn_down_kernel, L0_ffn_down_bias)
    x = x + _L1_xattn_ref(_layernorm(x, axis=-1), ctx_2048, L1_xattn_wq, L1_xattn_wk, L1_xattn_wv, L1_xattn_wo, L1_xattn_wk_ctx, L1_xattn_wv_ctx, L1_xattn_q_norm_w, L1_xattn_k_norm_w)
    x = x + _L1_ffn_ref(_layernorm(x, axis=-1), L1_ffn_w_fc, L1_ffn_w_proj)
    return x

_drawn_inputs = setup_inputs


def setup_inputs(seed=0):
    import zlib

    import numpy as np

    out = dict(_drawn_inputs(seed))
    spreads = {'L0_ffn_up_bias': (0.0, 0.1),
     'L0_ffn_down_bias': (0.0, 0.1),
     'L1_xattn_q_norm_w': (1.0, 0.6),
     'L1_xattn_k_norm_w': (1.0, 0.6)}
    factors = {}
    for name, (base, spread) in spreads.items():
        noise = np.random.default_rng([zlib.crc32(name.encode()), seed]).standard_normal(out[name].shape)
        drawn = base * np.exp(spread * noise) if base else spread * noise
        out[name] = jnp.asarray(drawn.astype(out[name].dtype))
    for name, factor in factors.items():
        out[name] = (out[name] * factor).astype(out[name].dtype)
    return out
```

```python
from contextlib import ExitStack

import concourse.bass as bass
from concourse import mybir

P = 128
F32 = mybir.dt.float32
BF16 = mybir.dt.bfloat16
FP16 = mybir.dt.float16
U8 = mybir.dt.uint8
U32 = mybir.dt.uint32
ALU = mybir.AluOpType
ACT = mybir.ActivationFunctionType
AX = mybir.AxisListType.X

NB, S, D = 8, 256, 256
T = 64
DH = D // P
TT = S // P
F = 1024
FK = F // P
NH, NG, HD = 16, 4, 128
REP = NH // NG
NP = NH // 2
LN_EPS, RMS_EPS = 1e-5, 1e-6
QBLK = 64
NBLK = 2 * F * D // QBLK // P
QMAX = 15.0
NSHRINK = 16
MAGIC = 1.5 * 2.0 ** 23
HALF_STEP = 1.5 * 2.0 ** 22
NEG = 1e30


def part(eng, sem, value):
    if not isinstance(value, int) or value > 0:
        eng.wait_ge(sem, value)


class Link:

    def __init__(self, eng, sem, base=0):
        self.eng, self.sem, self.base, self.n = eng, sem, base, 0

    def __call__(self, ins):
        self.n += 1
        ins.then_inc(self.sem, 1)
        self.eng.wait_ge(self.sem, self.base + self.n)


def block_a(nc, dr, sb, ex):
    with ExitStack() as ctx:
        def local(name, shape, dt):
            return ctx.enter_context(nc.sbuf_tensor(f"a_{name}", shape, dt))

        def sem(name):
            return ctx.enter_context(nc.semaphore(name))

        stage_q = local("stage_q", [P, DH, NH * HD], F32)
        stage_c = sb["xT_hi"][:].rearrange("p b h s -> p (b h s)").bitcast(F32
            ).rearrange("p (h g i d) -> p h g i d", h=DH, g=NG, i=2)
        stage_kv = stage_c
        stage_f = sb["W"]
        ctx_rows = local("ctx_rows", [P, NB // 2, D], F32)
        ctx_keys = sb["xT_lo"][0:T].rearrange("p b h s -> p (b h s)").bitcast(F32
            ).rearrange("p (b d) -> p b d", b=NB)
        wc_hi = local("wc_hi", [P, DH, NG * 2 * HD], BF16)
        wc_lo = local("wc_lo", [P, DH, NG * 2 * HD], BF16)
        vf_hi = local("vf_hi", [P, NB // 2, NG, HD], BF16)
        vf_lo = local("vf_lo", [P, NB // 2, NG, HD], BF16)
        knorm = local("knorm", [P, HD], F32)
        mask8 = local("mask8", [P, NB, T], U8)
        CH = 512
        blk = local("blk", [P, CH], F32)
        trunc = local("trunc", [P, CH], F32)
        expo = local("expo", [P, CH], F32)
        rnd = local("rnd", [P, CH], F32)
        quant = local("quant", [P, CH], F32)
        back = local("back", [P, 2, CH], F32)
        amax = local("amax", [P, CH // 32], F32)
        scale = local("scale", [P, CH // 32], F32)
        top = local("top", [P, CH // 32], F32)
        junk = local("junk", [P, 2, 2, HD], BF16)
        ssq = local("ssq", [P, 8, 2], F32)
        kraw = local("kraw", [P, 2, 2, HD], F32)
        kn = local("kn", [P, 2, 2, HD], F32)
        krms = local("krms", [P, 2, 2], F32)
        kvar = local("kvar", [P, 2, 2], F32)

        p_ctx = [ctx.enter_context(nc.psum_tensor(f"p_ctx{i}", [P, 512], F32)) for i in range(2)]
        p_kv = [ctx.enter_context(nc.psum_tensor(f"p_kv{i}", [P, 2, 2, HD], F32)) for i in range(2)]
        p_kt = [ctx.enter_context(nc.psum_tensor(f"p_kt{i}", [P, 2, P], F32)) for i in range(2)]

        ld_x, ld_ctx, ld_rows = sem("ld_x"), sem("ld_ctx"), sem("ld_rows")
        ld_tab, ld_mask, ld_up, ld_down = sem("ld_tab"), sem("ld_mask"), sem("ld_up"), sem("ld_down")
        ld_c, ld_q, ld_kv, ld_o = sem("ld_c"), sem("ld_q"), sem("ld_kv"), sem("ld_o")
        ld_small = sem("ld_small")
        hi_done, lo_done = sem("a_hi_done"), sem("a_lo_done")
        rows_t, ctx_hi_done, ctx_lo_done = sem("rows_t"), sem("ctx_hi_done"), sem("ctx_lo_done")
        kv_out, kv_act, kv_dve = sem("kv_out"), sem("kv_act"), sem("kv_dve")
        kn_done, kt_out, kt_hi, kt_lo = sem("kn_done"), sem("kt_out"), sem("kt_hi"), sem("kt_lo")
        fp4_done, fp4_copied = sem("fp4_done"), sem("fp4_copied")
        shifted, dve_link, pool_link = sem("shifted"), sem("a_dve_link"), sem("a_pool_link")
        half_set = sem("half_set")

        block = ctx.enter_context(nc.Block())
        units = [(r, gp) for r in range(NB // 2) for gp in range(2)]

        @block.sync
        def _(sp):
            sp.dma_start(stage_f[:, 0, :].rearrange("p (h n) -> p h n", h=DH),
                         dr["up"].rearrange("(h p) n -> p h n", p=P)).then_inc(ld_up, 16)
            sp.dma_start(ctx_rows[:], dr["ctx"].rearrange("(r b) k d -> (b k) r d", b=2)
                         ).then_inc(ld_rows, 16)
            sp.dma_start(sb["ident"][:], dr["ident"]).then_inc(ld_rows, 16)
            for i, w in enumerate(("wk_ctx", "wv_ctx")):
                for h in range(DH):
                    sp.dma_start(stage_c[:, h, :, i, :],
                                 dr[w][h * P:(h + 1) * P, :].rearrange("p (g d) -> p g d", g=NG)
                                 ).then_inc(ld_c, 16)
            sp.dma_start(stage_f[:, 1, :].rearrange("p (k n) -> p k n", k=FK),
                         dr["down"].rearrange("(k p) n -> p k n", p=P)).then_inc(ld_down, 16)
            sp.dma_start(sb["X"][:], dr["x"].rearrange("b (t p) d -> p (b t) d", p=P)).then_inc(ld_x, 16)
            sp.wait_ge(kv_act, len(units))
            sp.wait_ge(kv_dve, len(units))
            for dst, src in ((sb["vc_hi"], vf_hi), (sb["vc_lo"], vf_lo)):
                for half in range(2):
                    sp.dma_start(dst[:].rearrange("k (r b) g d -> k b r (g d)", b=2)[:, half],
                                 src[half * T:(half + 1) * T].rearrange("k r g d -> k r (g d)")
                                 ).then_inc(shifted, 16)
            for s, n in ((ld_x, 1), (shifted, 4)):
                sp.wait_ge(s, 16 * n)

        @block.scalar
        def _(act):
            act.dma_start(knorm[:], dr["k_norm"].partition_broadcast(P)).then_inc(ld_small, 16)
            act.dma_start(mask8[:], dr["mask"].partition_broadcast(P)).then_inc(ld_mask, 16)
            act.dma_start(ctx_keys, dr["ctx"].rearrange("b k d -> k b d")).then_inc(ld_ctx, 16)
            act.dma_start(stage_q[:], dr["wq"].rearrange("(h p) n -> p h n", p=P)).then_inc(ld_q, 16)
            act.wait_ge(ld_c, 64)
            nc.scalar.copy(wc_hi[:], stage_c.rearrange("p h g i d -> p h (g i d)")).then_inc(hi_done, 1)
            act.wait_ge(hi_done, 1)
            act.wait_ge(lo_done, 1)
            for i, w in enumerate(("wk", "wv")):
                for h in range(DH):
                    act.dma_start(stage_kv[:, h, :, i, :],
                                  dr[w][h * P:(h + 1) * P, :].rearrange("p (g d) -> p g d", g=NG)
                                  ).then_inc(ld_kv, 16)
            act.dma_start(sb["rope"][:, 0], dr["cos"].rearrange("(t p) d -> p t d", p=P)).then_inc(ld_tab, 16)
            act.dma_start(sb["rope"][:, 1], dr["sin"].rearrange("(t p) d -> p t d", p=P)).then_inc(ld_tab, 16)
            act.dma_start(sb["norms"][:, 0], dr["q_norm"].partition_broadcast(P)).then_inc(ld_tab, 16)
            act.dma_start(sb["norms"][:, 1], dr["k_norm"].partition_broadcast(P)).then_inc(ld_tab, 16)
            with nc.allow_non_contiguous_dma(reason="4 KB, once"):
                act.dma_start(sb["up_b"][:], dr["up_b"].rearrange("(k p) -> p k", p=P)).then_inc(ld_tab, 16)
            act.dma_start(sb["down_b"][:], dr["down_b"].partition_broadcast(P)).then_inc(ld_tab, 16)
            act.dma_start(sb["shrinks"][:], dr["shrinks"].partition_broadcast(P)).then_inc(ld_tab, 16)
            for h in range(DH):
                act.wait_ge(rows_t, h + 1)
                nc.scalar.copy(sb["ctxT_hi"][:, h], p_ctx[h][:]).then_inc(ctx_hi_done, 1)
            act.wait_ge(ld_ctx, 16)
            nc.scalar.copy(sb["ctx_hi"][:], ctx_keys).then_inc(hi_done, 1)

            def kt_copy(u):
                r, gp = units[u]
                act.wait_ge(kt_out, u + 1)
                nc.scalar.copy(sb["kcT_hi"][:, 2 * gp:2 * gp + 2, r * P:(r + 1) * P], p_kt[u % 2][:]
                               ).then_inc(kt_hi, 1)

            def fp4_copy(c):
                act.wait_ge(fp4_done, c + 1)
                nc.scalar.copy(sb["w4"][:, c // 4, (c % 4) * CH:(c % 4 + 1) * CH], back[:, c % 2]
                               ).then_inc(fp4_copied, 1)

            for u, (r, gp) in enumerate(units):
                fp4_copy(u)
                act.wait_ge(kv_out, u + 1)
                for i in range(2):
                    nc.scalar.activation(junk[:, u % 2, i], p_kv[u % 2][:, i, 0, :], ACT.Square,
                                         accum_out=ssq[:, u, i:i + 1])
                nc.scalar.copy(vf_hi[:, r, 2 * gp:2 * gp + 2, :], p_kv[u % 2][:, :, 1, :]).then_inc(kv_act, 1)
                if u >= 1:
                    kt_copy(u - 1)
            kt_copy(len(units) - 1)
            act.wait_ge(ld_q, 16)
            nc.scalar.copy(sb["wq_hi"][:], stage_q[:]).then_inc(hi_done, 1)
            act.wait_ge(ld_kv, 64)
            nc.scalar.copy(sb["wkv_hi"][:], stage_kv.rearrange("p h g i d -> p h (g i d)")).then_inc(hi_done, 1)
            act.wait_ge(hi_done, 4)
            act.wait_ge(lo_done, 4)
            act.dma_start(stage_q[:].rearrange("p h (k n) -> p (h k) n", n=D),
                          dr["wo"].rearrange("(k p) n -> p k n", p=P)).then_inc(ld_o, 16)
            act.wait_ge(ld_o, 16)
            nc.scalar.copy(sb["wo_hi"][:], stage_q[:].rearrange("p h (k n) -> p (h k) n", n=D)).then_inc(hi_done, 1)
            act.wait_ge(ld_tab, 16 * 7)

        @block.gpsimd
        def _(pool):
            link = Link(pool, pool_link)
            nc.gpsimd.memset(sb["magic"][:], MAGIC)
            nc.gpsimd.memset(sb["neghalf"][:], -0.5).then_inc(half_set, 1)
            pool.wait_ge(half_set, 1)
            pool.wait_ge(hi_done, 1)
            nc.gpsimd.tensor_tensor(wc_lo[:], stage_c.rearrange("p h g i d -> p h (g i d)"), wc_hi[:],
                                    ALU.subtract).then_inc(lo_done, 1)

            def kn_unit(u):
                pool.wait_ge(kv_act, u + 1)
                pool.wait_ge(kv_dve, u + 1)
                link(nc.gpsimd.tensor_scalar(kvar[:, u % 2], ssq[:, u], 1.0 / HD, RMS_EPS, ALU.mult, ALU.add))
                link(nc.gpsimd.tensor_tensor(krms[:, u % 2], kvar[:, u % 2], sb["neghalf"][:, 0:2], ALU.pow))
                if u >= 2:
                    pool.wait_ge(kt_out, u - 1)
                for i in range(2):
                    last = nc.gpsimd.tensor_scalar(kn[:, u % 2, i], kraw[:, u % 2, i], krms[:, u % 2, i:i + 1],
                                                   1.0, ALU.mult, ALU.mult)
                last.then_inc(kn_done, 1)

            for u in range(4):
                kn_unit(u)
            pool.wait_ge(hi_done, 2)
            nc.gpsimd.tensor_tensor(sb["ctx_lo"][:], ctx_keys, sb["ctx_hi"][:], ALU.subtract
                                    ).then_inc(lo_done, 1)
            for u in range(4, 8):
                kn_unit(u)
            pool.wait_ge(hi_done, 3)
            nc.gpsimd.tensor_tensor(sb["wq_lo"][:], stage_q[:], sb["wq_hi"][:], ALU.subtract).then_inc(lo_done, 1)
            pool.wait_ge(hi_done, 4)
            nc.gpsimd.tensor_tensor(sb["wkv_lo"][:], stage_kv.rearrange("p h g i d -> p h (g i d)"),
                                    sb["wkv_hi"][:], ALU.subtract).then_inc(lo_done, 1)
            pool.wait_ge(hi_done, 5)
            nc.gpsimd.tensor_tensor(sb["wo_lo"][:], stage_q[:].rearrange("p h (k n) -> p (h k) n", n=D),
                                    sb["wo_hi"][:], ALU.subtract).then_inc(lo_done, 1)
            pool.wait_ge(ld_mask, 16)
            nc.gpsimd.tensor_copy(sb["keep"][:], mask8[:]).then_inc(half_set, 1)
            pool.wait_ge(half_set, 2)
            nc.gpsimd.tensor_scalar(sb["drop"][:], sb["keep"][:], -1.0, NEG, ALU.add, ALU.mult
                                    ).then_inc(half_set, 1)
            nc.gpsimd.memset(sb["causal"][:], 0.0).then_inc(half_set, 1)
            pool.wait_ge(half_set, 4)
            nc.gpsimd.affine_select(out=sb["causal"][:], in_=sb["causal"][:], compare_op=ALU.is_ge, fill=-NEG,
                                    base=0, pattern=[[-1, P]], channel_multiplier=1).then_inc(half_set, 1)
            pool.wait_ge(ld_rows, 32)
            nc.gpsimd.tensor_copy(sb["ident16"][:], sb["ident"][:]).then_inc(half_set, 1)

        @block.vector
        def _(dve):
            link = Link(dve, dve_link)

            def fp4(c):
                dve.wait_ge(ld_up if c < 4 else ld_down, 16)
                src = stage_f[:, c // 4, (c % 4) * CH:(c % 4 + 1) * CH]
                link(nc.vector.transpose(blk[:], src))
                bits = blk[:].bitcast(U32)
                nc.vector.tensor_scalar(trunc[:].bitcast(U32), bits, 0x7FE00000, None, ALU.bitwise_and)
                link(nc.vector.tensor_scalar(expo[:].bitcast(U32), bits, 0x7F800000, None, ALU.bitwise_and))
                link(nc.vector.tensor_reduce(amax[:], trunc[:].rearrange("p (a b) -> p a b", b=32), AX, ALU.max))
                link(nc.vector.tensor_scalar(scale[:], amax[:], 1e-30, None, ALU.max))
                link(nc.vector.tensor_scalar(top[:].bitcast(U32), scale[:].bitcast(U32), 0x7F800000, None,
                                             ALU.bitwise_and))
                link(nc.vector.tensor_scalar(scale[:], top[:], 0.25, None, ALU.mult))
                link(nc.vector.tensor_scalar(top[:], scale[:], 6.0, None, ALU.mult))
                wide = [P, CH // 32, 32]
                e3 = expo[:].rearrange("p (a b) -> p a b", b=32)
                q3 = quant[:].rearrange("p (a b) -> p a b", b=32)
                link(nc.vector.tensor_tensor(e3, e3, scale[:].unsqueeze(2).to_broadcast(wide), ALU.max))
                link(nc.vector.tensor_scalar(trunc[:], trunc[:], 1.0625, None, ALU.mult))
                link(nc.vector.scalar_tensor_tensor(rnd[:], expo[:], HALF_STEP, trunc[:], ALU.mult, ALU.add))
                link(nc.vector.scalar_tensor_tensor(quant[:], expo[:], -HALF_STEP, rnd[:], ALU.mult, ALU.add))
                link(nc.vector.tensor_tensor(q3, q3, top[:].unsqueeze(2).to_broadcast(wide), ALU.min))
                link(nc.vector.scalar_tensor_tensor(rnd[:].bitcast(U32), bits, 0x80000000, quant[:].bitcast(U32),
                                                    ALU.bitwise_and, ALU.bitwise_or))
                if c >= 2:
                    dve.wait_ge(fp4_copied, c - 1)
                nc.vector.transpose(back[:, c % 2], rnd[:]).then_inc(fp4_done, 1)

            def kt_copy(u):
                r, gp = units[u]
                dve.wait_ge(kt_hi, u + 1)
                at = slice(2 * gp, 2 * gp + 2), slice(r * P, (r + 1) * P)
                nc.vector.tensor_tensor(sb["kcT_lo"][:, at[0], at[1]], p_kt[u % 2][:],
                                        sb["kcT_hi"][:, at[0], at[1]], ALU.subtract).then_inc(kt_lo, 1)

            fp4(0)
            fp4(1)
            for h in range(DH):
                dve.wait_ge(ctx_hi_done, h + 1)
                nc.vector.tensor_tensor(sb["ctxT_lo"][:, h], p_ctx[h][:], sb["ctxT_hi"][:, h], ALU.subtract
                                        ).then_inc(ctx_lo_done, 1)
            dve.wait_ge(ld_small, 16)
            for u, (r, gp) in enumerate(units):
                if u < 6:
                    fp4(u + 2)
                dve.wait_ge(kv_act, u + 1)
                if u >= 2:
                    dve.wait_ge(kn_done, u - 1)
                nc.vector.tensor_tensor(kraw[:, u % 2], p_kv[u % 2][:, :, 0, :],
                                        knorm[:].unsqueeze(1).to_broadcast([P, 2, HD]), ALU.mult)
                nc.vector.tensor_tensor(vf_lo[:, r, 2 * gp:2 * gp + 2, :], p_kv[u % 2][:, :, 1, :],
                                        vf_hi[:, r, 2 * gp:2 * gp + 2, :], ALU.subtract).then_inc(kv_dve, 1)
                if u >= 1:
                    kt_copy(u - 1)
            kt_copy(len(units) - 1)
            dve.wait_ge(half_set, 2)
            nc.vector.tensor_reduce(sb["valid"][:], sb["keep"][:], AX, ALU.max)
            dve.wait_ge(ld_tab, 16 * 7)
            for i in range(2):
                nrm = sb["norms"][:, i].rearrange("p (a d) -> p a d", a=1).to_broadcast([P, TT, HD])
                nc.vector.tensor_tensor(sb["cosw"][:, i], sb["rope"][:, 0], nrm, ALU.mult)
                swapped = sb["norms"][:, i].rearrange("p (a h d) -> p a h d", a=1, h=2)[:, :, ::-1, :]
                for t in range(TT):
                    nc.vector.tensor_tensor(sb["sinw"][:, i, t].rearrange("p (h d) -> p h d", h=2),
                                            sb["rope"][:, 1, t].rearrange("p (h d) -> p h d", h=2),
                                            swapped[:, 0], ALU.mult)

        @block.tensor
        def _(pe):
            pe.wait_ge(ld_rows, 32)
            for h in range(DH):
                for r in range(NB // 2):
                    last = nc.tensor.transpose(p_ctx[h][:, r * P:(r + 1) * P],
                                               ctx_rows[:, r, h * P:(h + 1) * P], sb["ident"][:])
                last.then_inc(rows_t, 1)
            pe.wait_ge(hi_done, 1)
            pe.wait_ge(lo_done, 1)
            pe.wait_ge(ctx_lo_done, DH)

            def kt_unit(u):
                pe.wait_ge(kn_done, u + 1)
                if u >= 2:
                    pe.wait_ge(kt_lo, u - 1)
                for i in range(2):
                    last = nc.tensor.transpose(p_kt[u % 2][:, i, :], kn[:, u % 2, i], sb["ident"][:])
                last.then_inc(kt_out, 1)

            for u, (r, gp) in enumerate(units):
                if u >= 2:
                    pe.wait_ge(kv_act, u - 1)
                    pe.wait_ge(kv_dve, u - 1)
                n = 0
                for h in range(DH):
                    rows = [sb[k][:, h, r * P:(r + 1) * P] for k in ("ctxT_hi", "ctxT_lo")]
                    cols = [w[:, h, gp * 512:(gp + 1) * 512] for w in (wc_hi, wc_lo)]
                    for a, b in ((0, 0), (0, 1), (1, 0)):
                        last = nc.tensor.matmul(p_kv[u % 2][:].rearrange("p g i d -> p (g i d)"),
                                                rows[a], cols[b], start=n == 0, stop=n == 3 * DH - 1)
                        n += 1
                last.then_inc(kv_out, 1)
                if u >= 1:
                    kt_unit(u - 1)
            kt_unit(len(units) - 1)



def block_b(nc, dr, sb):
    with ExitStack() as ctx:
        def local(name, shape, dt):
            return ctx.enter_context(nc.sbuf_tensor(f"b_{name}", shape, dt))

        def sem(name):
            return ctx.enter_context(nc.semaphore(name))

        def bank(name, shape):
            return ctx.enter_context(nc.psum_tensor(f"b_{name}", shape, F32))

        X = sb["X"]
        stats = local("stats", [P, 3, TT, 6], F32)
        mv = local("mv", [P, 3, TT, 2], F32)
        var = local("var", [P, 3, TT], F32)
        rstd = local("rstd", [P, 3, TT], F32)
        xn = local("xn", [P, 3, TT, D], F32)
        aT_hi = local("aT_hi", [P, DH, S], FP16)
        aT_lo = local("aT_lo", [P, DH, S], FP16)
        zT_hi = local("zT_hi", [P, DH, S], FP16)
        zT_lo = local("zT_lo", [P, DH, S], FP16)
        sc = local("sc", [P, TT, T], F32)
        scm = local("scm", [P, TT, T], F32)
        smax = local("smax", [P, TT], F32)
        nbias = local("nbias", [P, TT], F32)
        expd = local("expd", [P, TT, T], F32)
        rsum = local("rsum", [P, TT], F32)
        rinv = local("rinv", [P, TT], F32)
        rval = local("rval", [P, TT], F32)
        prob = local("prob", [P, TT, T], F32)
        pT_hi = local("pT_hi", [T, S], BF16)
        pT_lo = local("pT_lo", [T, S], BF16)
        gel = local("gel", [P, 2, 2, S], F32)
        gT_hi = local("gT_hi", [P, FK, S], BF16)
        gT_lo = local("gT_lo", [P, FK, S], BF16)
        xb = local("xb", [P, TT, D], F32)

        p_t = [bank(f"p_t{i}", [P, DH, S]) for i in range(2)]
        p_h = [bank(f"p_h{i}", [P, 2, S]) for i in range(2)]
        p_s = bank("p_s", [P, TT, T])
        p_r = bank("p_r", [P, TT, D])
        p_y = bank("p_y", [P, TT, D])

        norm_stat = [sem(f"norm_stat{n}") for n in range(3)]
        norm_rstd = [sem(f"norm_rstd{n}") for n in range(3)]
        norm_done = [sem(f"norm_done{n}") for n in range(3)]
        turned = [sem(f"turned{n}") for n in range(3)]
        turn_hi = [sem(f"turn_hi{n}") for n in range(3)]
        turn_lo = [sem(f"turn_lo{n}") for n in range(3)]
        scored, max_done, bias_done, exp_done, prob_done = (sem(x) for x in (
            "scored", "max_done", "bias_done", "exp_done", "prob_done"))
        probs_turned, probs_hi, probs_lo, read_out, attn_added = (sem(x) for x in (
            "probs_turned", "probs_hi", "probs_lo", "read_out", "attn_added"))
        up_out, gelu_done, gelu_hi, gelu_lo, down_out, ffn_added, bias_added = (sem(x) for x in (
            "up_out", "gelu_done", "gelu_hi", "gelu_lo", "down_out", "ffn_added", "bias_added"))
        ld_w = sem("ld_w")
        dve_link, pool_link = sem("b_dve_link"), sem("b_pool_link")
        pe_gate, dve_gate, pool_gate = sem("b_pe_gate"), sem("b_dve_gate"), sem("b_pool_gate")

        block = ctx.enter_context(nc.Block())


        def over_batches(eng, body):
            body(-1, True, False)
            body(0, True, True)
            with eng.Fori(1, NB - 1) as b:
                body(b, True, True)
            body(NB - 1, False, True)

        @block.sync
        def _(sp):
            sp.dma_start(sb["W"][:, 0, :].rearrange("p (k n) -> p k n", k=FK),
                         dr["w_fc"].rearrange("(k p) n -> p k n", p=P)).then_inc(ld_w, 16)
            sp.dma_start(sb["W"][:, 1, :].rearrange("p (h n) -> p h n", h=DH),
                         dr["w_proj"].rearrange("(h p) n -> p h n", p=P)).then_inc(ld_w, 16)
            sp.wait_ge(ld_w, 32)

        @block.tensor
        def _(pe):
            def turn(n, k, slot):
                pe.wait_ge(norm_done[n], k + 1)
                for t in range(TT):
                    for h in range(DH):
                        last = nc.tensor.transpose(p_t[slot][:, h, t * P:(t + 1) * P],
                                                   xn[:, n, t, h * P:(h + 1) * P], sb["ident"][:])
                last.then_inc(turned[n], 1)

            def up(b, j):
                part(pe, gelu_done, 4 * b + j - 1)
                for i in range(2):
                    k = 2 * j + i
                    n = 0
                    for h in range(DH):
                        w = sb["w4"][:, 0, h * F + k * P:h * F + (k + 1) * P]
                        for z in (zT_hi, zT_lo):
                            last = nc.tensor.matmul(p_h[j % 2][:, i, :], w, z[:, h, :], start=n == 0,
                                                    stop=n == 2 * DH - 1)
                            n += 1
                last.then_inc(up_out, 1)

            def down(b, j):
                pe.wait_ge(gelu_lo, 4 * b + j + 1)
                for k in (2 * j, 2 * j + 1):
                    for t in range(TT):
                        for g in (gT_hi, gT_lo):
                            first = k == 0 and t == 0 and g is gT_hi
                            last = nc.tensor.matmul(p_y[:, t, :], g[:, k, t * P:(t + 1) * P],
                                                    sb["w4"][:, 1, k * D:(k + 1) * D], start=first,
                                                    stop=k == FK - 1, skip_group_check=True)
                if j == 3:
                    last.then_inc(down_out, 1)

            def body(b, attn, ffn):
                a = b + 1
                if attn:
                    part(pe, turn_lo[1], a)
                    turn(0, a, 0)
                if ffn:
                    pe.wait_ge(turn_lo[1], b + 1)
                    up(b, 0)
                    up(b, 1)
                if attn:
                    pe.wait_ge(turn_lo[0], a + 1)
                    part(pe, max_done, a)
                    for t in range(TT):
                        n = 0
                        for h in range(DH):
                            q = [z[:, h, t * P:(t + 1) * P] for z in (aT_hi, aT_lo)]
                            c = [sb[k][:, h, bass.ds(a * T, T)] for k in ("ctxT_hi", "ctxT_lo")]
                            for i, j in ((0, 0), (0, 1), (1, 0)):
                                last = nc.tensor.matmul(p_s[:, t, :], q[i], c[j], start=n == 0,
                                                        stop=n == 3 * DH - 1)
                                n += 1
                    last.then_inc(scored, 1)
                if ffn:
                    up(b, 2)
                    part(pe, ffn_added, b)
                    down(b, 0)
                if attn:
                    pe.wait_ge(prob_done, a + 1)
                    if ffn:
                        part(pe, turn_lo[2], b)
                    pe.sem_inc(pe_gate, 1)
                    for t in range(TT):
                        last = nc.tensor.transpose(p_t[1][0:T, 0, t * P:(t + 1) * P], prob[:, t, :],
                                                   sb["ident"][:])
                    last.then_inc(probs_turned, 1)
                if ffn:
                    up(b, 3)
                    down(b, 1)
                if attn:
                    pe.wait_ge(probs_lo, a + 1)
                    part(pe, attn_added, a)
                    for t in range(TT):
                        p = [z[:, t * P:(t + 1) * P] for z in (pT_hi, pT_lo)]
                        v = [sb[k][:, bass.ds(a, 1), :].rearrange("k b d -> k (b d)") for k in ("ctx_hi", "ctx_lo")]
                        for n, (i, j) in enumerate(((0, 0), (0, 1), (1, 0))):
                            last = nc.tensor.matmul(p_r[:, t, :], p[i], v[j], start=n == 0, stop=n == 2)
                    last.then_inc(read_out, 1)
                if ffn:
                    down(b, 2)
                    down(b, 3)
                if attn:
                    turn(1, a, 0)
                if ffn:
                    turn(2, b, 1)

            over_batches(pe, body)

        @block.scalar
        def _(act):
            def turn(n, k, slot, hi):
                act.wait_ge(turned[n], k + 1)
                nc.scalar.copy(hi, p_t[slot][:]).then_inc(turn_hi[n], 1)

            def gelu(b, j):
                act.wait_ge(up_out, 4 * b + j + 1)
                part(act, gelu_lo, 4 * b + j - 1)
                for i in range(2):
                    k = 2 * j + i
                    last = nc.scalar.activation(gel[:, j % 2, i, :], p_h[j % 2][:, i, :], ACT.Gelu_apprx_tanh,
                                                bias=sb["up_b"][:, k:k + 1])
                last.then_inc(gelu_done, 1)

            def gelu_part(b, j):
                act.wait_ge(gelu_done, 4 * b + j + 1)
                nc.scalar.copy(gT_hi[:, 2 * j:2 * j + 2, :], gel[:, j % 2]).then_inc(gelu_hi, 1)

            def body(b, attn, ffn):
                a = b + 1
                if attn:
                    turn(0, a, 0, aT_hi[:])
                if ffn:
                    for j in range(2):
                        gelu(b, j)
                        if j == 0:
                            part(act, down_out, b)
                        gelu_part(b, j)
                if attn:
                    act.wait_ge(bias_done, a + 1)
                    for t in range(TT):
                        last = nc.scalar.activation(expd[:, t, :], scm[:, t, :], ACT.Exp, bias=nbias[:, t:t + 1],
                                                    scale=D ** -0.5, accum_out=rsum[:, t:t + 1])
                    last.then_inc(exp_done, 1)
                    act.wait_ge(probs_turned, a + 1)
                    nc.scalar.copy(pT_hi[:], p_t[1][0:T, 0, :]).then_inc(probs_hi, 1)
                if ffn:
                    for j in range(2, 4):
                        gelu(b, j)
                        gelu_part(b, j)
                if attn:
                    turn(1, a, 0, zT_hi[:])
                if ffn:
                    turn(2, b, 1, sb["xT_hi"][:, bass.ds(b, 1)].rearrange("p b h s -> p (b h) s"))

            over_batches(act, body)

        @block.gpsimd
        def _(pool):
            def rsqrt(n, k, link):
                pool.wait_ge(norm_stat[n], k + 1)
                pool.sem_inc(pool_gate, 1)
                link(nc.gpsimd.tensor_scalar(var[:, n], mv[:, n, :, 1], 1.0, LN_EPS, ALU.mult, ALU.add))
                nc.gpsimd.tensor_tensor(rstd[:, n], var[:, n], sb["neghalf"][:, 0:TT], ALU.pow
                                        ).then_inc(norm_rstd[n], 1)

            def body(b, attn, ffn):
                a = b + 1
                link = Link(pool, pool_link, 0 if isinstance(b, int) and b < 0 else 2 + 3 * b)
                if attn:
                    rsqrt(0, a, link)
                    pool.wait_ge(max_done, a + 1)
                    pool.sem_inc(pool_gate, 1)
                    nc.gpsimd.tensor_scalar(nbias[:], smax[:], -D ** -0.5, 1.0, ALU.mult, ALU.mult
                                            ).then_inc(bias_done, 1)
                if ffn:
                    part(pool, ffn_added, b)
                    pool.wait_ge(norm_done[1], b + 1)
                    nc.gpsimd.tensor_tensor(xb[:], X[:, bass.ds(b * TT, TT), :],
                                            sb["down_b"][:].unsqueeze(1).to_broadcast([P, TT, D]), ALU.add
                                            ).then_inc(bias_added, 1)
                if attn:
                    rsqrt(1, a, link)
                if ffn:
                    rsqrt(2, b, link)

            over_batches(pool, body)

        @block.vector
        def _(dve):
            def stat(n, b, link):
                dve.sem_inc(dve_gate, 1)
                for t in range(TT):
                    last = nc.vector.bn_stats(stats[:, n, t, :],
                                              X[:, bass.ds(b * TT + t, 1), :].rearrange("p a d -> p (a d)"))
                link(last)
                dve.sem_inc(dve_gate, 1)
                for t in range(TT):
                    last = nc.vector.bn_aggr(mv[:, n, t, :], stats[:, n, t, :])
                last.then_inc(norm_stat[n], 1)

            def normed(n, b, k):
                dve.wait_ge(norm_rstd[n], k + 1)
                part(dve, turned[n], k)
                for t in range(TT):
                    last = nc.vector.tensor_scalar(xn[:, n, t, :],
                                                   X[:, bass.ds(b * TT + t, 1), :].rearrange("p a d -> p (a d)"),
                                                   mv[:, n, t, 0:1], rstd[:, n, t:t + 1], ALU.subtract, ALU.mult)
                last.then_inc(norm_done[n], 1)

            def turn(n, k, slot, lo, hi):
                dve.wait_ge(turn_hi[n], k + 1)
                nc.vector.tensor_tensor(lo, p_t[slot][:], hi, ALU.subtract).then_inc(turn_lo[n], 1)

            def gelu_rest(b, j):
                dve.wait_ge(gelu_hi, 4 * b + j + 1)
                nc.vector.tensor_tensor(gT_lo[:, 2 * j:2 * j + 2, :], gel[:, j % 2], gT_hi[:, 2 * j:2 * j + 2, :],
                                        ALU.subtract).then_inc(gelu_lo, 1)

            ATTN_LINKS, FFN_LINKS = 6, 1

            def body(b, attn, ffn):
                a = b + 1
                both = ATTN_LINKS + FFN_LINKS
                base = 0 if isinstance(b, int) and b < 0 else ATTN_LINKS + both * b
                link = Link(dve, dve_link, base)
                if attn:
                    stat(0, a, link)
                    normed(0, a, a)
                    turn(0, a, 0, aT_lo[:], aT_hi[:])
                if ffn:
                    gelu_rest(b, 0)
                    gelu_rest(b, 1)
                if attn:
                    dve.wait_ge(scored, a + 1)
                    wide = [P, TT, T]
                    link(nc.vector.tensor_tensor(sc[:], p_s[:], sb["keep"][:, bass.ds(a, 1), :].to_broadcast(wide),
                                                 ALU.mult))
                    link(nc.vector.tensor_tensor(scm[:], sc[:], sb["drop"][:, bass.ds(a, 1), :].to_broadcast(wide),
                                                 ALU.add))
                    nc.vector.tensor_reduce(smax[:], scm[:], AX, ALU.max).then_inc(max_done, 1)
                    dve.wait_ge(exp_done, a + 1)
                    link(nc.vector.reciprocal(rinv[:], rsum[:]))
                    link(nc.vector.tensor_tensor(rval[:], rinv[:], sb["valid"][:, bass.ds(a, 1)].to_broadcast([P, TT]),
                                                 ALU.mult))
                    nc.vector.tensor_tensor(prob[:], expd[:], rval[:].unsqueeze(2).to_broadcast(wide), ALU.mult
                                            ).then_inc(prob_done, 1)
                    dve.wait_ge(probs_hi, a + 1)
                    nc.vector.tensor_tensor(pT_lo[:], p_t[1][0:T, 0, :], pT_hi[:], ALU.subtract
                                            ).then_inc(probs_lo, 1)
                if ffn:
                    gelu_rest(b, 2)
                if attn:
                    dve.wait_ge(read_out, a + 1)
                    here = X[:, bass.ds(a * TT, TT), :]
                    nc.vector.tensor_tensor(here, p_r[:], here, ALU.add).then_inc(attn_added, 1)
                    dve.wait_ge(attn_added, a + 1)
                if ffn:
                    gelu_rest(b, 3)
                if attn:
                    stat(1, a, link)
                    normed(1, a, a)
                    turn(1, a, 0, zT_lo[:], zT_hi[:])
                if ffn:
                    dve.wait_ge(down_out, b + 1)
                    dve.wait_ge(bias_added, b + 1)
                    nc.vector.tensor_tensor(X[:, bass.ds(b * TT, TT), :], p_y[:], xb[:], ALU.add
                                            ).then_inc(ffn_added, 1)
                    dve.wait_ge(ffn_added, b + 1)
                    stat(2, b, link)
                    normed(2, b, b)
                    xt = [sb[k][:, bass.ds(b, 1)].rearrange("p b h s -> p (b h) s") for k in ("xT_lo", "xT_hi")]
                    turn(2, b, 1, *xt)

            over_batches(dve, body)


def block_c(nc, sb):
    with ExitStack() as ctx:
        def local(name, shape, dt):
            return ctx.enter_context(nc.sbuf_tensor(f"c_{name}", shape, dt))

        def sem(name):
            return ctx.enter_context(nc.semaphore(name))

        def bank(name, shape):
            return ctx.enter_context(nc.psum_tensor(f"c_{name}", shape, F32))

        X = sb["X"]
        KW = T + S
        ROW = [T + P * (t + 1) for t in range(TT)]
        OFF = [0, ROW[0]]
        qT_hi = local("qT_hi", [P, NH, S], BF16)
        qT_lo = local("qT_lo", [P, NH, S], BF16)
        kT_hi = local("kT_hi", [P, NG, KW], BF16)
        kT_lo = local("kT_lo", [P, NG, KW], BF16)
        v_hi = local("v_hi", [P, TT, NG, HD], BF16)
        v_lo = local("v_lo", [P, TT, NG, HD], BF16)
        vctx_hi = local("vctx_hi", [T, NG, HD], BF16)
        vctx_lo = local("vctx_lo", [T, NG, HD], BF16)
        rc = local("rc", [P, 2, REP, HD], F32)
        rs = local("rs", [P, 2, REP, HD], F32)
        rot = local("rot", [P, 2, REP, HD], F32)
        krot = rot[:, 0, 0:TT]
        junk = local("junk", [P, REP, HD], BF16)
        ssq = local("ssq", [P, TT, NH], F32)
        ssk = local("ssk", [P, TT, NG], F32)
        qvar = local("qvar", [P, TT, REP], F32)
        qr = local("qr", [P, TT, REP], F32)
        qrms = local("qrms", [P, TT, NH], F32)
        kvar = local("kvar", [P, TT], F32)
        krms = local("krms", [P, TT], F32)
        smax = local("smax", [P, TT, 2], F32)
        nbias = local("nbias", [P, 2, TT, 2], F32)
        rsum = local("rsum", [P, 2, TT, 2], F32)
        rinv = local("rinv", [P, 2, TT, 2], F32)
        prob = local("prob", [P, 2, 2, sum(ROW)], F32)
        pT_hi = local("pT_hi", [P, 2, 3, 2 * S], BF16)
        pT_lo = local("pT_lo", [P, 2, 3, 2 * S], BF16)
        oT_hi = local("oT_hi", [P, 2, 2 * S], BF16)
        oT_lo = local("oT_lo", [P, 2, 2 * S], BF16)

        CH, CB = 512, 512 // QBLK
        NCH = 2 * 2048 // CH
        SB = NSHRINK // NB
        UB = SB * NCH
        Wf = sb["W"][:].rearrange("p m n -> p (m n)")
        mag = local("mag", [P, NCH * CH], F32)
        unit = local("unit", [P, 4, CH], F32)
        err = local("err", [P, NBLK], F32)
        best_err = local("best_err", [P, NBLK], F32)
        best = sb["best"]
        upd = local("upd", [P, NBLK], F32)
        keep_old = local("keep_old", [P, NBLK], F32)
        cur = local("cur", [P, 2, SB], F32)

        p_p = bank("p_p", [P, REP, HD])
        p_x = bank("p_x", [P, REP, P])
        p_s = [bank(f"p_s{i}", [P, 512]) for i in range(2)]
        p_t = [bank(f"p_t{i}", [P, 2 * S]) for i in range(2)]
        p_o = bank("p_o", [P, 2, S])
        p_y = bank("p_y", [P, TT, D])

        proj_out, proj_act, proj_dve, rot_done = (sem(x) for x in ("proj_out", "proj_act", "proj_dve", "rot_done"))
        x_out, x_hi, x_lo, ctx_in, q_scaled = (sem(x) for x in ("x_out", "x_hi", "x_lo", "ctx_in", "q_scaled"))
        scored, bias_done, exp_done, inv_done, prob_done = (sem(x) for x in (
            "c_scored", "c_bias_done", "c_exp_done", "inv_done", "c_prob_done"))
        t_out, t_hi, t_lo, o_out, o_hi, o_lo = (sem(x) for x in ("t_out", "t_hi", "t_lo", "o_out", "o_hi", "o_lo"))
        wo_done, y_added = sem("wo_done"), sem("y_added")
        mag_done, cur_set = sem("mag_done"), sem("cur_set")
        s_tick, s_near, s_nears, s_off, s_sqr, s_err, s_best = (sem(x) for x in (
            "s_tick", "s_near", "s_nears", "s_off", "s_sqr", "s_err", "s_best"))
        dve_link, pool_link = sem("c_dve_link"), sem("c_pool_link")
        pe_gate, pool_gate = sem("c_pe_gate"), sem("c_pool_gate")

        block = ctx.enter_context(nc.Block())

        STEPS = NP + 3

        def made(b, j, attn, nxt):
            if j < 2:
                return (NG - 1, b) if attn else None
            return ((j - 2) // 2, b + 1) if nxt and j < NP else None

        def over_batches(eng, body):
            body(-1, False, True)
            body(0, True, True)
            with eng.Fori(1, NB - 1) as b:
                body(b, True, True)
            body(NB - 1, True, False)

        def steps(b, attn, nxt):
            for j in range(STEPS):
                if attn or 2 <= j <= NP:
                    yield (j, made(b, j, attn, nxt),
                           made(b, j - 1, attn, nxt) if j >= 1 else None)

        @block.tensor
        def _(pe):
            def project(g, B, item):
                n = 3 * (NG * B + g) + item
                part(pe, proj_act, n)
                part(pe, proj_dve, n)
                rows = [sb[k][:, bass.ds(B, 1)].rearrange("p b h s -> p (b h) s") for k in ("xT_hi", "xT_lo")]
                if item < 2:
                    w = [sb[k][:, :, g * 512:(g + 1) * 512] for k in ("wq_hi", "wq_lo")]
                    tiles = [(item, p_p[:].rearrange("p a d -> p (a d)"))]
                else:
                    w = [sb[k][:, :, g * 256:(g + 1) * 256] for k in ("wkv_hi", "wkv_lo")]
                    tiles = [(t, p_p[:, 2 * t:2 * t + 2].rearrange("p a d -> p (a d)")) for t in range(TT)]
                for t, out in tiles:
                    i = 0
                    for h in range(DH):
                        for a, c in ((0, 0), (0, 1), (1, 0)):
                            last = nc.tensor.matmul(out, rows[a][:, h, t * P:(t + 1) * P], w[c][:, h, :],
                                                    start=i == 0, stop=i == 3 * DH - 1)
                            i += 1
                last.then_inc(proj_out, 1)

            def turn(g, B, item):
                n = 3 * (NG * B + g) + item
                pe.wait_ge(rot_done, n + 1)
                part(pe, x_lo, n)
                if item < 2:
                    for r in range(REP):
                        last = nc.tensor.transpose(p_x[:, r, :], rot[:, item, r, :], sb["ident"][:])
                else:
                    for t in range(TT):
                        last = nc.tensor.transpose(p_x[:, t, :], rot[:, 0, t, :], sb["ident"][:])
                last.then_inc(x_out, 1)

            def score(b, j):
                g = j * 2 // REP
                pe.wait_ge(x_lo, 3 * (NG * b + g) + 3)
                pe.wait_ge(ctx_in, NG * b + g + 1)
                part(pe, exp_done, NP * b + j)
                for i in range(2):
                    h = 2 * j + i
                    for t in range(TT):
                        out = p_s[i][:, OFF[t]:OFF[t] + ROW[t]]
                        q = [z[:, h, t * P:(t + 1) * P] for z in (qT_hi, qT_lo)]
                        k = [z[:, g, 0:ROW[t]] for z in (kT_hi, kT_lo)]
                        for n, (x, y) in enumerate(((0, 0), (0, 1), (1, 0))):
                            last = nc.tensor.matmul(out, q[x], k[y], start=n == 0, stop=n == 2)
                            if n == 0:
                                nc.tensor.matmul(out[:, ROW[t] - P:ROW[t]], sb["ident16"][:], sb["causal"][:],
                                                 start=False, stop=False, skip_group_check=True)
                last.then_inc(scored, 1)

            def turn_probs(b, j, u):
                n = 3 * (NP * b + j) + u
                pe.wait_ge(prob_done, NP * b + j + 1)
                part(pe, t_lo, n - 1)
                if u == 0:
                    pe.sem_inc(pe_gate, 1)
                out = p_t[(j + u) % 2]
                for i in range(2):
                    for t in range(TT):
                        if u == 2 and t == 0:
                            continue
                        lo, wide = (0, T) if u == 0 else (T + (u - 1) * P, P)
                        col = i * P if u == 2 else i * S + t * P
                        last = nc.tensor.transpose(out[0:wide, col:col + P],
                                                   prob[:, j % 2, i, OFF[t] + lo:OFF[t] + lo + wide],
                                                   sb["ident"][:])
                last.then_inc(t_out, 1)

            def values(b, j):
                g = j * 2 // REP
                pe.wait_ge(t_lo, 3 * (NP * b + j) + 3)
                part(pe, o_lo, NP * b + j)
                out = p_o[:].rearrange("p i s -> p (i s)")
                own = [[z[:, u, g, :] for z in (v_hi, v_lo)] for u in range(TT)]
                con = [z[:, g, :] for z in (vctx_hi, vctx_lo)]
                for u, (rows, wide, v) in enumerate(((P, 2 * S, own[0]), (T, 2 * S, con), (P, S, own[1]))):
                    at = (1, 0, 2)[u]
                    p = [z[0:rows, j % 2, at, 0:wide] for z in (pT_hi, pT_lo)]
                    dst = out if u < 2 else p_o[:, :, P:S]
                    for n, (x, y) in enumerate(((0, 0), (0, 1), (1, 0))):
                        rhs = p[y] if u < 2 else p[y].rearrange("p (i s) -> p i s", i=2)
                        last = nc.tensor.matmul(dst, v[x], rhs, start=u == 0 and n == 0,
                                                stop=u == 2 and n == 2, skip_group_check=True)
                last.then_inc(o_out, 1)

            def finish(b, j):
                pe.wait_ge(o_lo, NP * b + j + 1)
                if j == 0:
                    part(pe, y_added, b)
                for i in range(2):
                    h = 2 * j + i
                    for t in range(TT):
                        at = slice(i * S + t * P, i * S + (t + 1) * P)
                        o = [z[:, j % 2, at] for z in (oT_hi, oT_lo)]
                        w = [sb[k][:, h, :] for k in ("wo_hi", "wo_lo")]
                        for n, (x, y) in enumerate(((0, 0), (0, 1), (1, 0))):
                            last = nc.tensor.matmul(p_y[:, t, :], o[x], w[y],
                                                    start=j == 0 and i == 0 and t == 0 and n == 0,
                                                    stop=h == NH - 1 and n == 2, skip_group_check=True)
                last.then_inc(wo_done, 1)

            def body(b, attn, nxt):
                for j, now, before in steps(b, attn, nxt):
                    item = j % 2
                    if attn and j < NP:
                        score(b, j)
                    if now:
                        project(*now, item)
                    if attn and 1 <= j <= NP:
                        turn_probs(b, j - 1, 0)
                    if before:
                        turn(*before, 1 - item)
                    if attn and 2 <= j < NP + 2:
                        values(b, j - 2)
                    if attn and 1 <= j <= NP:
                        turn_probs(b, j - 1, 1)
                    if now and item == 1:
                        project(*now, 2)
                    if attn and 1 <= j <= NP:
                        turn_probs(b, j - 1, 2)
                    if before and item == 0:
                        turn(*before, 2)
                    if attn and 3 <= j:
                        finish(b, j - 3)

            over_batches(pe, body)

        @block.scalar
        def _(act):
            def squares(g, B, item):
                n = 3 * (NG * B + g) + item
                act.wait_ge(proj_out, n + 1)
                if item < 2:
                    part(act, q_scaled, NG * (B - 1) + g + 1)
                    for r in range(REP):
                        last = nc.scalar.activation(junk[:, r], p_p[:, r, :], ACT.Square,
                                                    accum_out=ssq[:, item, REP * g + r:REP * g + r + 1])
                else:
                    part(act, rot_done, 3 * (NG * (B - 1) + g) + 3)
                    for t in range(TT):
                        nc.scalar.activation(junk[:, t], p_p[:, 2 * t, :], ACT.Square, accum_out=ssk[:, t, g:g + 1])
                    part(act, o_out, NP * (B - 1) + 2 * g + 2)
                    last = nc.scalar.copy(v_hi[:, :, g, :],
                                          p_p[:].rearrange("p (t i) d -> p t i d", i=2)[:, :, 1, :])
                last.then_inc(proj_act, 1)

            def turn(g, B, item):
                act.wait_ge(x_out, 3 * (NG * B + g) + item + 1)
                part(act, scored, NP * (B - 1) + 2 * g + 2)
                if item < 2:
                    ins = nc.scalar.copy(qT_hi[:, REP * g:REP * (g + 1), item * P:(item + 1) * P], p_x[:])
                else:
                    ins = nc.scalar.copy(kT_hi[:, g, T:KW].rearrange("p (t s) -> p t s", t=TT), p_x[:, 0:TT, :])
                ins.then_inc(x_hi, 1)

            def exps(b, j):
                act.wait_ge(bias_done, NP * b + j + 1)
                part(act, t_out, 3 * (NP * b + j - 1))
                for i in range(2):
                    for t in range(TT):
                        last = nc.scalar.activation(prob[:, j % 2, i, OFF[t]:OFF[t] + ROW[t]],
                                                    p_s[i][:, OFF[t]:OFF[t] + ROW[t]], ACT.Exp,
                                                    bias=nbias[:, j % 2, t, i:i + 1],
                                                    scale=qrms[:, t, 2 * j + i:2 * j + i + 1],
                                                    accum_out=rsum[:, j % 2, t, i:i + 1])
                last.then_inc(exp_done, 1)

            def turn_probs(b, j, u):
                act.wait_ge(t_out, 3 * (NP * b + j) + u + 1)
                part(act, o_out, NP * b + j - 1)
                rows, wide = (T if u == 0 else P), (S if u == 2 else 2 * S)
                nc.scalar.copy(pT_hi[0:rows, j % 2, u, 0:wide], p_t[(j + u) % 2][0:rows, 0:wide]).then_inc(t_hi, 1)

            def values(b, j):
                act.wait_ge(o_out, NP * b + j + 1)
                part(act, wo_done, NP * b + j - 1)
                nc.scalar.copy(oT_hi[:, j % 2], p_o[:].rearrange("p i s -> p (i s)")).then_inc(o_hi, 1)

            def search_tick(b, u):
                n = UB * b + u
                if u % NCH == 0:
                    act.wait_ge(cur_set, b + 1)
                if isinstance(b, int) and b == 0:
                    act.wait_ge(mag_done, u % NCH + 1)
                part(act, s_err, n - 3)
                k, c = divmod(u, NCH)
                nc.scalar.activation(unit[:, u % 4], mag[:, c * CH:(c + 1) * CH], ACT.Identity,
                                     bias=sb["magic"][:, 0:1], scale=cur[:, 1, k:k + 1]).then_inc(s_tick, 1)

            def search_square(b, u):
                n = UB * b + u
                act.wait_ge(s_off, n + 1)
                nc.scalar.activation(unit[:, u % 4], unit[:, u % 4], ACT.Square).then_inc(s_sqr, 1)

            def body(b, attn, nxt):
                for j, now, before in steps(b, attn, nxt):
                    item = j % 2
                    if attn and j < NP:
                        exps(b, j)
                        search_tick(b, 2 * j)
                    if now:
                        squares(*now, item)
                    if attn and 1 <= j <= NP:
                        turn_probs(b, j - 1, 0)
                        search_square(b, 2 * j - 2)
                    if before:
                        turn(*before, 1 - item)
                    if attn and 2 <= j < NP + 2:
                        values(b, j - 2)
                    if attn and 1 <= j <= NP:
                        turn_probs(b, j - 1, 1)
                    if attn and j < NP:
                        search_tick(b, 2 * j + 1)
                    if now and item == 1:
                        squares(*now, 2)
                    if attn and 1 <= j <= NP:
                        turn_probs(b, j - 1, 2)
                        search_square(b, 2 * j - 1)
                    if before and item == 0:
                        turn(*before, 2)

            over_batches(act, body)

        @block.gpsimd
        def _(pool):
            PER_BATCH = NG * 6

            def rotate(g, B, item):
                n = 3 * (NG * B + g) + item
                link = Link(pool, pool_link, PER_BATCH * B + 6 * g + 2 * item)
                pool.wait_ge(proj_dve, n + 1)
                pool.wait_ge(proj_act, n + 1)
                if item < 2:
                    heads = slice(REP * g, REP * (g + 1))
                    part(pool, exp_done, NP * (B - 1) + 2 * g + 2)
                    pool.sem_inc(pool_gate, 1)
                    link(nc.gpsimd.tensor_scalar(qvar[:, item], ssq[:, item, heads], 1.0 / HD, RMS_EPS,
                                                 ALU.mult, ALU.add))
                    link(nc.gpsimd.tensor_tensor(qr[:, item], qvar[:, item], sb["neghalf"][:, 0:REP], ALU.pow))
                    pool.sem_inc(pool_gate, 1)
                    last = nc.gpsimd.tensor_scalar(qrms[:, item, heads], qr[:, item], HD ** -0.5, 1.0,
                                                   ALU.mult, ALU.mult)
                    if item == 1:
                        last.then_inc(q_scaled, 1)
                    part(pool, x_out, n if item == 0 else n - 2)
                    nc.gpsimd.tensor_tensor(rot[:, item], rc[:, item], rs[:, item], ALU.add).then_inc(rot_done, 1)
                else:
                    pool.sem_inc(pool_gate, 1)
                    link(nc.gpsimd.tensor_scalar(kvar[:], ssk[:, :, g], 1.0 / HD, RMS_EPS, ALU.mult, ALU.add))
                    nc.gpsimd.tensor_tensor(krms[:], kvar[:], sb["neghalf"][:, 0:TT], ALU.pow)
                    part(pool, x_out, n - 1)
                    link(nc.gpsimd.tensor_tensor(krot, rc[:, 0, 0:TT], rs[:, 0, 0:TT], ALU.add))
                    pool.sem_inc(pool_gate, 1)
                    for t in range(TT):
                        last = nc.gpsimd.tensor_scalar(rot[:, 0, t], rot[:, 0, t], krms[:, t:t + 1], 1.0,
                                                       ALU.mult, ALU.mult)
                    last.then_inc(rot_done, 1)
                    part(pool, scored, NP * (B - 1) + 2 * g + 2)
                    part(pool, o_out, NP * (B - 1) + 2 * g + 2)
                    for dst, src in ((kT_hi, "kcT_hi"), (kT_lo, "kcT_lo")):
                        nc.gpsimd.tensor_copy(dst[:, g, 0:T], sb[src][:, g, bass.ds(B * T, T)])
                    for dst, src in ((vctx_hi, "vc_hi"), (vctx_lo, "vc_lo")):
                        last = nc.gpsimd.tensor_copy(dst[:, g, :], sb[src][:, bass.ds(B, 1), g, :].rearrange(
                            "k b d -> k (b d)"))
                    last.then_inc(ctx_in, 1)

            def normalise(b, j):
                pool.wait_ge(inv_done, NP * b + j + 1)
                pool.sem_inc(pool_gate, 1)
                for i in range(2):
                    for t in range(TT):
                        p = prob[:, j % 2, i, OFF[t]:OFF[t] + ROW[t]]
                        last = nc.gpsimd.tensor_scalar(p, p, rinv[:, j % 2, t, i:i + 1], 1.0, ALU.mult, ALU.mult)
                last.then_inc(prob_done, 1)

            def search(b, u):
                n = UB * b + u
                k = u // NCH
                c = u % NCH
                pool.wait_ge(s_near, n + 1)
                pool.sem_inc(pool_gate, 1)
                nc.gpsimd.tensor_scalar(unit[:, u % 4], unit[:, u % 4], cur[:, 0, k:k + 1], 1.0,
                                        ALU.mult, ALU.mult).then_inc(s_nears, 1)
                pool.wait_ge(s_nears, n + 1)
                nc.gpsimd.tensor_tensor(unit[:, u % 4], unit[:, u % 4], mag[:, c * CH:(c + 1) * CH], ALU.subtract
                                        ).then_inc(s_off, 1)

            def body(b, attn, nxt):
                if attn:
                    part(pool, s_tick, UB * b)
                    part(pool, s_best, SB * b)
                    nc.gpsimd.tensor_copy(cur[:], sb["shrinks"][:, :, bass.ds(SB * b, SB)]).then_inc(cur_set, 1)
                    pool.wait_ge(cur_set, b + 1)
                for j, now, before in steps(b, attn, nxt):
                    item = j % 2
                    if attn and j < NP:
                        normalise(b, j)
                    if now:
                        rotate(*now, item)
                    if attn and j < NP:
                        search(b, 2 * j)
                    if now and item == 1:
                        rotate(*now, 2)
                    if attn and j < NP:
                        search(b, 2 * j + 1)

            over_batches(pool, body)

        @block.vector
        def _(dve):
            start = Link(dve, dve_link)
            HEAD_LINKS = 5

            blocks = Wf.rearrange("p (a b) -> p a b", b=QBLK)
            mb = mag[:].rearrange("p (a b) -> p a b", b=QBLK)
            start(nc.vector.tensor_scalar(mag[:].bitcast(U32), Wf.bitcast(U32), 0x7FFFFFFF, None, ALU.bitwise_and))
            start(nc.vector.tensor_reduce(err[:], mb, AX, ALU.max))
            start(nc.vector.tensor_scalar(sb["base"][:], err[:], 1e-8, 1.0 / QMAX, ALU.max, ALU.mult))
            start(nc.vector.reciprocal(upd[:], sb["base"][:]))
            nc.vector.memset(best_err[:], 3e38)
            start(nc.vector.memset(best[:], 1.0))
            for c in range(NCH):
                nc.vector.tensor_tensor(mb[:, c * CB:(c + 1) * CB], mb[:, c * CB:(c + 1) * CB],
                                        upd[:, c * CB:(c + 1) * CB].unsqueeze(2).to_broadcast([P, CB, QBLK]),
                                        ALU.mult).then_inc(mag_done, 1)

            def rope(g, B, item):
                n = 3 * (NG * B + g) + item
                dve.wait_ge(proj_act, n + 1)
                if item < 2:
                    part(dve, rot_done, n if item == 0 else n - 2)
                    cosw = sb["cosw"][:, 0, item].unsqueeze(1).to_broadcast([P, REP, HD])
                    nc.vector.tensor_tensor(rc[:, item], p_p[:], cosw, ALU.mult)
                    src = p_p[:].rearrange("p r (h d) -> p r h d", h=2)[:, :, ::-1, :]
                    sinw = sb["sinw"][:, 0, item].rearrange("p (a h d) -> p a h d", a=1, h=2
                                                            ).to_broadcast([P, REP, 2, HD // 2])
                    nc.vector.tensor_tensor(rs[:, item].rearrange("p r (h d) -> p r h d", h=2), src, sinw, ALU.mult
                                            ).then_inc(proj_dve, 1)
                else:
                    part(dve, rot_done, n - 1)
                    k = p_p[:].rearrange("p (t i) d -> p t i d", i=2)
                    nc.vector.tensor_tensor(rc[:, 0, 0:TT], k[:, :, 0, :], sb["cosw"][:, 1], ALU.mult)
                    src = k[:, :, 0, :].rearrange("p t (h d) -> p t h d", h=2)[:, :, ::-1, :]
                    nc.vector.tensor_tensor(rs[:, 0, 0:TT].rearrange("p t (h d) -> p t h d", h=2), src,
                                            sb["sinw"][:, 1].rearrange("p t (h d) -> p t h d", h=2), ALU.mult)
                    nc.vector.tensor_tensor(v_lo[:, :, g, :], k[:, :, 1, :], v_hi[:, :, g, :], ALU.subtract
                                            ).then_inc(proj_dve, 1)

            def turn(g, B, item):
                dve.wait_ge(x_hi, 3 * (NG * B + g) + item + 1)
                if item < 2:
                    at = slice(REP * g, REP * (g + 1)), slice(item * P, (item + 1) * P)
                    ins = nc.vector.tensor_tensor(qT_lo[:, at[0], at[1]], p_x[:], qT_hi[:, at[0], at[1]], ALU.subtract)
                else:
                    lo, hi = (z[:, g, T:KW].rearrange("p (t s) -> p t s", t=TT) for z in (kT_lo, kT_hi))
                    ins = nc.vector.tensor_tensor(lo, p_x[:, 0:TT, :], hi, ALU.subtract)
                ins.then_inc(x_lo, 1)

            def maxima(b, j, link):
                dve.wait_ge(scored, NP * b + j + 1)
                dve.wait_ge(q_scaled, NG * b + 2 * j // REP + 1)
                for i in range(2):
                    for t in range(TT):
                        last = nc.vector.tensor_reduce(smax[:, t, i:i + 1], p_s[i][:, OFF[t]:OFF[t] + ROW[t]],
                                                       AX, ALU.max)
                link(last)
                nc.vector.scalar_tensor_tensor(nbias[:, j % 2], smax[:], -1.0, qrms[:, :, 2 * j:2 * j + 2],
                                               ALU.mult, ALU.mult).then_inc(bias_done, 1)

            def inverses(b, j):
                dve.wait_ge(exp_done, NP * b + j + 1)
                nc.vector.reciprocal(rinv[:, j % 2], rsum[:, j % 2]).then_inc(inv_done, 1)

            def turn_probs(b, j, u):
                dve.wait_ge(t_hi, 3 * (NP * b + j) + u + 1)
                rows, wide = (T if u == 0 else P), (S if u == 2 else 2 * S)
                nc.vector.tensor_tensor(pT_lo[0:rows, j % 2, u, 0:wide], p_t[(j + u) % 2][0:rows, 0:wide],
                                        pT_hi[0:rows, j % 2, u, 0:wide], ALU.subtract).then_inc(t_lo, 1)

            def values(b, j):
                dve.wait_ge(o_hi, NP * b + j + 1)
                nc.vector.tensor_tensor(oT_lo[:, j % 2], p_o[:].rearrange("p i s -> p (i s)"), oT_hi[:, j % 2],
                                        ALU.subtract).then_inc(o_lo, 1)

            def search_near(b, u):
                n = UB * b + u
                dve.wait_ge(s_tick, n + 1)
                nc.vector.tensor_scalar(unit[:, u % 4], unit[:, u % 4], MAGIC + QMAX, -MAGIC, ALU.min, ALU.add
                                        ).then_inc(s_near, 1)

            def search_sum(b, u, link):
                n = UB * b + u
                k, c = divmod(u, NCH)
                dve.wait_ge(s_sqr, n + 1)
                nc.vector.tensor_reduce(err[:, c * CB:(c + 1) * CB],
                                        unit[:, u % 4].rearrange("p (a b) -> p a b", b=QBLK), AX, ALU.add
                                        ).then_inc(s_err, 1)
                if c == NCH - 1:
                    dve.wait_ge(s_err, n + 1)
                    link(nc.vector.tensor_tensor(upd[:], err[:], best_err[:], ALU.is_lt))
                    nc.vector.tensor_tensor(best_err[:], best_err[:], err[:], ALU.min)
                    link(nc.vector.tensor_scalar(keep_old[:], upd[:], -1.0, 1.0, ALU.mult, ALU.add))
                    link(nc.vector.tensor_tensor(best[:], best[:], keep_old[:], ALU.mult))
                    nc.vector.scalar_tensor_tensor(best[:], upd[:], cur[:, 0, k:k + 1], best[:],
                                                   ALU.mult, ALU.add).then_inc(s_best, 1)
                    dve.wait_ge(s_best, SB * b + k + 1)

            def body(b, attn, nxt):
                link = Link(dve, dve_link, HEAD_LINKS + (NP + 3 * SB) * b)
                for j, now, before in steps(b, attn, nxt):
                    item = j % 2
                    if attn and j < NP:
                        maxima(b, j, link)
                        search_near(b, 2 * j)
                    if now:
                        rope(*now, item)
                    if attn and j < NP:
                        inverses(b, j)
                    if attn and 1 <= j <= NP:
                        turn_probs(b, j - 1, 0)
                        search_sum(b, 2 * j - 2, link)
                    if before:
                        turn(*before, 1 - item)
                    if attn and 2 <= j < NP + 2:
                        values(b, j - 2)
                    if attn and 1 <= j <= NP:
                        turn_probs(b, j - 1, 1)
                    if attn and j < NP:
                        search_near(b, 2 * j + 1)
                    if now and item == 1:
                        rope(*now, 2)
                    if attn and 1 <= j <= NP:
                        turn_probs(b, j - 1, 2)
                        search_sum(b, 2 * j - 1, link)
                    if before and item == 0:
                        turn(*before, 2)
                if attn:
                    dve.wait_ge(wo_done, NP * (b + 1))
                    here = X[:, bass.ds(b * TT, TT), :]
                    nc.vector.tensor_tensor(here, p_y[:], here, ALU.add).then_inc(y_added, 1)

            over_batches(dve, body)


def block_d(nc, sb, out):
    with ExitStack() as ctx:
        def local(name, shape, dt):
            return ctx.enter_context(nc.sbuf_tensor(f"d_{name}", shape, dt))

        def sem(name):
            return ctx.enter_context(nc.semaphore(name))

        def bank(name, shape):
            return ctx.enter_context(nc.psum_tensor(f"d_{name}", shape, F32))

        X = sb["X"]
        GT = 4
        NGR = NB * TT // GT
        GS = GT * P
        CH, CB = 512, 512 // QBLK
        NCH = 2 * 2048 // CH
        Wf = sb["W"][:].rearrange("p m n -> p (m n)")
        fc_hi = local("fc_hi", [P, DH, F], BF16)
        fc_lo = local("fc_lo", [P, DH, F], BF16)
        pj_hi = local("pj_hi", [P, FK, D], BF16)
        pj_lo = local("pj_lo", [P, FK, D], BF16)
        step = local("step", [P, NBLK], F32)
        step_inv = local("step_inv", [P, NBLK], F32)
        unit = local("unit", [P, 2, CH], F32)
        tick = local("tick", [P, 2, CH], F32)
        near = local("near", [P, 2, CH], F32)
        deq = local("deq", [P, 2, CH], F32)
        moved = local("moved", [P, 2, CH], F32)
        wq = local("wq", [P, 2, CH], F32)
        stats = local("stats", [P, GT, 6], F32)
        mv = local("mv", [P, GT, 2], F32)
        var = local("var", [P, GT], F32)
        rstd = local("rstd", [P, GT], F32)
        xn = local("xn", [P, GT, D], F32)
        zT_hi = local("zT_hi", [P, 2, DH, GS], FP16)
        zT_lo = local("zT_lo", [P, 2, DH, GS], FP16)
        sq = local("sq", [P, 2, GS], F32)
        rect = local("rect", [P, 2, GS], F32)
        gT_hi = local("gT_hi", [P, 2, GS], BF16)
        gT_lo = local("gT_lo", [P, 2, GS], BF16)

        p_t = [bank(f"p_t{h}", [P, GS]) for h in range(DH)]
        p_h = [bank(f"p_h{i}", [P, GS]) for i in range(2)]
        p_y = [bank(f"p_y{i}", [P, 2, D]) for i in range(2)]

        deq_done, wq_done, w_out, w_hi, w_lo = (sem(x) for x in ("deq_done", "wq_done", "w_out", "w_hi", "w_lo"))
        norm_stat, norm_rstd, norm_done, turned, z_hi, z_lo = (sem(x) for x in (
            "d_norm_stat", "d_norm_rstd", "d_norm_done", "d_turned", "z_hi", "z_lo"))
        up_out, rect_done, sq_done, g_hi, g_lo, down_out, y_added, stored = (sem(x) for x in (
            "d_up_out", "rect_done", "sq_done", "g_hi", "g_lo", "d_down_out", "d_y_added", "stored"))
        dve_link, pool_link = sem("d_dve_link"), sem("d_pool_link")

        block = ctx.enter_context(nc.Block())

        def over_groups(body):
            body(-1, 1, False, True)
            for i in range(NGR):
                body(i, i % 2, True, i + 1 < NGR)
            body(NGR, NGR % 2, False, False)

        def weight_view(c, w):
            if c < NCH // 2:
                return [w[:, i * D + h * P:i * D + (h + 1) * P] for h in range(DH) for i in range(2)]
            return [w[:, i * P:(i + 1) * P] for i in range(4)]

        def weight_place(c, fc, pj):
            if c < NCH // 2:
                return fc[:, :, 2 * c * P:(2 * c + 2) * P], [DH, 2 * P]
            c -= NCH // 2
            h, k = c // 2, 4 * (c % 2)
            return pj[:, k:k + 4, h * P:(h + 1) * P], [4, P]

        @block.tensor
        def _(pe):
            def weights(c):
                pe.wait_ge(wq_done, c + 1)
                part(pe, w_lo, c - 1)
                for n, tile in enumerate(weight_view(c, wq[:, c % 2])):
                    last = nc.tensor.transpose(p_h[c % 2][:, n * P:(n + 1) * P], tile, sb["ident"][:])
                last.then_inc(w_out, 1)

            def up(i, k, slot):
                n = FK * i + k
                part(pe, sq_done, n - 1)
                for m, (h, a, c) in enumerate([(h, a, c) for h in range(DH) for a, c in ((0, 0), (0, 1), (1, 0))]):
                    w = (fc_hi, fc_lo)[a][:, h, k * P:(k + 1) * P]
                    z = (zT_hi, zT_lo)[c][:, slot, h, :]
                    last = nc.tensor.matmul(p_h[k % 2][:], w, z, start=m == 0, stop=m == 3 * DH - 1)
                last.then_inc(up_out, 1)

            def down(i, k):
                pe.wait_ge(g_lo, FK * i + k + 1)
                if k == 0:
                    part(pe, y_added, i)
                for t in range(GT):
                    for m, (a, c) in enumerate(((0, 0), (0, 1), (1, 0))):
                        g = (gT_hi, gT_lo)[a][:, k % 2, t * P:(t + 1) * P]
                        last = nc.tensor.matmul(p_y[t // 2][:, t % 2, :], g, (pj_hi, pj_lo)[c][:, k, :],
                                                start=k == 0 and t % 2 == 0 and m == 0,
                                                stop=k == FK - 1 and m == 2, skip_group_check=True)
                last.then_inc(down_out, 1)

            def turn(i):
                pe.wait_ge(norm_done, i + 1)
                part(pe, z_lo, DH * i)
                for h in range(DH):
                    for t in range(GT):
                        last = nc.tensor.transpose(p_t[h][:, t * P:(t + 1) * P], xn[:, t, h * P:(h + 1) * P],
                                                   sb["ident"][:])
                    last.then_inc(turned, 1)

            def body(i, slot, ffn, nxt):
                if i < 0:
                    turn(0)
                    for c in range(NCH):
                        weights(c)
                    pe.wait_ge(w_lo, NCH)
                    return
                for k in range(FK):
                    if ffn:
                        if k == 0:
                            pe.wait_ge(z_lo, DH * (i + 1))
                        up(i, k, slot)
                    m = FK * i + k - 2
                    if m >= 0 and m < FK * NGR:
                        down(m // FK, m % FK)
                    if nxt and k == 4:
                        turn(i + 1)

            over_groups(body)

        @block.scalar
        def _(act):
            def weights(c):
                act.wait_ge(w_out, c + 1)
                dst, (a, b) = weight_place(c, fc_hi, pj_hi)
                nc.scalar.copy(dst, p_h[c % 2][:].rearrange("p (a b) -> p a b", a=a)).then_inc(w_hi, 1)

            def turn(i, slot):
                for h in range(DH):
                    act.wait_ge(turned, DH * i + h + 1)
                    part(act, up_out, FK * (i - 1))
                    nc.scalar.copy(zT_hi[:, slot, h, :], p_t[h][:]).then_inc(z_hi, 1)

            def body(i, slot, ffn, nxt):
                if i < 0:
                    turn(0, 0)
                    for c in range(NCH):
                        weights(c)
                    return
                for k in range(FK):
                    if ffn:
                        n = FK * i + k
                        act.wait_ge(up_out, n + 1)
                        part(act, sq_done, n - 1)
                        nc.scalar.activation(rect[:, k % 2], p_h[k % 2][:], ACT.Relu).then_inc(rect_done, 1)
                        act.wait_ge(sq_done, n + 1)
                        part(act, down_out, n - 1)
                        nc.scalar.copy(gT_hi[:, k % 2], sq[:, k % 2]).then_inc(g_hi, 1)
                    if nxt and k == 4:
                        turn(i + 1, 1 - slot)

            over_groups(body)

        @block.gpsimd
        def _(pool):
            link = Link(pool, pool_link)

            def body(i, slot, ffn, nxt):
                if nxt:
                    pool.wait_ge(norm_stat, i + 2)
                    link(nc.gpsimd.tensor_scalar(var[:], mv[:, :, 1], 1.0, LN_EPS, ALU.mult, ALU.add))
                    nc.gpsimd.tensor_tensor(rstd[:], var[:], sb["neghalf"][:, 0:GT], ALU.pow).then_inc(norm_rstd, 1)
                if i < 0:
                    for c in range(NCH):
                        w = Wf[:, c * CH:(c + 1) * CH]
                        pool.wait_ge(deq_done, c + 1)
                        link(nc.gpsimd.tensor_tensor(moved[:, c % 2], deq[:, c % 2], w, ALU.subtract))
                        part(pool, w_out, c - 1)
                        nc.gpsimd.tensor_tensor(wq[:, c % 2], w, moved[:, c % 2], ALU.add).then_inc(wq_done, 1)

            over_groups(body)

        @block.vector
        def _(dve):
            link = Link(dve, dve_link)

            def dequantise(c):
                w = Wf[:, c * CH:(c + 1) * CH].rearrange("p (a b) -> p a b", b=QBLK)

                def wide(s):
                    return s[:, c * CB:(c + 1) * CB].unsqueeze(2).to_broadcast([P, CB, QBLK])

                def of(z):
                    return z[:, c % 2].rearrange("p (a b) -> p a b", b=QBLK)

                link(nc.vector.tensor_tensor(of(unit), w, wide(step_inv), ALU.mult))
                link(nc.vector.tensor_scalar(tick[:, c % 2], unit[:, c % 2], MAGIC, MAGIC - QMAX, ALU.add, ALU.max))
                link(nc.vector.tensor_scalar(near[:, c % 2], tick[:, c % 2], MAGIC + QMAX, -MAGIC, ALU.min, ALU.add))
                part(dve, wq_done, c - 1)
                nc.vector.tensor_tensor(of(deq), of(near), wide(step), ALU.mult).then_inc(deq_done, 1)

            def weights(c):
                dve.wait_ge(w_hi, c + 1)
                lo, (a, b) = weight_place(c, fc_lo, pj_lo)
                hi, _ = weight_place(c, fc_hi, pj_hi)
                nc.vector.tensor_tensor(lo, p_h[c % 2][:].rearrange("p (a b) -> p a b", a=a), hi, ALU.subtract
                                        ).then_inc(w_lo, 1)

            def stat(i):
                for t in range(GT):
                    last = nc.vector.bn_stats(stats[:, t, :], X[:, GT * i + t, :])
                link(last)
                for t in range(GT):
                    last = nc.vector.bn_aggr(mv[:, t, :], stats[:, t, :])
                last.then_inc(norm_stat, 1)

            def normed(i):
                dve.wait_ge(norm_rstd, i + 1)
                part(dve, turned, DH * i)
                for t in range(GT):
                    last = nc.vector.tensor_scalar(xn[:, t, :], X[:, GT * i + t, :], mv[:, t, 0:1], rstd[:, t:t + 1],
                                                   ALU.subtract, ALU.mult)
                last.then_inc(norm_done, 1)

            def turn(i, slot):
                for h in range(DH):
                    dve.wait_ge(z_hi, DH * i + h + 1)
                    nc.vector.tensor_tensor(zT_lo[:, slot, h, :], p_t[h][:], zT_hi[:, slot, h, :], ALU.subtract
                                            ).then_inc(z_lo, 1)

            def square(i, k):
                n = FK * i + k
                dve.wait_ge(rect_done, n + 1)
                part(dve, g_lo, n - 1)
                nc.vector.tensor_tensor(sq[:, k % 2], rect[:, k % 2], rect[:, k % 2], ALU.mult).then_inc(sq_done, 1)

            def rest(i, k):
                n = FK * i + k
                dve.wait_ge(g_hi, n + 1)
                nc.vector.tensor_tensor(gT_lo[:, k % 2], sq[:, k % 2], gT_hi[:, k % 2], ALU.subtract
                                        ).then_inc(g_lo, 1)

            def add(i):
                dve.wait_ge(down_out, FK * (i + 1))
                for s in range(2):
                    here = X[:, GT * i + 2 * s:GT * i + 2 * s + 2, :]
                    last = nc.vector.tensor_tensor(here, p_y[s][:], here, ALU.add)
                last.then_inc(y_added, 1)

            def body(i, slot, ffn, nxt):
                if i < 0:
                    stat(0)
                    link(nc.vector.tensor_tensor(step[:], sb["base"][:], sb["best"][:], ALU.mult))
                    link(nc.vector.reciprocal(step_inv[:], step[:]))
                    dequantise(0)
                    normed(0)
                    dequantise(1)
                    turn(0, 0)
                    for c in range(NCH):
                        weights(c)
                        if c + 2 < NCH:
                            dequantise(c + 2)
                    return
                if nxt:
                    stat(i + 1)
                for k in range(FK):
                    if ffn:
                        square(i, k)
                        if nxt and k == 2:
                            normed(i + 1)
                        rest(i, k)
                    if i > 0 and k == 1:
                        add(i - 1)
                    if nxt and k == 4:
                        turn(i + 1, 1 - slot)

            over_groups(body)

        @block.sync
        def _(sp):
            for i in range(NGR):
                sp.wait_ge(y_added, i + 1)
                for s in range(GT // TT):
                    b = GT // TT * i + s
                    sp.dma_start(out[b].rearrange("(t p) d -> p t d", p=P), X[:, TT * b:TT * (b + 1), :]
                                 ).then_inc(stored, 16)
            sp.wait_ge(stored, 16 * NB)


def program(nc, out, **dr):
    with ExitStack() as ctx:
        sb = {}

        def keep(name, shape, dt, where=None):
            sb[name] = (where or ctx).enter_context(nc.sbuf_tensor(f"{name}", shape, dt))

        keep("X", [P, NB * TT, D], F32)
        keep("W", [P, 2, 2048], F32)
        keep("wq_hi", [P, DH, NH * HD], BF16)
        keep("wq_lo", [P, DH, NH * HD], BF16)
        keep("wkv_hi", [P, DH, NG * 2 * HD], BF16)
        keep("wkv_lo", [P, DH, NG * 2 * HD], BF16)
        keep("wo_hi", [P, NH, D], BF16)
        keep("wo_lo", [P, NH, D], BF16)
        keep("xT_hi", [P, NB, DH, S], FP16)
        keep("xT_lo", [P, NB, DH, S], FP16)
        keep("kcT_hi", [P, NG, NB * T], BF16)
        keep("kcT_lo", [P, NG, NB * T], BF16)
        keep("vc_hi", [T, NB, NG, HD], BF16)
        keep("vc_lo", [T, NB, NG, HD], BF16)
        keep("cosw", [P, 2, TT, HD], F32)
        keep("sinw", [P, 2, TT, HD], F32)
        keep("shrinks", [P, 2, NSHRINK], F32)
        keep("ident", [P, P], F32)
        keep("ident16", [P, P], BF16)
        keep("causal", [P, P], BF16)
        keep("neghalf", [P, 8], F32)
        keep("magic", [P, 1], F32)
        keep("base", [P, NBLK], F32)
        keep("best", [P, NBLK], F32)
        with ExitStack() as early:
            keep("w4", [P, 2, 2048], BF16, early)
            keep("ctxT_hi", [P, DH, NB * T], BF16, early)
            keep("ctxT_lo", [P, DH, NB * T], BF16, early)
            keep("ctx_hi", [T, NB, D], BF16, early)
            keep("ctx_lo", [T, NB, D], BF16, early)
            keep("keep", [P, NB, T], F32, early)
            keep("drop", [P, NB, T], F32, early)
            keep("valid", [P, NB], F32, early)
            keep("rope", [P, 2, TT, HD], F32, early)
            keep("norms", [P, 2, HD], F32, early)
            keep("up_b", [P, FK], F32, early)
            keep("down_b", [P, D], F32, early)
            block_a(nc, dr, sb, ctx)
            block_b(nc, dr, sb)
        block_c(nc, sb)
        block_d(nc, sb, out)


_OUT = (NB, S, D)


def kernel(**inputs):
    import numpy as np
    import concourse.bacc as bacc
    from concourse.bass_utils import run_bass_kernel_spmd as run

    names = {
        "x": "x", "ctx": "ctx_2048", "mask": "mask_BxS2_bk0", "up": "L0_ffn_up_kernel", "up_b": "L0_ffn_up_bias",
        "down": "L0_ffn_down_kernel", "down_b": "L0_ffn_down_bias", "wq": "L1_xattn_wq", "wk": "L1_xattn_wk",
        "wv": "L1_xattn_wv", "wo": "L1_xattn_wo", "wk_ctx": "L1_xattn_wk_ctx", "wv_ctx": "L1_xattn_wv_ctx",
        "q_norm": "L1_xattn_q_norm_w", "k_norm": "L1_xattn_k_norm_w", "w_fc": "L1_ffn_w_fc",
        "w_proj": "L1_ffn_w_proj",
    }
    arrays = {k: np.ascontiguousarray(inputs[n]) for k, n in names.items()}
    freq = np.float32(1.0) / np.float32(10000.0) ** (np.arange(0, HD, 2, dtype=np.float32) / np.float32(HD))
    angle = np.outer(np.arange(S, dtype=np.float32), freq.astype(np.float32)).astype(np.float32)
    arrays["cos"] = np.concatenate([np.cos(angle)] * 2, -1).astype(np.float32)
    arrays["sin"] = np.concatenate([-np.sin(angle), np.sin(angle)], -1).astype(np.float32)
    shrinks = np.linspace(0.4, 1.0, NSHRINK).astype(np.float32)
    arrays["shrinks"] = np.stack([shrinks, np.float32(1.0) / shrinks]).astype(np.float32)
    arrays["ident"] = np.eye(P, dtype=np.float32)

    nc = bacc.Bacc("TRN2", target_bir_lowering=False, num_devices=1)
    given, aps = {}, {}
    for k, a in arrays.items():
        given[f"in_{k}"] = a
        aps[k] = nc.dram_tensor(f"in_{k}", a.shape, mybir.dt.from_np(a.dtype), kind="ExternalInput").ap()
    out = nc.dram_tensor("out", _OUT, F32, kind="ExternalOutput").ap()
    program(nc, out, **aps)
    return run(nc, [given], core_ids=[0]).results[0]["out"]
```

```python
from contextlib import ExitStack

import concourse.bass as bass
from concourse import mybir

P = 128
F32 = mybir.dt.float32
BF16 = mybir.dt.bfloat16
FP16 = mybir.dt.float16
U8 = mybir.dt.uint8
U32 = mybir.dt.uint32
ALU = mybir.AluOpType
ACT = mybir.ActivationFunctionType
AX = mybir.AxisListType.X

NB, S, D = 8, 256, 256
T = 64
DH = D // P
TT = S // P
F = 1024
FK = F // P
NH, NG, HD = 16, 4, 128
REP = NH // NG
NP = NH // 2
LN_EPS, RMS_EPS = 1e-5, 1e-6
QBLK = 64
NBLK = 2 * F * D // QBLK // P
QMAX = 15.0
NSHRINK = 16
MAGIC = 1.5 * 2.0 ** 23
HALF_STEP = 1.5 * 2.0 ** 22
NEG = 1e30


def part(eng, sem, value):
    if not isinstance(value, int) or value > 0:
        eng.wait_ge(sem, value)


class Link:

    def __init__(self, eng, sem, base=0):
        self.eng, self.sem, self.base, self.n = eng, sem, base, 0

    def __call__(self, ins):
        self.n += 1
        ins.then_inc(self.sem, 1)
        self.eng.wait_ge(self.sem, self.base + self.n)


class Search:
    CH = 512
    CB = CH // QBLK
    UNITS = 2 * 2048 // CH
    LINKS = 3

    def __init__(self, nc, sb, sem, name, first):
        self.nc, self.sb, self.first = nc, sb, first
        self.loaded, self.ticked, self.neared, self.scaled, self.off, self.squared, self.summed, self.chosen = (
            sem(f"{name}_{x}") for x in ("shrink_loaded", "ticked", "neared", "scaled", "off", "squared",
                                         "summed", "chosen"))
        self.gate = sem(f"{name}_search_gate")

    def slot(self, u):
        return self.sb["unit"][:, u % 2]

    def mag(self, u):
        return self.sb["mag"][:, u * self.CH:(u + 1) * self.CH]

    def load(self, pool, b):
        part(pool, self.chosen, b)
        self.nc.gpsimd.tensor_copy(self.sb["cur"][:], self.sb["shrinks"][:, :, bass.ds(self.first + b, 1)]
                                   ).then_inc(self.loaded, 1)

    def tick(self, act, b, u):
        n = self.UNITS * b + u
        act.wait_ge(self.loaded, b + 1)
        part(act, self.summed, n - 1)
        self.nc.scalar.activation(self.slot(u), self.mag(u), ACT.Identity, bias=self.sb["magic"][:, 0:1],
                                  scale=self.sb["cur"][:, 1]).then_inc(self.ticked, 1)

    def near(self, dve, b, u):
        dve.wait_ge(self.ticked, self.UNITS * b + u + 1)
        self.nc.vector.tensor_scalar(self.slot(u), self.slot(u), MAGIC + QMAX, -MAGIC, ALU.min, ALU.add
                                     ).then_inc(self.neared, 1)

    def distance(self, pool, b, u):
        n = self.UNITS * b + u
        pool.wait_ge(self.neared, n + 1)
        pool.sem_inc(self.gate, 1)
        self.nc.gpsimd.tensor_scalar(self.slot(u), self.slot(u), self.sb["cur"][:, 0], 1.0, ALU.mult, ALU.mult
                                     ).then_inc(self.scaled, 1)
        pool.wait_ge(self.scaled, n + 1)
        self.nc.gpsimd.tensor_tensor(self.slot(u), self.slot(u), self.mag(u), ALU.subtract).then_inc(self.off, 1)

    def square(self, act, b, u):
        act.wait_ge(self.off, self.UNITS * b + u + 1)
        self.nc.scalar.activation(self.slot(u), self.slot(u), ACT.Square).then_inc(self.squared, 1)

    def total(self, dve, b, u, link):
        n = self.UNITS * b + u
        nc, sb = self.nc, self.sb
        dve.wait_ge(self.squared, n + 1)
        nc.vector.tensor_reduce(sb["err"][:, u * self.CB:(u + 1) * self.CB],
                                self.slot(u).rearrange("p (a b) -> p a b", b=QBLK), AX, ALU.add
                                ).then_inc(self.summed, 1)
        if u == self.UNITS - 1:
            dve.wait_ge(self.summed, n + 1)
            link(nc.vector.tensor_tensor(sb["upd"][:], sb["err"][:], sb["best_err"][:], ALU.is_lt))
            nc.vector.tensor_tensor(sb["best_err"][:], sb["best_err"][:], sb["err"][:], ALU.min)
            link(nc.vector.tensor_scalar(sb["stay"][:], sb["upd"][:], -1.0, 1.0, ALU.mult, ALU.add))
            link(nc.vector.tensor_tensor(sb["best"][:], sb["best"][:], sb["stay"][:], ALU.mult))
            nc.vector.scalar_tensor_tensor(sb["best"][:], sb["upd"][:], sb["cur"][:, 0], sb["best"][:],
                                           ALU.mult, ALU.add).then_inc(self.chosen, 1)
            dve.wait_ge(self.chosen, b + 1)


def block_a(nc, dr, sb, ex):
    with ExitStack() as ctx:
        def local(name, shape, dt):
            return ctx.enter_context(nc.sbuf_tensor(f"a_{name}", shape, dt))

        def sem(name):
            return ctx.enter_context(nc.semaphore(name))

        stage_q = sb["mag"][:].rearrange("p (h n) -> p h n", h=DH)
        stage_c = sb["xT_hi"][:].rearrange("p b h s -> p (b h s)").bitcast(F32
            ).rearrange("p (h g i d) -> p h g i d", h=DH, g=NG, i=2)
        stage_kv = stage_c
        stage_f = sb["W"]
        ctx_rows = local("ctx_rows", [P, NB // 2, D], F32)
        ctx_keys = sb["xT_lo"][0:T].rearrange("p b h s -> p (b h s)").bitcast(F32
            ).rearrange("p (b d) -> p b d", b=NB)
        wc_hi = local("wc_hi", [P, DH, NG * 2 * HD], BF16)
        wc_lo = local("wc_lo", [P, DH, NG * 2 * HD], BF16)
        vf_hi = local("vf_hi", [P, NB // 2, NG, HD], BF16)
        vf_lo = local("vf_lo", [P, NB // 2, NG, HD], BF16)
        knorm = local("knorm", [P, HD], F32)
        mask8 = local("mask8", [P, NB, T], U8)
        CH = 512
        blk = local("blk", [P, CH], F32)
        trunc = local("trunc", [P, CH], F32)
        expo = local("expo", [P, CH], F32)
        rnd = local("rnd", [P, CH], F32)
        quant = local("quant", [P, CH], F32)
        back = local("back", [P, 2, CH], F32)
        amax = local("amax", [P, CH // 32], F32)
        scale = local("scale", [P, CH // 32], F32)
        top = local("top", [P, CH // 32], F32)
        junk = local("junk", [P, 2, 2, HD], BF16)
        ssq = local("ssq", [P, 8, 2], F32)
        kraw = local("kraw", [P, 2, 2, HD], F32)
        kn = local("kn", [P, 2, 2, HD], F32)
        krms = local("krms", [P, 2, 2], F32)
        kvar = local("kvar", [P, 2, 2], F32)

        p_ctx = [ctx.enter_context(nc.psum_tensor(f"p_ctx{i}", [P, 512], F32)) for i in range(2)]
        p_kv = [ctx.enter_context(nc.psum_tensor(f"p_kv{i}", [P, 2, 2, HD], F32)) for i in range(2)]
        p_kt = [ctx.enter_context(nc.psum_tensor(f"p_kt{i}", [P, 2, P], F32)) for i in range(2)]

        ld_x, ld_ctx, ld_rows = sem("ld_x"), sem("ld_ctx"), sem("ld_rows")
        ld_tab, ld_mask, ld_up, ld_down = sem("ld_tab"), sem("ld_mask"), sem("ld_up"), sem("ld_down")
        ld_c, ld_q, ld_kv, ld_o = sem("ld_c"), sem("ld_q"), sem("ld_kv"), sem("ld_o")
        ld_small = sem("ld_small")
        hi_done, lo_done = sem("a_hi_done"), sem("a_lo_done")
        rows_t, ctx_hi_done, ctx_lo_done = sem("rows_t"), sem("ctx_hi_done"), sem("ctx_lo_done")
        kv_out, kv_act, kv_dve = sem("kv_out"), sem("kv_act"), sem("kv_dve")
        kn_done, kt_out, kt_hi, kt_lo = sem("kn_done"), sem("kt_out"), sem("kt_hi"), sem("kt_lo")
        fp4_done, fp4_copied = sem("fp4_done"), sem("fp4_copied")
        shifted, dve_link, pool_link = sem("shifted"), sem("a_dve_link"), sem("a_pool_link")
        half_set = sem("half_set")

        block = ctx.enter_context(nc.Block())
        units = [(r, gp) for r in range(NB // 2) for gp in range(2)]

        @block.sync
        def _(sp):
            sp.dma_start(stage_f[:, 0, :].rearrange("p (h n) -> p h n", h=DH),
                         dr["up"].rearrange("(h p) n -> p h n", p=P)).then_inc(ld_up, 16)
            sp.dma_start(ctx_rows[:], dr["ctx"].rearrange("(r b) k d -> (b k) r d", b=2)
                         ).then_inc(ld_rows, 16)
            sp.dma_start(sb["ident"][:], dr["ident"]).then_inc(ld_rows, 16)
            for i, w in enumerate(("wk_ctx", "wv_ctx")):
                for h in range(DH):
                    sp.dma_start(stage_c[:, h, :, i, :],
                                 dr[w][h * P:(h + 1) * P, :].rearrange("p (g d) -> p g d", g=NG)
                                 ).then_inc(ld_c, 16)
            sp.dma_start(stage_f[:, 1, :].rearrange("p (k n) -> p k n", k=FK),
                         dr["down"].rearrange("(k p) n -> p k n", p=P)).then_inc(ld_down, 16)
            sp.dma_start(sb["X"][:], dr["x"].rearrange("b (t p) d -> p (b t) d", p=P)).then_inc(ld_x, 16)
            sp.wait_ge(kv_act, len(units))
            sp.wait_ge(kv_dve, len(units))
            for dst, src in ((sb["vc_hi"], vf_hi), (sb["vc_lo"], vf_lo)):
                for half in range(2):
                    sp.dma_start(dst[:].rearrange("k (r b) g d -> k b r (g d)", b=2)[:, half],
                                 src[half * T:(half + 1) * T].rearrange("k r g d -> k r (g d)")
                                 ).then_inc(shifted, 16)
            for s, n in ((ld_x, 1), (shifted, 4)):
                sp.wait_ge(s, 16 * n)

        @block.scalar
        def _(act):
            act.dma_start(knorm[:], dr["k_norm"].partition_broadcast(P)).then_inc(ld_small, 16)
            act.dma_start(mask8[:], dr["mask"].partition_broadcast(P)).then_inc(ld_mask, 16)
            act.dma_start(ctx_keys, dr["ctx"].rearrange("b k d -> k b d")).then_inc(ld_ctx, 16)
            act.dma_start(stage_q, dr["wq"].rearrange("(h p) n -> p h n", p=P)).then_inc(ld_q, 16)
            act.wait_ge(ld_c, 64)
            nc.scalar.copy(wc_hi[:], stage_c.rearrange("p h g i d -> p h (g i d)")).then_inc(hi_done, 1)
            act.wait_ge(hi_done, 1)
            act.wait_ge(lo_done, 1)
            for i, w in enumerate(("wk", "wv")):
                for h in range(DH):
                    act.dma_start(stage_kv[:, h, :, i, :],
                                  dr[w][h * P:(h + 1) * P, :].rearrange("p (g d) -> p g d", g=NG)
                                  ).then_inc(ld_kv, 16)
            act.dma_start(sb["rope"][:, 0], dr["cos"].rearrange("(t p) d -> p t d", p=P)).then_inc(ld_tab, 16)
            act.dma_start(sb["rope"][:, 1], dr["sin"].rearrange("(t p) d -> p t d", p=P)).then_inc(ld_tab, 16)
            act.dma_start(sb["norms"][:, 0], dr["q_norm"].partition_broadcast(P)).then_inc(ld_tab, 16)
            act.dma_start(sb["norms"][:, 1], dr["k_norm"].partition_broadcast(P)).then_inc(ld_tab, 16)
            with nc.allow_non_contiguous_dma(reason="4 KB, once"):
                act.dma_start(sb["up_b"][:], dr["up_b"].rearrange("(k p) -> p k", p=P)).then_inc(ld_tab, 16)
            act.dma_start(sb["down_b"][:], dr["down_b"].partition_broadcast(P)).then_inc(ld_tab, 16)
            act.dma_start(sb["shrinks"][:], dr["shrinks"].partition_broadcast(P)).then_inc(ld_tab, 16)
            for h in range(DH):
                act.wait_ge(rows_t, h + 1)
                nc.scalar.copy(sb["ctxT_hi"][:, h], p_ctx[h][:]).then_inc(ctx_hi_done, 1)
            act.wait_ge(ld_ctx, 16)
            nc.scalar.copy(sb["ctx_hi"][:], ctx_keys).then_inc(hi_done, 1)

            def kt_copy(u):
                r, gp = units[u]
                act.wait_ge(kt_out, u + 1)
                nc.scalar.copy(sb["kcT_hi"][:, 2 * gp:2 * gp + 2, r * P:(r + 1) * P], p_kt[u % 2][:]
                               ).then_inc(kt_hi, 1)

            def fp4_copy(c):
                act.wait_ge(fp4_done, c + 1)
                nc.scalar.copy(sb["w4"][:, c // 4, (c % 4) * CH:(c % 4 + 1) * CH], back[:, c % 2]
                               ).then_inc(fp4_copied, 1)

            for u, (r, gp) in enumerate(units):
                fp4_copy(u)
                act.wait_ge(kv_out, u + 1)
                for i in range(2):
                    nc.scalar.activation(junk[:, u % 2, i], p_kv[u % 2][:, i, 0, :], ACT.Square,
                                         accum_out=ssq[:, u, i:i + 1])
                nc.scalar.copy(vf_hi[:, r, 2 * gp:2 * gp + 2, :], p_kv[u % 2][:, :, 1, :]).then_inc(kv_act, 1)
                if u >= 1:
                    kt_copy(u - 1)
            kt_copy(len(units) - 1)
            act.wait_ge(ld_q, 16)
            nc.scalar.copy(sb["wq_hi"][:], stage_q).then_inc(hi_done, 1)
            act.wait_ge(ld_kv, 64)
            nc.scalar.copy(sb["wkv_hi"][:], stage_kv.rearrange("p h g i d -> p h (g i d)")).then_inc(hi_done, 1)
            act.wait_ge(hi_done, 4)
            act.wait_ge(lo_done, 4)
            act.dma_start(stage_q.rearrange("p h (k n) -> p (h k) n", n=D),
                          dr["wo"].rearrange("(k p) n -> p k n", p=P)).then_inc(ld_o, 16)
            act.wait_ge(ld_o, 16)
            nc.scalar.copy(sb["wo_hi"][:], stage_q.rearrange("p h (k n) -> p (h k) n", n=D)).then_inc(hi_done, 1)
            act.wait_ge(ld_tab, 16 * 7)

        @block.gpsimd
        def _(pool):
            link = Link(pool, pool_link)
            nc.gpsimd.memset(sb["magic"][:], MAGIC)
            nc.gpsimd.memset(sb["neghalf"][:], -0.5).then_inc(half_set, 1)
            pool.wait_ge(half_set, 1)
            pool.wait_ge(hi_done, 1)
            nc.gpsimd.tensor_tensor(wc_lo[:], stage_c.rearrange("p h g i d -> p h (g i d)"), wc_hi[:],
                                    ALU.subtract).then_inc(lo_done, 1)

            def kn_unit(u):
                pool.wait_ge(kv_act, u + 1)
                pool.wait_ge(kv_dve, u + 1)
                link(nc.gpsimd.tensor_scalar(kvar[:, u % 2], ssq[:, u], 1.0 / HD, RMS_EPS, ALU.mult, ALU.add))
                link(nc.gpsimd.tensor_tensor(krms[:, u % 2], kvar[:, u % 2], sb["neghalf"][:, 0:2], ALU.pow))
                if u >= 2:
                    pool.wait_ge(kt_out, u - 1)
                for i in range(2):
                    last = nc.gpsimd.tensor_scalar(kn[:, u % 2, i], kraw[:, u % 2, i], krms[:, u % 2, i:i + 1],
                                                   1.0, ALU.mult, ALU.mult)
                last.then_inc(kn_done, 1)

            for u in range(4):
                kn_unit(u)
            pool.wait_ge(hi_done, 2)
            nc.gpsimd.tensor_tensor(sb["ctx_lo"][:], ctx_keys, sb["ctx_hi"][:], ALU.subtract
                                    ).then_inc(lo_done, 1)
            for u in range(4, 8):
                kn_unit(u)
            pool.wait_ge(hi_done, 3)
            nc.gpsimd.tensor_tensor(sb["wq_lo"][:], stage_q, sb["wq_hi"][:], ALU.subtract).then_inc(lo_done, 1)
            pool.wait_ge(hi_done, 4)
            nc.gpsimd.tensor_tensor(sb["wkv_lo"][:], stage_kv.rearrange("p h g i d -> p h (g i d)"),
                                    sb["wkv_hi"][:], ALU.subtract).then_inc(lo_done, 1)
            pool.wait_ge(hi_done, 5)
            nc.gpsimd.tensor_tensor(sb["wo_lo"][:], stage_q.rearrange("p h (k n) -> p (h k) n", n=D),
                                    sb["wo_hi"][:], ALU.subtract).then_inc(lo_done, 1)
            pool.wait_ge(ld_mask, 16)
            nc.gpsimd.tensor_copy(sb["keep"][:], mask8[:]).then_inc(half_set, 1)
            pool.wait_ge(half_set, 2)
            nc.gpsimd.tensor_scalar(sb["drop"][:], sb["keep"][:], -1.0, NEG, ALU.add, ALU.mult
                                    ).then_inc(half_set, 1)
            nc.gpsimd.memset(sb["causal"][:], 0.0).then_inc(half_set, 1)
            pool.wait_ge(half_set, 4)
            nc.gpsimd.affine_select(out=sb["causal"][:], in_=sb["causal"][:], compare_op=ALU.is_ge, fill=-NEG,
                                    base=0, pattern=[[-1, P]], channel_multiplier=1).then_inc(half_set, 1)
            pool.wait_ge(ld_rows, 32)
            nc.gpsimd.tensor_copy(sb["ident16"][:], sb["ident"][:]).then_inc(half_set, 1)

        @block.vector
        def _(dve):
            link = Link(dve, dve_link)

            def fp4(c):
                dve.wait_ge(ld_up if c < 4 else ld_down, 16)
                src = stage_f[:, c // 4, (c % 4) * CH:(c % 4 + 1) * CH]
                link(nc.vector.transpose(blk[:], src))
                bits = blk[:].bitcast(U32)
                nc.vector.tensor_scalar(trunc[:].bitcast(U32), bits, 0x7FE00000, None, ALU.bitwise_and)
                link(nc.vector.tensor_scalar(expo[:].bitcast(U32), bits, 0x7F800000, None, ALU.bitwise_and))
                link(nc.vector.tensor_reduce(amax[:], trunc[:].rearrange("p (a b) -> p a b", b=32), AX, ALU.max))
                link(nc.vector.tensor_scalar(scale[:], amax[:], 1e-30, None, ALU.max))
                link(nc.vector.tensor_scalar(top[:].bitcast(U32), scale[:].bitcast(U32), 0x7F800000, None,
                                             ALU.bitwise_and))
                link(nc.vector.tensor_scalar(scale[:], top[:], 0.25, None, ALU.mult))
                link(nc.vector.tensor_scalar(top[:], scale[:], 6.0, None, ALU.mult))
                wide = [P, CH // 32, 32]
                e3 = expo[:].rearrange("p (a b) -> p a b", b=32)
                q3 = quant[:].rearrange("p (a b) -> p a b", b=32)
                link(nc.vector.tensor_tensor(e3, e3, scale[:].unsqueeze(2).to_broadcast(wide), ALU.max))
                link(nc.vector.tensor_scalar(trunc[:], trunc[:], 1.0625, None, ALU.mult))
                link(nc.vector.scalar_tensor_tensor(rnd[:], expo[:], HALF_STEP, trunc[:], ALU.mult, ALU.add))
                link(nc.vector.scalar_tensor_tensor(quant[:], expo[:], -HALF_STEP, rnd[:], ALU.mult, ALU.add))
                link(nc.vector.tensor_tensor(q3, q3, top[:].unsqueeze(2).to_broadcast(wide), ALU.min))
                link(nc.vector.scalar_tensor_tensor(rnd[:].bitcast(U32), bits, 0x80000000, quant[:].bitcast(U32),
                                                    ALU.bitwise_and, ALU.bitwise_or))
                if c >= 2:
                    dve.wait_ge(fp4_copied, c - 1)
                nc.vector.transpose(back[:, c % 2], rnd[:]).then_inc(fp4_done, 1)

            def kt_copy(u):
                r, gp = units[u]
                dve.wait_ge(kt_hi, u + 1)
                at = slice(2 * gp, 2 * gp + 2), slice(r * P, (r + 1) * P)
                nc.vector.tensor_tensor(sb["kcT_lo"][:, at[0], at[1]], p_kt[u % 2][:],
                                        sb["kcT_hi"][:, at[0], at[1]], ALU.subtract).then_inc(kt_lo, 1)

            fp4(0)
            fp4(1)
            for h in range(DH):
                dve.wait_ge(ctx_hi_done, h + 1)
                nc.vector.tensor_tensor(sb["ctxT_lo"][:, h], p_ctx[h][:], sb["ctxT_hi"][:, h], ALU.subtract
                                        ).then_inc(ctx_lo_done, 1)
            dve.wait_ge(ld_small, 16)
            for u, (r, gp) in enumerate(units):
                if u < 6:
                    fp4(u + 2)
                dve.wait_ge(kv_act, u + 1)
                if u >= 2:
                    dve.wait_ge(kn_done, u - 1)
                nc.vector.tensor_tensor(kraw[:, u % 2], p_kv[u % 2][:, :, 0, :],
                                        knorm[:].unsqueeze(1).to_broadcast([P, 2, HD]), ALU.mult)
                nc.vector.tensor_tensor(vf_lo[:, r, 2 * gp:2 * gp + 2, :], p_kv[u % 2][:, :, 1, :],
                                        vf_hi[:, r, 2 * gp:2 * gp + 2, :], ALU.subtract).then_inc(kv_dve, 1)
                if u >= 1:
                    kt_copy(u - 1)
            kt_copy(len(units) - 1)
            dve.wait_ge(half_set, 2)
            nc.vector.tensor_reduce(sb["valid"][:], sb["keep"][:], AX, ALU.max)
            dve.wait_ge(ld_tab, 16 * 7)
            for i in range(2):
                nrm = sb["norms"][:, i].rearrange("p (a d) -> p a d", a=1).to_broadcast([P, TT, HD])
                nc.vector.tensor_tensor(sb["cosw"][:, i], sb["rope"][:, 0], nrm, ALU.mult)
                swapped = sb["norms"][:, i].rearrange("p (a h d) -> p a h d", a=1, h=2)[:, :, ::-1, :]
                for t in range(TT):
                    nc.vector.tensor_tensor(sb["sinw"][:, i, t].rearrange("p (h d) -> p h d", h=2),
                                            sb["rope"][:, 1, t].rearrange("p (h d) -> p h d", h=2),
                                            swapped[:, 0], ALU.mult)

        @block.tensor
        def _(pe):
            pe.wait_ge(ld_rows, 32)
            for h in range(DH):
                for r in range(NB // 2):
                    last = nc.tensor.transpose(p_ctx[h][:, r * P:(r + 1) * P],
                                               ctx_rows[:, r, h * P:(h + 1) * P], sb["ident"][:])
                last.then_inc(rows_t, 1)
            pe.wait_ge(hi_done, 1)
            pe.wait_ge(lo_done, 1)
            pe.wait_ge(ctx_lo_done, DH)

            def kt_unit(u):
                pe.wait_ge(kn_done, u + 1)
                if u >= 2:
                    pe.wait_ge(kt_lo, u - 1)
                for i in range(2):
                    last = nc.tensor.transpose(p_kt[u % 2][:, i, :], kn[:, u % 2, i], sb["ident"][:])
                last.then_inc(kt_out, 1)

            for u, (r, gp) in enumerate(units):
                if u >= 2:
                    pe.wait_ge(kv_act, u - 1)
                    pe.wait_ge(kv_dve, u - 1)
                n = 0
                for h in range(DH):
                    rows = [sb[k][:, h, r * P:(r + 1) * P] for k in ("ctxT_hi", "ctxT_lo")]
                    cols = [w[:, h, gp * 512:(gp + 1) * 512] for w in (wc_hi, wc_lo)]
                    for a, b in ((0, 0), (0, 1), (1, 0)):
                        last = nc.tensor.matmul(p_kv[u % 2][:].rearrange("p g i d -> p (g i d)"),
                                                rows[a], cols[b], start=n == 0, stop=n == 3 * DH - 1)
                        n += 1
                last.then_inc(kv_out, 1)
                if u >= 1:
                    kt_unit(u - 1)
            kt_unit(len(units) - 1)



def block_b(nc, dr, sb):
    with ExitStack() as ctx:
        def local(name, shape, dt):
            return ctx.enter_context(nc.sbuf_tensor(f"b_{name}", shape, dt))

        def sem(name):
            return ctx.enter_context(nc.semaphore(name))

        def bank(name, shape):
            return ctx.enter_context(nc.psum_tensor(f"b_{name}", shape, F32))

        X = sb["X"]
        stats = local("stats", [P, 3, TT, 6], F32)
        mv = local("mv", [P, 3, TT, 2], F32)
        var = local("var", [P, 3, TT], F32)
        rstd = local("rstd", [P, 3, TT], F32)
        xn = local("xn", [P, 3, TT, D], F32)
        aT_hi = local("aT_hi", [P, DH, S], FP16)
        aT_lo = local("aT_lo", [P, DH, S], FP16)
        zT_hi = local("zT_hi", [P, DH, S], FP16)
        zT_lo = local("zT_lo", [P, DH, S], FP16)
        sc = local("sc", [P, TT, T], F32)
        scm = local("scm", [P, TT, T], F32)
        smax = local("smax", [P, TT], F32)
        nbias = local("nbias", [P, TT], F32)
        expd = local("expd", [P, TT, T], F32)
        rsum = local("rsum", [P, TT], F32)
        rinv = local("rinv", [P, TT], F32)
        rval = local("rval", [P, TT], F32)
        prob = local("prob", [P, TT, T], F32)
        pT_hi = local("pT_hi", [T, S], BF16)
        pT_lo = local("pT_lo", [T, S], BF16)
        gel = local("gel", [P, 2, 2, S], F32)
        gT_hi = local("gT_hi", [P, FK, S], BF16)
        gT_lo = local("gT_lo", [P, FK, S], BF16)
        xb = local("xb", [P, TT, D], F32)

        p_t = [bank(f"p_t{i}", [P, DH, S]) for i in range(2)]
        p_h = [bank(f"p_h{i}", [P, 2, S]) for i in range(2)]
        p_s = bank("p_s", [P, TT, T])
        p_r = bank("p_r", [P, TT, D])
        p_y = bank("p_y", [P, TT, D])

        outer_stat, outer_rstd, outer_done = sem("outer_stat"), sem("outer_rstd"), sem("outer_done")
        ffn_stat, ffn_rstd, ffn_normed = sem("ffn_stat"), sem("ffn_rstd"), sem("ffn_normed")
        turned = [sem(f"turned{n}") for n in range(3)]
        turn_hi = [sem(f"turn_hi{n}") for n in range(3)]
        turn_lo = [sem(f"turn_lo{n}") for n in range(3)]
        scored, max_done, bias_done, exp_done, prob_done = (sem(x) for x in (
            "scored", "max_done", "bias_done", "exp_done", "prob_done"))
        probs_turned, probs_hi, probs_lo, read_out, attn_added = (sem(x) for x in (
            "probs_turned", "probs_hi", "probs_lo", "read_out", "attn_added"))
        up_out, gelu_done, gelu_hi, gelu_lo, down_out, ffn_added, bias_added = (sem(x) for x in (
            "up_out", "gelu_done", "gelu_hi", "gelu_lo", "down_out", "ffn_added", "bias_added"))
        ld_w, mag_set = sem("ld_w"), sem("mag_set")
        attn_link, outer_link, search_link, mag_link = (sem(x) for x in (
            "attn_link", "outer_link", "b_search_link", "mag_link"))
        pool_outer_link, pool_ffn_link = sem("pool_outer_link"), sem("pool_ffn_link")
        pe_gate, dve_gate, pool_gate = sem("b_pe_gate"), sem("b_dve_gate"), sem("b_pool_gate")
        find = Search(nc, sb, sem, "b", 0)

        block = ctx.enter_context(nc.Block())

        STEPS = 8

        def has(b, head=True, attn=True, ffn=True, tail=True):
            return b, head, attn, ffn, tail

        def over_batches(eng, body):
            body(*has(-2, attn=False, ffn=False, tail=False))
            body(*has(-1, ffn=False, tail=False))
            body(*has(0, tail=False))
            with eng.Fori(1, NB - 2) as b:
                body(*has(b))
            body(*has(NB - 2, head=False))
            body(*has(NB - 1, head=False, attn=False))
            body(*has(NB, head=False, attn=False, ffn=False))

        @block.sync
        def _(sp):
            sp.dma_start(sb["W"][:, 0, :].rearrange("p (k n) -> p k n", k=FK),
                         dr["w_fc"].rearrange("(k p) n -> p k n", p=P)).then_inc(ld_w, 16)
            sp.dma_start(sb["W"][:, 1, :].rearrange("p (h n) -> p h n", h=DH),
                         dr["w_proj"].rearrange("(h p) n -> p h n", p=P)).then_inc(ld_w, 16)
            sp.wait_ge(ld_w, 32)

        @block.tensor
        def _(pe):
            def turn(n, k, slot):
                for t in range(TT):
                    for h in range(DH):
                        last = nc.tensor.transpose(p_t[slot][:, h, t * P:(t + 1) * P],
                                                   xn[:, n, t, h * P:(h + 1) * P], sb["ident"][:])
                last.then_inc(turned[n], 1)

            def up(b, j):
                pe.wait_ge(turn_lo[2], b + 1)
                part(pe, gelu_done, 4 * b + j - 1)
                for i in range(2):
                    k = 2 * j + i
                    n = 0
                    for h in range(DH):
                        w = sb["w4"][:, 0, h * F + k * P:h * F + (k + 1) * P]
                        for z in (zT_hi, zT_lo):
                            last = nc.tensor.matmul(p_h[j % 2][:, i, :], w, z[:, h, :], start=n == 0,
                                                    stop=n == 2 * DH - 1)
                            n += 1
                last.then_inc(up_out, 1)

            def down(b, j):
                pe.wait_ge(gelu_lo, 4 * b + j + 1)
                if j == 0:
                    part(pe, ffn_added, b)
                for k in (2 * j, 2 * j + 1):
                    for t in range(TT):
                        for g in (gT_hi, gT_lo):
                            first = k == 0 and t == 0 and g is gT_hi
                            last = nc.tensor.matmul(p_y[:, t, :], g[:, k, t * P:(t + 1) * P],
                                                    sb["w4"][:, 1, k * D:(k + 1) * D], start=first,
                                                    stop=k == FK - 1, skip_group_check=True)
                last.then_inc(down_out, 1)

            def score(a):
                pe.wait_ge(turn_lo[0], a + 1)
                part(pe, max_done, a)
                for t in range(TT):
                    n = 0
                    for h in range(DH):
                        q = [z[:, h, t * P:(t + 1) * P] for z in (aT_hi, aT_lo)]
                        c = [sb[k][:, h, bass.ds(a * T, T)] for k in ("ctxT_hi", "ctxT_lo")]
                        for i, j in ((0, 0), (0, 1), (1, 0)):
                            last = nc.tensor.matmul(p_s[:, t, :], q[i], c[j], start=n == 0,
                                                    stop=n == 3 * DH - 1)
                            n += 1
                last.then_inc(scored, 1)

            def turn_probs(a):
                pe.wait_ge(prob_done, a + 1)
                part(pe, turn_lo[2], a)
                pe.sem_inc(pe_gate, 1)
                for t in range(TT):
                    last = nc.tensor.transpose(p_t[1][0:T, 0, t * P:(t + 1) * P], prob[:, t, :], sb["ident"][:])
                last.then_inc(probs_turned, 1)

            def read(a):
                pe.wait_ge(probs_lo, a + 1)
                part(pe, attn_added, a)
                for t in range(TT):
                    p = [z[:, t * P:(t + 1) * P] for z in (pT_hi, pT_lo)]
                    v = [sb[k][:, bass.ds(a, 1), :].rearrange("k b d -> k (b d)") for k in ("ctx_hi", "ctx_lo")]
                    for n, (i, j) in enumerate(((0, 0), (0, 1), (1, 0))):
                        last = nc.tensor.matmul(p_r[:, t, :], p[i], v[j], start=n == 0, stop=n == 2)
                last.then_inc(read_out, 1)

            def body(b, head, attn, ffn, tail):
                for j in range(STEPS):
                    if j == 0 and attn:
                        score(b + 1)
                    if j == 1 and tail:
                        down(b - 1, 3)
                    if j % 2 and ffn:
                        up(b, j // 2)
                    if j == 3 and attn:
                        turn_probs(b + 1)
                    if j >= 3 and j % 2 and ffn:
                        down(b, j // 2 - 1)
                    if j == 4 and attn:
                        read(b + 1)
                    if j == 5 and head:
                        pe.wait_ge(outer_done, b + 3)
                        if tail:
                            part(pe, turn_lo[1], b - 1)
                        turn(0, b + 2, 0)
                    if j == 6 and tail:
                        pe.wait_ge(outer_done, b + 3)
                        pe.wait_ge(turn_lo[0], b + 3 if head else NB)
                        turn(1, b - 1, 0)
                    if j == 7 and attn:
                        pe.wait_ge(ffn_normed, b + 2)
                        pe.wait_ge(probs_lo, b + 2)
                        turn(2, b + 1, 1)

            over_batches(pe, body)

        @block.scalar
        def _(act):
            def turn(n, k, slot, hi):
                act.wait_ge(turned[n], k + 1)
                nc.scalar.copy(hi, p_t[slot][:]).then_inc(turn_hi[n], 1)

            def gelu(b, j):
                act.wait_ge(up_out, 4 * b + j + 1)
                part(act, gelu_lo, 4 * b + j - 1)
                for i in range(2):
                    k = 2 * j + i
                    last = nc.scalar.activation(gel[:, j % 2, i, :], p_h[j % 2][:, i, :], ACT.Gelu_apprx_tanh,
                                                bias=sb["up_b"][:, k:k + 1])
                last.then_inc(gelu_done, 1)

            def gelu_part(b, j):
                act.wait_ge(gelu_done, 4 * b + j + 1)
                part(act, down_out, 4 * (b - 1) + j + 1)
                nc.scalar.copy(gT_hi[:, 2 * j:2 * j + 2, :], gel[:, j % 2]).then_inc(gelu_hi, 1)

            def exps(a):
                act.wait_ge(bias_done, a + 1)
                for t in range(TT):
                    last = nc.scalar.activation(expd[:, t, :], scm[:, t, :], ACT.Exp, bias=nbias[:, t:t + 1],
                                                scale=D ** -0.5, accum_out=rsum[:, t:t + 1])
                last.then_inc(exp_done, 1)

            def body(b, head, attn, ffn, tail):
                for j in range(STEPS):
                    if j == 1 and attn:
                        exps(b + 1)
                    if j % 2 and ffn:
                        gelu(b, j // 2)
                    if ffn:
                        find.tick(act, b, j)
                        if j >= 1:
                            find.square(act, b, j - 1)
                    if j % 2 and ffn:
                        gelu_part(b, j // 2)
                    if j == 4 and attn:
                        act.wait_ge(probs_turned, b + 2)
                        nc.scalar.copy(pT_hi[:], p_t[1][0:T, 0, :]).then_inc(probs_hi, 1)
                    if j == 5 and head:
                        turn(0, b + 2, 0, aT_hi[:])
                    if j == 6 and tail:
                        turn(1, b - 1, 0, sb["xT_hi"][:, bass.ds(b - 1, 1)].rearrange("p b h s -> p (b h) s"))
                    if j == 7 and attn:
                        turn(2, b + 1, 1, zT_hi[:])
                if ffn:
                    find.square(act, b, STEPS - 1)

            over_batches(act, body)

        @block.gpsimd
        def _(pool):
            def rsqrt(n, m, link, done):
                pool.sem_inc(pool_gate, 1)
                here = slice(n, n + m)
                link(nc.gpsimd.tensor_scalar(var[:, here], mv[:, here, :, 1], 1.0, LN_EPS, ALU.mult, ALU.add))
                half = sb["neghalf"][:, 0:m * TT].rearrange("p (m t) -> p m t", t=TT)
                nc.gpsimd.tensor_tensor(rstd[:, here], var[:, here], half, ALU.pow).then_inc(done, 1)

            def body(b, head, attn, ffn, tail):
                if ffn:
                    if isinstance(b, int) and b == 0:
                        pool.wait_ge(mag_set, 1)
                    find.load(pool, b)
                for j in range(STEPS):
                    if j == 1 and attn:
                        pool.wait_ge(max_done, b + 2)
                        pool.sem_inc(pool_gate, 1)
                        nc.gpsimd.tensor_scalar(nbias[:], smax[:], -D ** -0.5, 1.0, ALU.mult, ALU.mult
                                                ).then_inc(bias_done, 1)
                    if j == 4:
                        pool.wait_ge(outer_stat, b + 3)
                        n, m = (0, 2) if head and tail else (0, 1) if head else (1, 1)
                        if head or tail:
                            rsqrt(n, m, Link(pool, pool_outer_link, b + 2), outer_rstd)
                    if j == 6 and attn:
                        pool.wait_ge(ffn_stat, b + 2)
                        rsqrt(2, 1, Link(pool, pool_ffn_link, b + 1), ffn_rstd)
                    if ffn:
                        find.distance(pool, b, j)
                    if j == 3 and ffn:
                        part(pool, ffn_added, b)
                        pool.wait_ge(ffn_normed, b + 1)
                        nc.gpsimd.tensor_tensor(xb[:], X[:, bass.ds(b * TT, TT), :],
                                                sb["down_b"][:].unsqueeze(1).to_broadcast([P, TT, D]), ALU.add
                                                ).then_inc(bias_added, 1)

            over_batches(pool, body)

        @block.vector
        def _(dve):
            def magnitudes():
                link = Link(dve, mag_link)
                blocks = sb["mag"][:].rearrange("p (a b) -> p a b", b=QBLK)
                dve.wait_ge(ld_w, 32)
                link(nc.vector.tensor_scalar(sb["mag"][:].bitcast(U32),
                                             sb["W"][:].rearrange("p m n -> p (m n)").bitcast(U32),
                                             0x7FFFFFFF, None, ALU.bitwise_and))
                link(nc.vector.tensor_reduce(sb["err"][:], blocks, AX, ALU.max))
                link(nc.vector.tensor_scalar(sb["base"][:], sb["err"][:], 1e-8, 1.0 / QMAX, ALU.max, ALU.mult))
                link(nc.vector.reciprocal(sb["upd"][:], sb["base"][:]))
                nc.vector.memset(sb["best_err"][:], 3e38)
                link(nc.vector.memset(sb["best"][:], 1.0))
                nc.vector.tensor_tensor(blocks, blocks, sb["upd"][:].unsqueeze(2).to_broadcast([P, NBLK, QBLK]),
                                        ALU.mult).then_inc(mag_set, 1)
                dve.wait_ge(mag_set, 1)

            def stat(batches, link, done):
                at = [(n, t, b) for n, b in batches.items() for t in range(TT)]
                dve.sem_inc(dve_gate, 1)
                for n, t, b in at:
                    last = nc.vector.bn_stats(stats[:, n, t, :],
                                              X[:, bass.ds(b * TT + t, 1), :].rearrange("p a d -> p (a d)"))
                link(last)
                dve.sem_inc(dve_gate, 1)
                for n, t, b in at:
                    last = nc.vector.bn_aggr(mv[:, n, t, :], stats[:, n, t, :])
                last.then_inc(done, 1)

            def normed(batches, done):
                for n, b in batches.items():
                    for t in range(TT):
                        last = nc.vector.tensor_scalar(xn[:, n, t, :],
                                                       X[:, bass.ds(b * TT + t, 1), :].rearrange("p a d -> p (a d)"),
                                                       mv[:, n, t, 0:1], rstd[:, n, t:t + 1],
                                                       ALU.subtract, ALU.mult)
                last.then_inc(done, 1)

            def turn(n, k, slot, lo, hi):
                dve.wait_ge(turn_hi[n], k + 1)
                nc.vector.tensor_tensor(lo, p_t[slot][:], hi, ALU.subtract).then_inc(turn_lo[n], 1)

            def gelu_rest(b, j):
                dve.wait_ge(gelu_hi, 4 * b + j + 1)
                nc.vector.tensor_tensor(gT_lo[:, 2 * j:2 * j + 2, :], gel[:, j % 2], gT_hi[:, 2 * j:2 * j + 2, :],
                                        ALU.subtract).then_inc(gelu_lo, 1)

            def body(b, head, attn, ffn, tail):
                a = b + 1
                wide = [P, TT, T]
                link = Link(dve, attn_link, 4 * a + a)
                choose = Link(dve, search_link, find.LINKS * b)
                outer = {}
                if head:
                    outer[0] = b + 2
                if tail:
                    outer[1] = b - 1
                for j in range(STEPS):
                    if j == 0 and attn:
                        dve.wait_ge(scored, a + 1)
                        link(nc.vector.tensor_tensor(sc[:], p_s[:],
                                                     sb["keep"][:, bass.ds(a, 1), :].to_broadcast(wide), ALU.mult))
                        link(nc.vector.tensor_tensor(scm[:], sc[:],
                                                     sb["drop"][:, bass.ds(a, 1), :].to_broadcast(wide), ALU.add))
                        nc.vector.tensor_reduce(smax[:], scm[:], AX, ALU.max).then_inc(max_done, 1)
                    if j == 2 and attn:
                        dve.wait_ge(exp_done, a + 1)
                        link(nc.vector.reciprocal(rinv[:], rsum[:]))
                        link(nc.vector.tensor_tensor(rval[:], rinv[:],
                                                     sb["valid"][:, bass.ds(a, 1)].to_broadcast([P, TT]), ALU.mult))
                        nc.vector.tensor_tensor(prob[:], expd[:], rval[:].unsqueeze(2).to_broadcast(wide), ALU.mult
                                                ).then_inc(prob_done, 1)
                    if j == 4 and attn:
                        dve.wait_ge(probs_hi, a + 1)
                        nc.vector.tensor_tensor(pT_lo[:], p_t[1][0:T, 0, :], pT_hi[:], ALU.subtract
                                                ).then_inc(probs_lo, 1)
                    if j == 4 and outer:
                        dve.wait_ge(outer_rstd, b + 3)
                        part(dve, turned[0], (b + 2) if head else NB)
                        if tail:
                            part(dve, turned[1], b - 1)
                        normed(outer, outer_done)
                    if j == 6 and attn:
                        dve.wait_ge(ffn_rstd, a + 1)
                        part(dve, turned[2], a)
                        normed({2: a}, ffn_normed)
                    if ffn:
                        find.near(dve, b, j)
                    if j == 0 and tail:
                        gelu_rest(b - 1, 3)
                    if j >= 2 and j % 2 == 0 and ffn:
                        gelu_rest(b, j // 2 - 1)
                    if j == 2 and tail:
                        dve.wait_ge(down_out, 4 * b)
                        dve.wait_ge(bias_added, b)
                        nc.vector.tensor_tensor(X[:, bass.ds((b - 1) * TT, TT), :], p_y[:], xb[:], ALU.add
                                                ).then_inc(ffn_added, 1)
                    if ffn and j >= 1:
                        find.total(dve, b, j - 1, choose)
                    if j == 3 and outer:
                        if tail:
                            dve.wait_ge(ffn_added, b)
                        stat(outer, Link(dve, outer_link, b + 2), outer_stat)
                    if j == 5 and attn:
                        dve.wait_ge(read_out, a + 1)
                        here = X[:, bass.ds(a * TT, TT), :]
                        nc.vector.tensor_tensor(here, p_r[:], here, ALU.add).then_inc(attn_added, 1)
                        dve.wait_ge(attn_added, a + 1)
                        stat({2: a}, link, ffn_stat)
                    if j == 6 and head:
                        turn(0, b + 2, 0, aT_lo[:], aT_hi[:])
                    if j == 7 and tail:
                        xt = [sb[k][:, bass.ds(b - 1, 1)].rearrange("p b h s -> p (b h) s")
                              for k in ("xT_lo", "xT_hi")]
                        turn(1, b - 1, 0, *xt)
                    if j == 7 and attn:
                        turn(2, b + 1, 1, zT_lo[:], zT_hi[:])
                if ffn:
                    find.total(dve, b, STEPS - 1, choose)
                if isinstance(b, int) and b == -1:
                    magnitudes()

            over_batches(dve, body)


def block_c(nc, sb):
    with ExitStack() as ctx:
        def local(name, shape, dt):
            return ctx.enter_context(nc.sbuf_tensor(f"c_{name}", shape, dt))

        def sem(name):
            return ctx.enter_context(nc.semaphore(name))

        def bank(name, shape):
            return ctx.enter_context(nc.psum_tensor(f"c_{name}", shape, F32))

        X = sb["X"]
        ROW = [T + P * (t + 1) for t in range(TT)]
        OFF = [0, ROW[0]]
        qT_hi = local("qT_hi", [P, NH, S], BF16)
        qT_lo = local("qT_lo", [P, NH, S], BF16)
        kT_hi = local("kT_hi", [P, NG, S], BF16)
        kT_lo = local("kT_lo", [P, NG, S], BF16)
        v_hi = local("v_hi", [P, TT, NG, HD], BF16)
        v_lo = local("v_lo", [P, TT, NG, HD], BF16)
        rc = local("rc", [P, REP + 1, HD], F32)
        rs = local("rs", [P, REP + 1, HD], F32)
        rot = local("rot", [P, 2, REP + 1, HD], F32)
        junk = local("junk", [P, REP, HD], BF16)
        ssq = local("ssq", [P, REP + 1], F32)
        mean = local("mean", [P, REP + 1], F32)
        rms = local("rms", [P, REP + 1], F32)
        qrms = local("qrms", [P, NH, TT], F32)
        smax = local("smax", [P, 2, TT], F32)
        nbias = local("nbias", [P, 2, 2, TT], F32)
        rsum = local("rsum", [P, 2, 2, TT], F32)
        rinv = local("rinv", [P, 2, 2, TT], F32)
        prob = local("prob", [P, 2, 2, sum(ROW)], F32)
        pT_hi = local("pT_hi", [P, 2, 3, 2 * S], BF16)
        pT_lo = local("pT_lo", [P, 2, 3, 2 * S], BF16)
        oT_hi = local("oT_hi", [P, 2, 2 * S], BF16)
        oT_lo = local("oT_lo", [P, 2, 2 * S], BF16)

        p_p = bank("p_p", [P, REP, HD])
        p_x = bank("p_x", [P, REP, P])
        p_s = [bank(f"p_s{i}", [P, 512]) for i in range(2)]
        p_t = [bank(f"p_t{i}", [P, 2 * S]) for i in range(2)]
        p_o = bank("p_o", [P, 2, S])
        p_y = bank("p_y", [P, TT, D])

        proj_out, proj_act, proj_dve, rot_done = (sem(x) for x in ("proj_out", "proj_act", "proj_dve", "rot_done"))
        x_out, x_hi, x_lo, q_scaled = (sem(x) for x in ("x_out", "x_hi", "x_lo", "q_scaled"))
        scored, bias_done, exp_done, inv_done, prob_done = (sem(x) for x in (
            "c_scored", "c_bias_done", "c_exp_done", "inv_done", "c_prob_done"))
        t_out, t_hi, t_lo, o_out, o_hi, o_lo = (sem(x) for x in ("t_out", "t_hi", "t_lo", "o_out", "o_hi", "o_lo"))
        wo_done, y_added = sem("wo_done"), sem("y_added")
        max_done, search_link, pool_link = sem("c_max_done"), sem("c_search_link"), sem("c_pool_link")
        pe_gate, pool_gate = sem("c_pe_gate"), sem("c_pool_gate")
        find = Search(nc, sb, sem, "c", NB)

        block = ctx.enter_context(nc.Block())

        LAG = 3

        def over_batches(eng, body):
            body(-1, False, True)
            body(0, True, True)
            with eng.Fori(1, NB - 1) as b:
                body(b, True, True)
            body(NB - 1, True, False)

        def made(b, j, attn, nxt):
            if j < 0:
                return (1, b) if attn else None
            if j < 4:
                return (2 + j // 2, b) if attn else None
            return ((j - 4) // 2, b + 1) if nxt and j < NP else None

        def steps(b, attn, nxt):
            for j in range(NP if nxt else NP + LAG):
                def pair(lag):
                    k = j - lag
                    if not attn or k >= NP or (k < 0 and isinstance(b, int) and b == 0):
                        return None
                    return (b, k) if k >= 0 else (b - 1, k + NP)

                ahead = (b, j + 1) if attn and j < NP - 1 else (b + 1, 0) if nxt and j == NP - 1 else None
                yield j, made(b, j, attn, nxt), made(b, j - 1, attn, nxt), pair, ahead

        @block.tensor
        def _(pe):
            def project(g, B, t, kv):
                n = 2 * (2 * (NG * B + g) + t) + kv
                part(pe, proj_act, n)
                part(pe, proj_dve, n)
                rows = [sb[k][:, bass.ds(B, 1)].rearrange("p b h s -> p (b h) s") for k in ("xT_hi", "xT_lo")]
                wide = 2 * HD if kv else REP * HD
                w = [sb[k][:, :, g * wide:(g + 1) * wide] for k in (("wkv_hi", "wkv_lo") if kv else ("wq_hi", "wq_lo"))]
                out = p_p[:].rearrange("p a d -> p (a d)")[:, 0:wide]
                i = 0
                for h in range(DH):
                    for a, c in ((0, 0), (0, 1), (1, 0)):
                        last = nc.tensor.matmul(out, rows[a][:, h, t * P:(t + 1) * P], w[c][:, h, :],
                                                start=i == 0, stop=i == 3 * DH - 1)
                        i += 1
                last.then_inc(proj_out, 1)

            def turn(g, B, t, kv):
                n = 2 * (2 * (NG * B + g) + t) + kv
                pe.wait_ge(rot_done, n + 1)
                part(pe, x_lo, n)
                for r in ([REP] if kv else range(REP)):
                    last = nc.tensor.transpose(p_x[:, r % REP, :], rot[:, t, r, :], sb["ident"][:])
                last.then_inc(x_out, 1)

            def score(b, j, i):
                g = j * 2 // REP
                h = 2 * j + i
                pe.wait_ge(x_lo, 4 * (NG * b + g) + 4)
                part(pe, exp_done, 2 * (NP * b + j - 1) + i + 1)
                for t in range(TT):
                    out = p_s[i][:, OFF[t]:OFF[t] + ROW[t]]
                    q = [z[:, h, t * P:(t + 1) * P] for z in (qT_hi, qT_lo)]
                    k = [z[:, g, 0:ROW[t] - T] for z in (kT_hi, kT_lo)]
                    kc = [sb[z][:, g, bass.ds(b * T, T)] for z in ("kcT_hi", "kcT_lo")]
                    for n, (x, y) in enumerate(((0, 0), (0, 1), (1, 0))):
                        nc.tensor.matmul(out[:, 0:T], q[x], kc[y], start=n == 0, stop=n == 2,
                                         skip_group_check=True)
                        last = nc.tensor.matmul(out[:, T:ROW[t]], q[x], k[y], start=False, stop=n == 2,
                                                skip_group_check=True)
                        if n == 0:
                            nc.tensor.matmul(out[:, ROW[t] - P:ROW[t]], sb["ident16"][:], sb["causal"][:],
                                             start=False, stop=False, skip_group_check=True)
                last.then_inc(scored, 1)

            def turn_probs(b, j, u):
                n = 3 * (NP * b + j) + u
                pe.wait_ge(prob_done, 2 * (NP * b + j) + 2)
                part(pe, t_lo, n - 1)
                if u == 0:
                    pe.sem_inc(pe_gate, 1)
                out = p_t[(j + u) % 2]
                for i in range(2):
                    for t in range(TT):
                        if u == 2 and t == 0:
                            continue
                        lo, wide = (0, T) if u == 0 else (T + (u - 1) * P, P)
                        col = i * P if u == 2 else i * S + t * P
                        last = nc.tensor.transpose(out[0:wide, col:col + P],
                                                   prob[:, j % 2, i, OFF[t] + lo:OFF[t] + lo + wide],
                                                   sb["ident"][:])
                last.then_inc(t_out, 1)

            def values(b, j):
                g = j * 2 // REP
                pe.wait_ge(t_lo, 3 * (NP * b + j) + 3)
                part(pe, o_lo, NP * b + j)
                out = p_o[:].rearrange("p i s -> p (i s)")
                own = [[z[:, u, g, :] for z in (v_hi, v_lo)] for u in range(TT)]
                con = [sb[z][:, bass.ds(b, 1), g, :].rearrange("k b d -> k (b d)") for z in ("vc_hi", "vc_lo")]
                for u, (rows, wide, v) in enumerate(((P, 2 * S, own[0]), (T, 2 * S, con), (P, S, own[1]))):
                    at = (1, 0, 2)[u]
                    p = [z[0:rows, j % 2, at, 0:wide] for z in (pT_hi, pT_lo)]
                    dst = out if u < 2 else p_o[:, :, P:S]
                    for n, (x, y) in enumerate(((0, 0), (0, 1), (1, 0))):
                        rhs = p[y] if u < 2 else p[y].rearrange("p (i s) -> p i s", i=2)
                        last = nc.tensor.matmul(dst, v[x], rhs, start=u == 0 and n == 0,
                                                stop=u == 2 and n == 2, skip_group_check=True)
                last.then_inc(o_out, 1)

            def finish(b, j):
                pe.wait_ge(o_lo, NP * b + j + 1)
                if j == 0:
                    part(pe, y_added, b)
                for i in range(2):
                    h = 2 * j + i
                    for t in range(TT):
                        at = slice(i * S + t * P, i * S + (t + 1) * P)
                        o = [z[:, j % 2, at] for z in (oT_hi, oT_lo)]
                        w = [sb[k][:, h, :] for k in ("wo_hi", "wo_lo")]
                        for n, (x, y) in enumerate(((0, 0), (0, 1), (1, 0))):
                            last = nc.tensor.matmul(p_y[:, t, :], o[x], w[y],
                                                    start=j == 0 and i == 0 and t == 0 and n == 0,
                                                    stop=h == NH - 1 and n == 2, skip_group_check=True)
                last.then_inc(wo_done, 1)

            def body(b, attn, nxt):
                for j, now, before, pair, ahead in steps(b, attn, nxt):
                    t = j % 2
                    if pair(1):
                        turn_probs(*pair(1), 0)
                    if now:
                        project(*now, t, 0)
                    if pair(1):
                        turn_probs(*pair(1), 1)
                    if before:
                        turn(*before, 1 - t, 0)
                    if ahead:
                        score(*ahead, 0)
                    if pair(3):
                        finish(*pair(3))
                    if now:
                        project(*now, t, 1)
                    if pair(1):
                        turn_probs(*pair(1), 2)
                    if before:
                        turn(*before, 1 - t, 1)
                    if ahead:
                        score(*ahead, 1)
                    if pair(2):
                        values(*pair(2))

            over_batches(pe, body)

        @block.scalar
        def _(act):
            def squares(g, B, t, kv):
                n = 2 * (NG * B + g) + t
                act.wait_ge(proj_out, 2 * n + kv + 1)
                part(act, q_scaled, n)
                for r in range(1 if kv else REP):
                    at = REP if kv else r
                    last = nc.scalar.activation(junk[:, r], p_p[:, r, :], ACT.Square, accum_out=ssq[:, at:at + 1])
                if kv:
                    part(act, o_out, NP * (B - 1) + 2 * g + 2)
                    last = nc.scalar.copy(v_hi[:, t, g, :], p_p[:, 1, :])
                last.then_inc(proj_act, 1)

            def turn(g, B, t, kv):
                act.wait_ge(x_out, 2 * (2 * (NG * B + g) + t) + kv + 1)
                part(act, scored, 2 * (NP * (B - 1) + 2 * g + 2))
                if kv:
                    ins = nc.scalar.copy(kT_hi[:, g, t * P:(t + 1) * P], p_x[:, 0, :])
                else:
                    ins = nc.scalar.copy(qT_hi[:, REP * g:REP * (g + 1), t * P:(t + 1) * P], p_x[:])
                ins.then_inc(x_hi, 1)

            def exps(b, j, i):
                n = NP * b + j
                act.wait_ge(bias_done, 2 * n + i + 1)
                part(act, t_out, 3 * (n - 1))
                for t in range(TT):
                    last = nc.scalar.activation(prob[:, j % 2, i, OFF[t]:OFF[t] + ROW[t]],
                                                p_s[i][:, OFF[t]:OFF[t] + ROW[t]], ACT.Exp,
                                                bias=nbias[:, j % 2, i, t:t + 1],
                                                scale=qrms[:, 2 * j + i, t:t + 1],
                                                accum_out=rsum[:, j % 2, i, t:t + 1])
                last.then_inc(exp_done, 1)

            def turn_probs(b, j, u):
                act.wait_ge(t_out, 3 * (NP * b + j) + u + 1)
                part(act, o_out, NP * b + j - 1)
                rows, wide = (T if u == 0 else P), (S if u == 2 else 2 * S)
                nc.scalar.copy(pT_hi[0:rows, j % 2, u, 0:wide], p_t[(j + u) % 2][0:rows, 0:wide]).then_inc(t_hi, 1)

            def values(b, j):
                act.wait_ge(o_out, NP * b + j + 1)
                part(act, wo_done, NP * b + j - 1)
                nc.scalar.copy(oT_hi[:, j % 2], p_o[:].rearrange("p i s -> p (i s)")).then_inc(o_hi, 1)

            def body(b, attn, nxt):
                for j, now, before, pair, ahead in steps(b, attn, nxt):
                    t = j % 2
                    if pair(0):
                        exps(*pair(0), 0)
                    if pair(1):
                        turn_probs(*pair(1), 0)
                    if pair(0):
                        exps(*pair(0), 1)
                    if pair(3):
                        values(*pair(3))
                    if now:
                        squares(*now, t, 0)
                    if pair(1):
                        turn_probs(*pair(1), 1)
                    if pair(0):
                        find.tick(act, b, j)
                    if before:
                        turn(*before, 1 - t, 0)
                    if pair(0) and j:
                        find.square(act, b, j - 1)
                    if now:
                        squares(*now, t, 1)
                    if pair(1):
                        turn_probs(*pair(1), 2)
                    if before:
                        turn(*before, 1 - t, 1)
                    if pair(0) and j == NP - 1:
                        find.square(act, b, j)

            over_batches(act, body)

        @block.gpsimd
        def _(pool):
            def rotate(g, B, t, kv):
                n = 2 * (NG * B + g) + t
                pool.wait_ge(proj_dve, 2 * n + kv + 1)
                part(pool, x_out, 2 * (n - 2) + kv + 1)
                if not kv:
                    nc.gpsimd.tensor_tensor(rot[:, t, 0:REP], rc[:, 0:REP], rs[:, 0:REP], ALU.add
                                            ).then_inc(rot_done, 1)
                    return
                link = Link(pool, pool_link, 3 * n)
                part(pool, exp_done, 2 * (NP * (B - 1) + 2 * g + 2))
                pool.sem_inc(pool_gate, 1)
                link(nc.gpsimd.tensor_scalar(mean[:], ssq[:], 1.0 / HD, RMS_EPS, ALU.mult, ALU.add))
                link(nc.gpsimd.tensor_tensor(rms[:], mean[:], sb["neghalf"][:, 0:REP + 1], ALU.pow))
                pool.sem_inc(pool_gate, 1)
                nc.gpsimd.tensor_scalar(qrms[:, REP * g:REP * (g + 1), t], rms[:, 0:REP], HD ** -0.5, 1.0,
                                        ALU.mult, ALU.mult).then_inc(q_scaled, 1)
                link(nc.gpsimd.tensor_tensor(rot[:, t, REP], rc[:, REP], rs[:, REP], ALU.add))
                pool.sem_inc(pool_gate, 1)
                nc.gpsimd.tensor_scalar(rot[:, t, REP], rot[:, t, REP], rms[:, REP:REP + 1], 1.0,
                                        ALU.mult, ALU.mult).then_inc(rot_done, 1)

            def normalise(b, j, i):
                pool.wait_ge(inv_done, 2 * (NP * b + j) + i + 1)
                pool.sem_inc(pool_gate, 1)
                for t in range(TT):
                    p = prob[:, j % 2, i, OFF[t]:OFF[t] + ROW[t]]
                    last = nc.gpsimd.tensor_scalar(p, p, rinv[:, j % 2, i, t:t + 1], 1.0, ALU.mult, ALU.mult)
                last.then_inc(prob_done, 1)

            def body(b, attn, nxt):
                if attn:
                    find.load(pool, b)
                for j, now, before, pair, ahead in steps(b, attn, nxt):
                    t = j % 2
                    if pair(0):
                        normalise(*pair(0), 0)
                        normalise(*pair(0), 1)
                    if now:
                        rotate(*now, t, 0)
                    if pair(0):
                        find.distance(pool, b, j)
                    if now:
                        rotate(*now, t, 1)

            over_batches(pool, body)

        @block.vector
        def _(dve):
            def rope(g, B, t, kv):
                n = 2 * (NG * B + g) + t
                dve.wait_ge(proj_act, 2 * n + kv + 1)
                part(dve, rot_done, 2 * (n - 1) + kv + 1)
                heads, at = (1, slice(REP, REP + 1)) if kv else (REP, slice(0, REP))
                cosw = sb["cosw"][:, kv, t].unsqueeze(1).to_broadcast([P, heads, HD])
                nc.vector.tensor_tensor(rc[:, at], p_p[:, 0:heads], cosw, ALU.mult)
                src = p_p[:, 0:heads].rearrange("p r (h d) -> p r h d", h=2)[:, :, ::-1, :]
                sinw = sb["sinw"][:, kv, t].rearrange("p (a h d) -> p a h d", a=1, h=2
                                                      ).to_broadcast([P, heads, 2, HD // 2])
                last = nc.vector.tensor_tensor(rs[:, at].rearrange("p r (h d) -> p r h d", h=2), src, sinw, ALU.mult)
                if kv:
                    last = nc.vector.tensor_tensor(v_lo[:, t, g, :], p_p[:, 1, :], v_hi[:, t, g, :], ALU.subtract)
                last.then_inc(proj_dve, 1)

            def turn(g, B, t, kv):
                dve.wait_ge(x_hi, 2 * (2 * (NG * B + g) + t) + kv + 1)
                at = slice(t * P, (t + 1) * P)
                if kv:
                    ins = nc.vector.tensor_tensor(kT_lo[:, g, at], p_x[:, 0, :], kT_hi[:, g, at], ALU.subtract)
                else:
                    heads = slice(REP * g, REP * (g + 1))
                    ins = nc.vector.tensor_tensor(qT_lo[:, heads, at], p_x[:], qT_hi[:, heads, at], ALU.subtract)
                ins.then_inc(x_lo, 1)

            def maxima(b, j, i):
                dve.wait_ge(scored, 2 * (NP * b + j) + i + 1)
                for t in range(TT):
                    last = nc.vector.tensor_reduce(smax[:, i, t:t + 1], p_s[i][:, OFF[t]:OFF[t] + ROW[t]],
                                                   AX, ALU.max)
                last.then_inc(max_done, 1)

            def biases(b, j, i):
                n = 2 * (NP * b + j) + i
                dve.wait_ge(max_done, n + 1)
                dve.wait_ge(q_scaled, 2 * (NG * b + 2 * j // REP) + 2)
                nc.vector.scalar_tensor_tensor(nbias[:, j % 2, i], smax[:, i], -1.0, qrms[:, 2 * j + i],
                                               ALU.mult, ALU.mult).then_inc(bias_done, 1)

            def inverses(b, j, i):
                n = 2 * (NP * b + j) + i
                dve.wait_ge(exp_done, n + 1)
                nc.vector.reciprocal(rinv[:, j % 2, i], rsum[:, j % 2, i]).then_inc(inv_done, 1)

            def turn_probs(b, j, u):
                dve.wait_ge(t_hi, 3 * (NP * b + j) + u + 1)
                rows, wide = (T if u == 0 else P), (S if u == 2 else 2 * S)
                nc.vector.tensor_tensor(pT_lo[0:rows, j % 2, u, 0:wide], p_t[(j + u) % 2][0:rows, 0:wide],
                                        pT_hi[0:rows, j % 2, u, 0:wide], ALU.subtract).then_inc(t_lo, 1)

            def add(b):
                dve.wait_ge(wo_done, NP * (b + 1))
                here = X[:, bass.ds(b * TT, TT), :]
                nc.vector.tensor_tensor(here, p_y[:], here, ALU.add).then_inc(y_added, 1)

            def values(b, j):
                dve.wait_ge(o_hi, NP * b + j + 1)
                nc.vector.tensor_tensor(oT_lo[:, j % 2], p_o[:].rearrange("p i s -> p (i s)"), oT_hi[:, j % 2],
                                        ALU.subtract).then_inc(o_lo, 1)

            def body(b, attn, nxt):
                link = Link(dve, search_link, find.LINKS * b)
                for j, now, before, pair, ahead in steps(b, attn, nxt):
                    t = j % 2
                    if pair(1):
                        turn_probs(*pair(1), 0)
                    if pair(0):
                        inverses(*pair(0), 0)
                        inverses(*pair(0), 1)
                    if pair(3):
                        values(*pair(3))
                    if now:
                        rope(*now, t, 0)
                    if pair(1):
                        turn_probs(*pair(1), 1)
                    if pair(0):
                        find.near(dve, b, j)
                    if before:
                        turn(*before, 1 - t, 0)
                    if ahead:
                        maxima(*ahead, 0)
                    if pair(0) and j:
                        find.total(dve, b, j - 1, link)
                    if ahead:
                        biases(*ahead, 0)
                    if now:
                        rope(*now, t, 1)
                    if pair(1):
                        turn_probs(*pair(1), 2)
                    if before:
                        turn(*before, 1 - t, 1)
                    if ahead:
                        maxima(*ahead, 1)
                        biases(*ahead, 1)
                    if j % NP == 2 and pair(3):
                        add(pair(3)[0])
                    if pair(0) and j == NP - 1:
                        find.total(dve, b, j, link)

            over_batches(dve, body)


def block_d(nc, sb, out):
    with ExitStack() as ctx:
        def local(name, shape, dt):
            return ctx.enter_context(nc.sbuf_tensor(f"d_{name}", shape, dt))

        def sem(name):
            return ctx.enter_context(nc.semaphore(name))

        def bank(name, shape):
            return ctx.enter_context(nc.psum_tensor(f"d_{name}", shape, F32))

        X = sb["X"]
        GT = 4
        NGR = NB * TT // GT
        GS = GT * P
        CH, CB = 512, 512 // QBLK
        NCH = 2 * 2048 // CH
        Wf = sb["W"][:].rearrange("p m n -> p (m n)")
        fc_hi = local("fc_hi", [P, DH, F], BF16)
        fc_lo = local("fc_lo", [P, DH, F], BF16)
        pj_hi = local("pj_hi", [P, FK, D], BF16)
        pj_lo = local("pj_lo", [P, FK, D], BF16)
        step = local("step", [P, NBLK], F32)
        step_inv = local("step_inv", [P, NBLK], F32)
        unit = local("unit", [P, 2, CH], F32)
        tick = local("tick", [P, 2, CH], F32)
        near = local("near", [P, 2, CH], F32)
        deq = local("deq", [P, 2, CH], F32)
        moved = local("moved", [P, 2, CH], F32)
        wq = local("wq", [P, 2, CH], F32)
        stats = local("stats", [P, GT, 6], F32)
        mv = local("mv", [P, GT, 2], F32)
        var = local("var", [P, GT], F32)
        rstd = local("rstd", [P, GT], F32)
        xn = local("xn", [P, GT, D], F32)
        zT_hi = local("zT_hi", [P, 2, DH, GS], FP16)
        zT_lo = local("zT_lo", [P, 2, DH, GS], FP16)
        sq = local("sq", [P, 2, GS], F32)
        rect = local("rect", [P, 2, GS], F32)
        gT_hi = local("gT_hi", [P, 2, GS], BF16)
        gT_lo = local("gT_lo", [P, 2, GS], BF16)

        p_t = [bank(f"p_t{h}", [P, GS]) for h in range(DH)]
        p_h = [bank(f"p_h{i}", [P, GS]) for i in range(2)]
        p_y = [bank(f"p_y{i}", [P, 2, D]) for i in range(2)]

        deq_done, wq_done, w_out, w_hi, w_lo = (sem(x) for x in ("deq_done", "wq_done", "w_out", "w_hi", "w_lo"))
        norm_stat, norm_rstd, norm_done, turned, z_hi, z_lo = (sem(x) for x in (
            "d_norm_stat", "d_norm_rstd", "d_norm_done", "d_turned", "z_hi", "z_lo"))
        up_out, rect_done, sq_done, g_hi, g_lo, down_out, y_added, stored = (sem(x) for x in (
            "d_up_out", "rect_done", "sq_done", "g_hi", "g_lo", "d_down_out", "d_y_added", "stored"))
        dve_link, pool_link = sem("d_dve_link"), sem("d_pool_link")

        block = ctx.enter_context(nc.Block())

        def over_groups(body):
            body(-1, 1, False, True)
            for i in range(NGR):
                body(i, i % 2, True, i + 1 < NGR)
            body(NGR, NGR % 2, False, False)

        def weight_view(c, w):
            if c < NCH // 2:
                return [w[:, i * D + h * P:i * D + (h + 1) * P] for h in range(DH) for i in range(2)]
            return [w[:, i * P:(i + 1) * P] for i in range(4)]

        def weight_place(c, fc, pj):
            if c < NCH // 2:
                return fc[:, :, 2 * c * P:(2 * c + 2) * P], [DH, 2 * P]
            c -= NCH // 2
            h, k = c // 2, 4 * (c % 2)
            return pj[:, k:k + 4, h * P:(h + 1) * P], [4, P]

        @block.tensor
        def _(pe):
            def weights(c):
                pe.wait_ge(wq_done, c + 1)
                part(pe, w_lo, c - 1)
                for n, tile in enumerate(weight_view(c, wq[:, c % 2])):
                    last = nc.tensor.transpose(p_h[c % 2][:, n * P:(n + 1) * P], tile, sb["ident"][:])
                last.then_inc(w_out, 1)

            def up(i, k, slot):
                n = FK * i + k
                part(pe, sq_done, n - 1)
                for m, (h, a, c) in enumerate([(h, a, c) for h in range(DH) for a, c in ((0, 0), (0, 1), (1, 0))]):
                    w = (fc_hi, fc_lo)[a][:, h, k * P:(k + 1) * P]
                    z = (zT_hi, zT_lo)[c][:, slot, h, :]
                    last = nc.tensor.matmul(p_h[k % 2][:], w, z, start=m == 0, stop=m == 3 * DH - 1)
                last.then_inc(up_out, 1)

            def down(i, k):
                pe.wait_ge(g_lo, FK * i + k + 1)
                if k == 0:
                    part(pe, y_added, i)
                for t in range(GT):
                    for m, (a, c) in enumerate(((0, 0), (0, 1), (1, 0))):
                        g = (gT_hi, gT_lo)[a][:, k % 2, t * P:(t + 1) * P]
                        last = nc.tensor.matmul(p_y[t // 2][:, t % 2, :], g, (pj_hi, pj_lo)[c][:, k, :],
                                                start=k == 0 and t % 2 == 0 and m == 0,
                                                stop=k == FK - 1 and m == 2, skip_group_check=True)
                last.then_inc(down_out, 1)

            def turn(i):
                pe.wait_ge(norm_done, i + 1)
                part(pe, z_lo, DH * i)
                for h in range(DH):
                    for t in range(GT):
                        last = nc.tensor.transpose(p_t[h][:, t * P:(t + 1) * P], xn[:, t, h * P:(h + 1) * P],
                                                   sb["ident"][:])
                    last.then_inc(turned, 1)

            def body(i, slot, ffn, nxt):
                if i < 0:
                    turn(0)
                    for c in range(NCH):
                        weights(c)
                    pe.wait_ge(w_lo, NCH)
                    return
                for k in range(FK):
                    if ffn:
                        if k == 0:
                            pe.wait_ge(z_lo, DH * (i + 1))
                        up(i, k, slot)
                    m = FK * i + k - 2
                    if m >= 0 and m < FK * NGR:
                        down(m // FK, m % FK)
                    if nxt and k == 4:
                        turn(i + 1)

            over_groups(body)

        @block.scalar
        def _(act):
            def weights(c):
                act.wait_ge(w_out, c + 1)
                dst, (a, b) = weight_place(c, fc_hi, pj_hi)
                nc.scalar.copy(dst, p_h[c % 2][:].rearrange("p (a b) -> p a b", a=a)).then_inc(w_hi, 1)

            def turn(i, slot):
                for h in range(DH):
                    act.wait_ge(turned, DH * i + h + 1)
                    part(act, up_out, FK * (i - 1))
                    nc.scalar.copy(zT_hi[:, slot, h, :], p_t[h][:]).then_inc(z_hi, 1)

            def body(i, slot, ffn, nxt):
                if i < 0:
                    turn(0, 0)
                    for c in range(NCH):
                        weights(c)
                    return
                for k in range(FK):
                    if ffn:
                        n = FK * i + k
                        act.wait_ge(up_out, n + 1)
                        part(act, sq_done, n - 1)
                        nc.scalar.activation(rect[:, k % 2], p_h[k % 2][:], ACT.Relu).then_inc(rect_done, 1)
                        act.wait_ge(sq_done, n + 1)
                        part(act, down_out, n - 1)
                        nc.scalar.copy(gT_hi[:, k % 2], sq[:, k % 2]).then_inc(g_hi, 1)
                    if nxt and k == 4:
                        turn(i + 1, 1 - slot)

            over_groups(body)

        @block.gpsimd
        def _(pool):
            link = Link(pool, pool_link)

            def body(i, slot, ffn, nxt):
                if nxt:
                    pool.wait_ge(norm_stat, i + 2)
                    link(nc.gpsimd.tensor_scalar(var[:], mv[:, :, 1], 1.0, LN_EPS, ALU.mult, ALU.add))
                    nc.gpsimd.tensor_tensor(rstd[:], var[:], sb["neghalf"][:, 0:GT], ALU.pow).then_inc(norm_rstd, 1)
                if i < 0:
                    for c in range(NCH):
                        w = Wf[:, c * CH:(c + 1) * CH]
                        pool.wait_ge(deq_done, c + 1)
                        link(nc.gpsimd.tensor_tensor(moved[:, c % 2], deq[:, c % 2], w, ALU.subtract))
                        part(pool, w_out, c - 1)
                        nc.gpsimd.tensor_tensor(wq[:, c % 2], w, moved[:, c % 2], ALU.add).then_inc(wq_done, 1)

            over_groups(body)

        @block.vector
        def _(dve):
            link = Link(dve, dve_link)

            def dequantise(c):
                w = Wf[:, c * CH:(c + 1) * CH].rearrange("p (a b) -> p a b", b=QBLK)

                def wide(s):
                    return s[:, c * CB:(c + 1) * CB].unsqueeze(2).to_broadcast([P, CB, QBLK])

                def of(z):
                    return z[:, c % 2].rearrange("p (a b) -> p a b", b=QBLK)

                link(nc.vector.tensor_tensor(of(unit), w, wide(step_inv), ALU.mult))
                link(nc.vector.tensor_scalar(tick[:, c % 2], unit[:, c % 2], MAGIC, MAGIC - QMAX, ALU.add, ALU.max))
                link(nc.vector.tensor_scalar(near[:, c % 2], tick[:, c % 2], MAGIC + QMAX, -MAGIC, ALU.min, ALU.add))
                part(dve, wq_done, c - 1)
                nc.vector.tensor_tensor(of(deq), of(near), wide(step), ALU.mult).then_inc(deq_done, 1)

            def weights(c):
                dve.wait_ge(w_hi, c + 1)
                lo, (a, b) = weight_place(c, fc_lo, pj_lo)
                hi, _ = weight_place(c, fc_hi, pj_hi)
                nc.vector.tensor_tensor(lo, p_h[c % 2][:].rearrange("p (a b) -> p a b", a=a), hi, ALU.subtract
                                        ).then_inc(w_lo, 1)

            def stat(i):
                for t in range(GT):
                    last = nc.vector.bn_stats(stats[:, t, :], X[:, GT * i + t, :])
                link(last)
                for t in range(GT):
                    last = nc.vector.bn_aggr(mv[:, t, :], stats[:, t, :])
                last.then_inc(norm_stat, 1)

            def normed(i):
                dve.wait_ge(norm_rstd, i + 1)
                part(dve, turned, DH * i)
                for t in range(GT):
                    last = nc.vector.tensor_scalar(xn[:, t, :], X[:, GT * i + t, :], mv[:, t, 0:1], rstd[:, t:t + 1],
                                                   ALU.subtract, ALU.mult)
                last.then_inc(norm_done, 1)

            def turn(i, slot):
                for h in range(DH):
                    dve.wait_ge(z_hi, DH * i + h + 1)
                    nc.vector.tensor_tensor(zT_lo[:, slot, h, :], p_t[h][:], zT_hi[:, slot, h, :], ALU.subtract
                                            ).then_inc(z_lo, 1)

            def square(i, k):
                n = FK * i + k
                dve.wait_ge(rect_done, n + 1)
                part(dve, g_lo, n - 1)
                nc.vector.tensor_tensor(sq[:, k % 2], rect[:, k % 2], rect[:, k % 2], ALU.mult).then_inc(sq_done, 1)

            def rest(i, k):
                n = FK * i + k
                dve.wait_ge(g_hi, n + 1)
                nc.vector.tensor_tensor(gT_lo[:, k % 2], sq[:, k % 2], gT_hi[:, k % 2], ALU.subtract
                                        ).then_inc(g_lo, 1)

            def add(i):
                dve.wait_ge(down_out, FK * (i + 1))
                for s in range(2):
                    here = X[:, GT * i + 2 * s:GT * i + 2 * s + 2, :]
                    last = nc.vector.tensor_tensor(here, p_y[s][:], here, ALU.add)
                last.then_inc(y_added, 1)

            def body(i, slot, ffn, nxt):
                if i < 0:
                    stat(0)
                    link(nc.vector.tensor_tensor(step[:], sb["base"][:], sb["best"][:], ALU.mult))
                    link(nc.vector.reciprocal(step_inv[:], step[:]))
                    dequantise(0)
                    normed(0)
                    dequantise(1)
                    turn(0, 0)
                    for c in range(NCH):
                        weights(c)
                        if c + 2 < NCH:
                            dequantise(c + 2)
                    return
                if nxt:
                    stat(i + 1)
                for k in range(FK):
                    if ffn:
                        square(i, k)
                        if nxt and k == 2:
                            normed(i + 1)
                        rest(i, k)
                    if i > 0 and k == 1:
                        add(i - 1)
                    if nxt and k == 4:
                        turn(i + 1, 1 - slot)

            over_groups(body)

        @block.sync
        def _(sp):
            for i in range(NGR):
                sp.wait_ge(y_added, i + 1)
                for s in range(GT // TT):
                    b = GT // TT * i + s
                    sp.dma_start(out[b].rearrange("(t p) d -> p t d", p=P), X[:, TT * b:TT * (b + 1), :]
                                 ).then_inc(stored, 16)
            sp.wait_ge(stored, 16 * NB)


def program(nc, out, **dr):
    with ExitStack() as ctx:
        sb = {}

        def keep(name, shape, dt, where=None):
            sb[name] = (where or ctx).enter_context(nc.sbuf_tensor(f"{name}", shape, dt))

        keep("X", [P, NB * TT, D], F32)
        keep("W", [P, 2, 2048], F32)
        keep("wq_hi", [P, DH, NH * HD], BF16)
        keep("wq_lo", [P, DH, NH * HD], BF16)
        keep("wkv_hi", [P, DH, NG * 2 * HD], BF16)
        keep("wkv_lo", [P, DH, NG * 2 * HD], BF16)
        keep("wo_hi", [P, NH, D], BF16)
        keep("wo_lo", [P, NH, D], BF16)
        keep("xT_hi", [P, NB, DH, S], FP16)
        keep("xT_lo", [P, NB, DH, S], FP16)
        keep("kcT_hi", [P, NG, NB * T], BF16)
        keep("kcT_lo", [P, NG, NB * T], BF16)
        keep("vc_hi", [T, NB, NG, HD], BF16)
        keep("vc_lo", [T, NB, NG, HD], BF16)
        keep("cosw", [P, 2, TT, HD], F32)
        keep("sinw", [P, 2, TT, HD], F32)
        keep("shrinks", [P, 2, NSHRINK], F32)
        keep("ident", [P, P], F32)
        keep("ident16", [P, P], BF16)
        keep("causal", [P, P], BF16)
        keep("neghalf", [P, 16], F32)
        keep("mag", [P, NBLK * QBLK], F32)
        keep("unit", [P, 2, Search.CH], F32)
        keep("cur", [P, 2, 1], F32)
        for name in ("err", "best_err", "upd", "stay", "base", "best"):
            keep(name, [P, NBLK], F32)
        keep("magic", [P, 1], F32)
        with ExitStack() as early:
            keep("w4", [P, 2, 2048], BF16, early)
            keep("ctxT_hi", [P, DH, NB * T], BF16, early)
            keep("ctxT_lo", [P, DH, NB * T], BF16, early)
            keep("ctx_hi", [T, NB, D], BF16, early)
            keep("ctx_lo", [T, NB, D], BF16, early)
            keep("keep", [P, NB, T], F32, early)
            keep("drop", [P, NB, T], F32, early)
            keep("valid", [P, NB], F32, early)
            keep("rope", [P, 2, TT, HD], F32, early)
            keep("norms", [P, 2, HD], F32, early)
            keep("up_b", [P, FK], F32, early)
            keep("down_b", [P, D], F32, early)
            block_a(nc, dr, sb, ctx)
            block_b(nc, dr, sb)
        block_c(nc, sb)
        block_d(nc, sb, out)


_OUT = (NB, S, D)


def kernel(**inputs):
    import numpy as np
    import concourse.bacc as bacc
    from concourse.bass_utils import run_bass_kernel_spmd as run

    names = {
        "x": "x", "ctx": "ctx_2048", "mask": "mask_BxS2_bk0", "up": "L0_ffn_up_kernel", "up_b": "L0_ffn_up_bias",
        "down": "L0_ffn_down_kernel", "down_b": "L0_ffn_down_bias", "wq": "L1_xattn_wq", "wk": "L1_xattn_wk",
        "wv": "L1_xattn_wv", "wo": "L1_xattn_wo", "wk_ctx": "L1_xattn_wk_ctx", "wv_ctx": "L1_xattn_wv_ctx",
        "q_norm": "L1_xattn_q_norm_w", "k_norm": "L1_xattn_k_norm_w", "w_fc": "L1_ffn_w_fc",
        "w_proj": "L1_ffn_w_proj",
    }
    arrays = {k: np.ascontiguousarray(inputs[n]) for k, n in names.items()}
    freq = np.float32(1.0) / np.float32(10000.0) ** (np.arange(0, HD, 2, dtype=np.float32) / np.float32(HD))
    angle = np.outer(np.arange(S, dtype=np.float32), freq.astype(np.float32)).astype(np.float32)
    arrays["cos"] = np.concatenate([np.cos(angle)] * 2, -1).astype(np.float32)
    arrays["sin"] = np.concatenate([-np.sin(angle), np.sin(angle)], -1).astype(np.float32)
    shrinks = np.linspace(0.4, 1.0, NSHRINK).astype(np.float32)
    arrays["shrinks"] = np.stack([shrinks, np.float32(1.0) / shrinks]).astype(np.float32)
    arrays["ident"] = np.eye(P, dtype=np.float32)

    nc = bacc.Bacc("TRN2", target_bir_lowering=False, num_devices=1)
    given, aps = {}, {}
    for k, a in arrays.items():
        given[f"in_{k}"] = a
        aps[k] = nc.dram_tensor(f"in_{k}", a.shape, mybir.dt.from_np(a.dtype), kind="ExternalInput").ap()
    out = nc.dram_tensor("out", _OUT, F32, kind="ExternalOutput").ap()
    program(nc, out, **aps)
    return run(nc, [given], core_ids=[0]).results[0]["out"]
```

```python
from contextlib import ExitStack

import concourse.bass as bass
from concourse import mybir

P = 128
F32 = mybir.dt.float32
BF16 = mybir.dt.bfloat16
FP16 = mybir.dt.float16
U8 = mybir.dt.uint8
U32 = mybir.dt.uint32
ALU = mybir.AluOpType
ACT = mybir.ActivationFunctionType
AX = mybir.AxisListType.X

NB, S, D = 8, 256, 256
T = 64
DH = D // P
TT = S // P
F = 1024
FK = F // P
NH, NG, HD = 16, 4, 128
REP = NH // NG
NP = NH // 2
LN_EPS, RMS_EPS = 1e-5, 1e-6
QBLK = 64
NBLK = 2 * F * D // QBLK // P
QMAX = 15.0
NSHRINK = 16
MAGIC = 1.5 * 2.0 ** 23
HALF_STEP = 1.5 * 2.0 ** 22
NEG = 1e30


def part(eng, sem, value):
    if not isinstance(value, int) or value > 0:
        eng.wait_ge(sem, value)


class Link:

    def __init__(self, eng, sem, base=0):
        self.eng, self.sem, self.base, self.n = eng, sem, base, 0

    def __call__(self, ins):
        self.n += 1
        ins.then_inc(self.sem, 1)
        self.eng.wait_ge(self.sem, self.base + self.n)


class Search:
    CH = 512
    CB = CH // QBLK
    UNITS = 2 * 2048 // CH
    RING = 4
    LINKS = 3

    def __init__(self, nc, sb, sem, name, first):
        self.nc, self.sb, self.first = nc, sb, first
        self.loaded, self.taken, self.ticked, self.neared, self.scaled, self.off, self.squared, self.summed, \
            self.chosen = (sem(f"{name}_{x}") for x in (
                "shrink_loaded", "shrink_taken", "ticked", "neared", "scaled", "off", "squared", "summed", "chosen"))
        self.gate = sem(f"{name}_search_gate")

    def slot(self, u):
        return self.sb["unit"][:, u % self.RING]

    def mag(self, u):
        return self.sb["mag"][:, u * self.CH:(u + 1) * self.CH]

    def load(self, pool, b, last=False):
        nc, sb = self.nc, self.sb
        part(pool, self.ticked, self.UNITS * b)
        if not last:
            nc.gpsimd.tensor_copy(sb["cur"][:], sb["shrinks"][:, :, bass.ds(self.first + b, 1)]
                                  ).then_inc(self.loaded, 1)
        if not isinstance(b, int) or b > 0:
            nc.gpsimd.tensor_copy(sb["took"][:], sb["shrinks"][:, 0, bass.ds(self.first + b - 1, 1)]
                                  ).then_inc(self.taken, 1)

    def tick(self, act, b, u):
        n = self.UNITS * b + u
        act.wait_ge(self.loaded, b + 1)
        part(act, self.summed, n - self.RING + 1)
        self.nc.scalar.activation(self.slot(u), self.mag(u), ACT.Identity, bias=self.sb["magic"][:, 0:1],
                                  scale=self.sb["cur"][:, 1]).then_inc(self.ticked, 1)

    def near(self, dve, b, u):
        dve.wait_ge(self.ticked, self.UNITS * b + u + 1)
        self.nc.vector.tensor_scalar(self.slot(u), self.slot(u), MAGIC + QMAX, -MAGIC, ALU.min, ALU.add
                                     ).then_inc(self.neared, 1)

    def distance(self, pool, b, u):
        n = self.UNITS * b + u
        pool.wait_ge(self.neared, n + 1)
        pool.sem_inc(self.gate, 1)
        self.nc.gpsimd.tensor_scalar(self.slot(u), self.slot(u), self.sb["cur"][:, 0], 1.0, ALU.mult, ALU.mult
                                     ).then_inc(self.scaled, 1)
        pool.wait_ge(self.scaled, n + 1)
        self.nc.gpsimd.tensor_tensor(self.slot(u), self.slot(u), self.mag(u), ALU.subtract).then_inc(self.off, 1)

    def square(self, act, b, u):
        act.wait_ge(self.off, self.UNITS * b + u + 1)
        self.nc.scalar.activation(self.slot(u), self.slot(u), ACT.Square).then_inc(self.squared, 1)

    def total(self, dve, b, u):
        dve.wait_ge(self.squared, self.UNITS * b + u + 1)
        self.nc.vector.tensor_reduce(self.sb["err"][:, u * self.CB:(u + 1) * self.CB],
                                     self.slot(u).rearrange("p (a b) -> p a b", b=QBLK), AX, ALU.add
                                     ).then_inc(self.summed, 1)

    def choose(self, dve, b, link):
        nc, sb = self.nc, self.sb
        dve.wait_ge(self.summed, self.UNITS * (b + 1))
        link(nc.vector.tensor_tensor(sb["upd"][:], sb["err"][:], sb["best_err"][:], ALU.is_lt))
        nc.vector.tensor_tensor(sb["best_err"][:], sb["best_err"][:], sb["err"][:], ALU.min)
        link(nc.vector.tensor_scalar(sb["stay"][:], sb["upd"][:], -1.0, 1.0, ALU.mult, ALU.add))
        link(nc.vector.tensor_tensor(sb["best"][:], sb["best"][:], sb["stay"][:], ALU.mult))
        dve.wait_ge(self.taken, b + 1)
        nc.vector.scalar_tensor_tensor(sb["best"][:], sb["upd"][:], sb["took"][:, 0:1], sb["best"][:],
                                       ALU.mult, ALU.add).then_inc(self.chosen, 1)
        dve.wait_ge(self.chosen, b + 1)


def block_a(nc, dr, sb, ex):
    with ExitStack() as ctx:
        def local(name, shape, dt):
            return ctx.enter_context(nc.sbuf_tensor(f"a_{name}", shape, dt))

        def sem(name):
            return ctx.enter_context(nc.semaphore(name))

        stage_q = sb["mag"][:].rearrange("p (h n) -> p h n", h=DH)
        stage_o = sb["mag"][:].rearrange("p (k n) -> p k n", n=D)
        stage_c = sb["xT_hi"][:].rearrange("p b h s -> p (b h s)").bitcast(F32
            ).rearrange("p (h g i d) -> p h g i d", h=DH, g=NG, i=2)
        stage_kv = stage_c
        stage_f = sb["W"]
        ctx_rows = local("ctx_rows", [P, NB // 2, D], F32)
        ctx_keys = sb["xT_lo"][0:T].rearrange("p b h s -> p (b h s)").bitcast(F32
            ).rearrange("p (b d) -> p b d", b=NB)
        wc_hi = local("wc_hi", [P, DH, NG * 2 * HD], BF16)
        wc_lo = local("wc_lo", [P, DH, NG * 2 * HD], BF16)
        vf_hi = local("vf_hi", [P, NB // 2, NG, HD], BF16)
        vf_lo = local("vf_lo", [P, NB // 2, NG, HD], BF16)
        knorm = local("knorm", [P, HD], F32)
        mask8 = local("mask8", [P, NB, T], U8)
        CH = 1024
        CHUNKS = 2 * 2048 // CH
        blk = local("blk", [P, CH], F32)
        quant = local("quant", [P, CH], F32)
        step = sb["unit"][:, 0:2].rearrange("p a n -> p (a n)")
        amax = local("amax", [P, CH // 32], F32)
        scale = local("scale", [P, CH // 32], F32)
        top = local("top", [P, CH // 32], F32)
        junk = local("junk", [P, 2, 2, HD], BF16)
        ssq = local("ssq", [P, 8, 2], F32)
        kraw = local("kraw", [P, 2, 2, HD], F32)
        kn = local("kn", [P, 2, 2, HD], F32)
        krms = local("krms", [P, 2, 2], F32)
        kvar = local("kvar", [P, 2, 2], F32)

        p_ctx = [ctx.enter_context(nc.psum_tensor(f"p_ctx{i}", [P, 512], F32)) for i in range(2)]
        p_kv = [ctx.enter_context(nc.psum_tensor(f"p_kv{i}", [P, 2, 2, HD], F32)) for i in range(2)]
        p_kt = [ctx.enter_context(nc.psum_tensor(f"p_kt{i}", [P, 2, P], F32)) for i in range(2)]

        ld_x, ld_ctx, ld_rows = sem("ld_x"), sem("ld_ctx"), sem("ld_rows")
        ld_tab, ld_mask = sem("ld_tab"), sem("ld_mask")
        ld_f = [sem(f"ld_f{c}") for c in range(4)]
        ld_c, ld_q, ld_kv, ld_o = sem("ld_c"), sem("ld_q"), sem("ld_kv"), sem("ld_o")
        ld_small = sem("ld_small")
        hi_done, lo_done = sem("a_hi_done"), sem("a_lo_done")
        rows_t, ctx_hi_done, ctx_lo_done = sem("rows_t"), sem("ctx_hi_done"), sem("ctx_lo_done")
        kv_out, kv_act, kv_dve = sem("kv_out"), sem("kv_act"), sem("kv_dve")
        kn_done, kt_out, kt_hi, kt_lo = sem("kn_done"), sem("kt_out"), sem("kt_hi"), sem("kt_lo")
        fp4_done, fp4_copied = sem("fp4_done"), sem("fp4_copied")
        shifted, dve_link, pool_link = sem("shifted"), sem("a_dve_link"), sem("a_pool_link")
        half_set = sem("half_set")

        block = ctx.enter_context(nc.Block())
        units = [(r, gp) for r in range(NB // 2) for gp in range(2)]

        @block.sync
        def _(sp):
            sp.dma_start(sb["ident"][:], dr["ident"]).then_inc(ld_rows, 16)
            sp.dma_start(ctx_rows[:], dr["ctx"].rearrange("(r b) k d -> (b k) r d", b=2)
                         ).then_inc(ld_rows, 16)
            sp.dma_start(stage_f[:, 0, 0:F], dr["up"][0:P, :]).then_inc(ld_f[0], 16)
            for i, w in enumerate(("wk_ctx", "wv_ctx")):
                for h in range(DH):
                    sp.dma_start(stage_c[:, h, :, i, :],
                                 dr[w][h * P:(h + 1) * P, :].rearrange("p (g d) -> p g d", g=NG)
                                 ).then_inc(ld_c, 16)
            sp.dma_start(stage_f[:, 0, F:2 * F], dr["up"][P:2 * P, :]).then_inc(ld_f[1], 16)
            for i in range(2):
                sp.dma_start(stage_f[:, 1, i * CH:(i + 1) * CH].rearrange("p (k n) -> p k n", n=D),
                             dr["down"][i * 4 * P:(i + 1) * 4 * P].rearrange("(k p) n -> p k n", p=P)
                             ).then_inc(ld_f[2 + i], 16)
            sp.dma_start(sb["X"][:], dr["x"].rearrange("b (t p) d -> p (b t) d", p=P)).then_inc(ld_x, 16)
            sp.dma_start(sb["rope"][:, 0], dr["cos"].rearrange("(t p) d -> p t d", p=P)).then_inc(ld_tab, 16)
            sp.dma_start(sb["rope"][:, 1], dr["sin"].rearrange("(t p) d -> p t d", p=P)).then_inc(ld_tab, 16)
            sp.dma_start(sb["norms"][:, 0], dr["q_norm"].partition_broadcast(P)).then_inc(ld_tab, 16)
            sp.dma_start(sb["norms"][:, 1], dr["k_norm"].partition_broadcast(P)).then_inc(ld_tab, 16)
            with nc.allow_non_contiguous_dma(reason="4 KB, once"):
                sp.dma_start(sb["up_b"][:], dr["up_b"].rearrange("(k p) -> p k", p=P)).then_inc(ld_tab, 16)
            sp.dma_start(sb["down_b"][:], dr["down_b"].partition_broadcast(P)).then_inc(ld_tab, 16)
            sp.dma_start(sb["shrinks"][:], dr["shrinks"].partition_broadcast(P)).then_inc(ld_tab, 16)
            sp.wait_ge(hi_done, 1)
            sp.wait_ge(lo_done, 1)
            for i, w in enumerate(("wk", "wv")):
                for h in range(DH):
                    sp.dma_start(stage_kv[:, h, :, i, :],
                                 dr[w][h * P:(h + 1) * P, :].rearrange("p (g d) -> p g d", g=NG)
                                 ).then_inc(ld_kv, 16)
            sp.wait_ge(hi_done, 3)
            sp.wait_ge(lo_done, 4)
            sp.dma_start(stage_o, dr["wo"].rearrange("(k p) n -> p k n", p=P)).then_inc(ld_o, 16)
            sp.wait_ge(kv_act, len(units))
            sp.wait_ge(kv_dve, len(units))
            for dst, src in ((sb["vc_hi"], vf_hi), (sb["vc_lo"], vf_lo)):
                for half in range(2):
                    sp.dma_start(dst[:].rearrange("k (r b) g d -> k b r (g d)", b=2)[:, half],
                                 src[half * T:(half + 1) * T].rearrange("k r g d -> k r (g d)")
                                 ).then_inc(shifted, 16)
            for s, n in ((ld_x, 1), (ld_tab, 7), (shifted, 4)):
                sp.wait_ge(s, 16 * n)

        @block.scalar
        def _(act):
            act.dma_start(knorm[:], dr["k_norm"].partition_broadcast(P)).then_inc(ld_small, 16)
            act.dma_start(mask8[:], dr["mask"].partition_broadcast(P)).then_inc(ld_mask, 16)
            act.dma_start(ctx_keys, dr["ctx"].rearrange("b k d -> k b d")).then_inc(ld_ctx, 16)
            act.dma_start(stage_q, dr["wq"].rearrange("(h p) n -> p h n", p=P)).then_inc(ld_q, 16)
            act.wait_ge(ld_c, 64)
            nc.scalar.copy(wc_hi[:], stage_c.rearrange("p h g i d -> p h (g i d)")).then_inc(hi_done, 1)
            for h in range(DH):
                act.wait_ge(rows_t, h + 1)
                nc.scalar.copy(sb["ctxT_hi"][:, h], p_ctx[h][:]).then_inc(ctx_hi_done, 1)
            act.wait_ge(ld_ctx, 16)
            nc.scalar.copy(sb["ctx_hi"][:], ctx_keys).then_inc(hi_done, 1)

            def kt_copy(u):
                r, gp = units[u]
                act.wait_ge(kt_out, u + 1)
                nc.scalar.copy(sb["kcT_hi"][:, 2 * gp:2 * gp + 2, r * P:(r + 1) * P], p_kt[u % 2][:]
                               ).then_inc(kt_hi, 1)

            def fp4_copy(c):
                act.wait_ge(fp4_done, c + 1)
                at = slice((c % 2) * CH, (c % 2 + 1) * CH)
                nc.scalar.copy(sb["w4"][:, c // 2, at], stage_f[:, c // 2, at]).then_inc(fp4_copied, 1)

            def wq_hi():
                act.wait_ge(ld_q, 16)
                nc.scalar.copy(sb["wq_hi"][:], stage_q).then_inc(hi_done, 1)

            def wkv_hi():
                act.wait_ge(ld_kv, 64)
                nc.scalar.copy(sb["wkv_hi"][:], stage_kv.rearrange("p h g i d -> p h (g i d)")).then_inc(hi_done, 1)

            def wo_hi():
                act.wait_ge(ld_o, 16)
                nc.scalar.copy(sb["wo_hi"][:], stage_o).then_inc(hi_done, 1)

            beside = {0: [wq_hi], 1: [fp4_copy, 0], 2: [wkv_hi], 3: [fp4_copy, 1], 5: [fp4_copy, 2], 6: [wo_hi],
                      7: [fp4_copy, 3]}
            for u, (r, gp) in enumerate(units):
                act.wait_ge(kv_out, u + 1)
                for i in range(2):
                    nc.scalar.activation(junk[:, u % 2, i], p_kv[u % 2][:, i, 0, :], ACT.Square,
                                         accum_out=ssq[:, u, i:i + 1])
                nc.scalar.copy(vf_hi[:, r, 2 * gp:2 * gp + 2, :], p_kv[u % 2][:, :, 1, :]).then_inc(kv_act, 1)
                if u >= 1:
                    kt_copy(u - 1)
                if u in beside:
                    beside[u][0](*beside[u][1:])
            kt_copy(len(units) - 1)

        @block.gpsimd
        def _(pool):
            link = Link(pool, pool_link)
            nc.gpsimd.memset(sb["magic"][:], MAGIC)
            nc.gpsimd.memset(sb["neghalf"][:], -0.5).then_inc(half_set, 1)
            pool.wait_ge(half_set, 1)
            pool.wait_ge(ld_mask, 16)
            nc.gpsimd.tensor_copy(sb["keep"][:], mask8[:]).then_inc(half_set, 1)
            pool.wait_ge(half_set, 2)
            nc.gpsimd.tensor_scalar(sb["drop"][:], sb["keep"][:], -1.0, NEG, ALU.add, ALU.mult
                                    ).then_inc(half_set, 1)
            nc.gpsimd.memset(sb["causal"][:], 0.0).then_inc(half_set, 1)
            pool.wait_ge(half_set, 4)
            nc.gpsimd.affine_select(out=sb["causal"][:], in_=sb["causal"][:], compare_op=ALU.is_ge, fill=-NEG,
                                    base=0, pattern=[[-1, P]], channel_multiplier=1).then_inc(half_set, 1)
            pool.wait_ge(ld_rows, 32)
            nc.gpsimd.tensor_copy(sb["ident16"][:], sb["ident"][:]).then_inc(half_set, 1)

            def rest(lo, whole, hi, n):
                pool.wait_ge(hi_done, n)
                nc.gpsimd.tensor_tensor(lo, whole, hi, ALU.subtract).then_inc(lo_done, 1)

            rest(wc_lo[:], stage_c.rearrange("p h g i d -> p h (g i d)"), wc_hi[:], 1)

            def kn_unit(u):
                pool.wait_ge(kv_act, u + 1)
                pool.wait_ge(kv_dve, u + 1)
                link(nc.gpsimd.tensor_scalar(kvar[:, u % 2], ssq[:, u], 1.0 / HD, RMS_EPS, ALU.mult, ALU.add))
                link(nc.gpsimd.tensor_tensor(krms[:, u % 2], kvar[:, u % 2], sb["neghalf"][:, 0:2], ALU.pow))
                if u >= 2:
                    pool.wait_ge(kt_out, u - 1)
                for i in range(2):
                    last = nc.gpsimd.tensor_scalar(kn[:, u % 2, i], kraw[:, u % 2, i], krms[:, u % 2, i:i + 1],
                                                   1.0, ALU.mult, ALU.mult)
                last.then_inc(kn_done, 1)

            half = NH // 2
            beside = {0: [(sb["ctx_lo"][:], ctx_keys, sb["ctx_hi"][:], 2)],
                      1: [(sb["wq_lo"][:, 0], stage_q[:, 0], sb["wq_hi"][:, 0], 3)],
                      2: [(sb["wq_lo"][:, 1], stage_q[:, 1], sb["wq_hi"][:, 1], 3)],
                      3: [(sb["wkv_lo"][:], stage_kv.rearrange("p h g i d -> p h (g i d)"), sb["wkv_hi"][:], 4)],
                      **{u: [(sb["wo_lo"][:, k:k + half], stage_o[:, k:k + half], sb["wo_hi"][:, k:k + half], 5)]
                         for u, k in ((6, 0), (7, half))}}
            for u in range(len(units)):
                kn_unit(u)
                for what in beside.get(u, ()):
                    rest(*what)

        @block.vector
        def _(dve):
            link = Link(dve, dve_link)

            wide = [P, CH // 32, 32]
            blocks = lambda x: x.rearrange("p (a b) -> p a b", b=32)

            def fp4_scales(c):
                dve.wait_ge(ld_f[c], 16)
                link(nc.vector.transpose(blk[:], stage_f[:, c // 2, (c % 2) * CH:(c % 2 + 1) * CH]))
                bits = blk[:].bitcast(U32)
                link(nc.vector.tensor_scalar(quant[:].bitcast(U32), bits, 0x7FE00000, None, ALU.bitwise_and))
                nc.vector.tensor_scalar(step.bitcast(U32), bits, 0x7F800000, None, ALU.bitwise_and)
                link(nc.vector.tensor_reduce(amax[:], blocks(quant[:]), AX, ALU.max))
                link(nc.vector.tensor_scalar(scale[:], amax[:], 1e-30, None, ALU.max))
                link(nc.vector.tensor_scalar(top[:].bitcast(U32), scale[:].bitcast(U32), 0x7F800000, None,
                                             ALU.bitwise_and))
                link(nc.vector.tensor_scalar(scale[:], top[:], 0.25, None, ALU.mult))
                link(nc.vector.tensor_scalar(top[:], scale[:], 6.0, None, ALU.mult))

            def fp4_round(c):
                bits = blk[:].bitcast(U32)
                nc.vector.scalar_tensor_tensor(blocks(quant[:]), blocks(quant[:]), 1.0625,
                                               top[:].unsqueeze(2).to_broadcast(wide), ALU.mult, ALU.min)
                link(nc.vector.tensor_tensor(blocks(step), blocks(step), scale[:].unsqueeze(2).to_broadcast(wide),
                                             ALU.max))
                link(nc.vector.scalar_tensor_tensor(quant[:], step, HALF_STEP, quant[:], ALU.mult, ALU.add))
                link(nc.vector.scalar_tensor_tensor(quant[:], step, -HALF_STEP, quant[:], ALU.mult, ALU.add))
                link(nc.vector.scalar_tensor_tensor(step.bitcast(U32), bits, 0x80000000, quant[:].bitcast(U32),
                                                    ALU.bitwise_and, ALU.bitwise_or))
                nc.vector.transpose(stage_f[:, c // 2, (c % 2) * CH:(c % 2 + 1) * CH], step).then_inc(fp4_done, 1)

            def kt_copy(u):
                r, gp = units[u]
                dve.wait_ge(kt_hi, u + 1)
                at = slice(2 * gp, 2 * gp + 2), slice(r * P, (r + 1) * P)
                nc.vector.tensor_tensor(sb["kcT_lo"][:, at[0], at[1]], p_kt[u % 2][:],
                                        sb["kcT_hi"][:, at[0], at[1]], ALU.subtract).then_inc(kt_lo, 1)

            fp4_scales(0)
            fp4_round(0)
            for h in range(DH):
                dve.wait_ge(ctx_hi_done, h + 1)
                nc.vector.tensor_tensor(sb["ctxT_lo"][:, h], p_ctx[h][:], sb["ctxT_hi"][:, h], ALU.subtract
                                        ).then_inc(ctx_lo_done, 1)
            dve.wait_ge(ld_small, 16)
            for u, (r, gp) in enumerate(units):
                if u < 2 * (CHUNKS - 1):
                    (fp4_round if u % 2 else fp4_scales)(1 + u // 2)
                dve.wait_ge(kv_act, u + 1)
                if u >= 2:
                    dve.wait_ge(kn_done, u - 1)
                nc.vector.tensor_tensor(kraw[:, u % 2], p_kv[u % 2][:, :, 0, :],
                                        knorm[:].unsqueeze(1).to_broadcast([P, 2, HD]), ALU.mult)
                nc.vector.tensor_tensor(vf_lo[:, r, 2 * gp:2 * gp + 2, :], p_kv[u % 2][:, :, 1, :],
                                        vf_hi[:, r, 2 * gp:2 * gp + 2, :], ALU.subtract).then_inc(kv_dve, 1)
                if u >= 1:
                    kt_copy(u - 1)
            kt_copy(len(units) - 1)
            dve.wait_ge(half_set, 2)
            nc.vector.tensor_reduce(sb["valid"][:], sb["keep"][:], AX, ALU.max)
            dve.wait_ge(ld_tab, 16 * 7)
            for i in range(2):
                nrm = sb["norms"][:, i].rearrange("p (a d) -> p a d", a=1).to_broadcast([P, TT, HD])
                nc.vector.tensor_tensor(sb["cosw"][:, i], sb["rope"][:, 0], nrm, ALU.mult)
                swapped = sb["norms"][:, i].rearrange("p (a h d) -> p a h d", a=1, h=2)[:, :, ::-1, :]
                for t in range(TT):
                    nc.vector.tensor_tensor(sb["sinw"][:, i, t].rearrange("p (h d) -> p h d", h=2),
                                            sb["rope"][:, 1, t].rearrange("p (h d) -> p h d", h=2),
                                            swapped[:, 0], ALU.mult)

        @block.tensor
        def _(pe):
            pe.wait_ge(ld_rows, 32)
            for h in range(DH):
                for r in range(NB // 2):
                    last = nc.tensor.transpose(p_ctx[h][:, r * P:(r + 1) * P],
                                               ctx_rows[:, r, h * P:(h + 1) * P], sb["ident"][:])
                last.then_inc(rows_t, 1)
            pe.wait_ge(hi_done, 1)
            pe.wait_ge(lo_done, 1)
            pe.wait_ge(ctx_lo_done, DH)

            def kt_unit(u):
                pe.wait_ge(kn_done, u + 1)
                if u >= 2:
                    pe.wait_ge(kt_lo, u - 1)
                for i in range(2):
                    last = nc.tensor.transpose(p_kt[u % 2][:, i, :], kn[:, u % 2, i], sb["ident"][:])
                last.then_inc(kt_out, 1)

            for u, (r, gp) in enumerate(units):
                if u >= 2:
                    pe.wait_ge(kv_act, u - 1)
                    pe.wait_ge(kv_dve, u - 1)
                n = 0
                for h in range(DH):
                    rows = [sb[k][:, h, r * P:(r + 1) * P] for k in ("ctxT_hi", "ctxT_lo")]
                    cols = [w[:, h, gp * 512:(gp + 1) * 512] for w in (wc_hi, wc_lo)]
                    for a, b in ((0, 0), (0, 1), (1, 0)):
                        last = nc.tensor.matmul(p_kv[u % 2][:].rearrange("p g i d -> p (g i d)"),
                                                rows[a], cols[b], start=n == 0, stop=n == 3 * DH - 1)
                        n += 1
                last.then_inc(kv_out, 1)
                if u >= 1:
                    kt_unit(u - 1)
            kt_unit(len(units) - 1)



def block_b(nc, dr, sb):
    with ExitStack() as ctx:
        def local(name, shape, dt):
            return ctx.enter_context(nc.sbuf_tensor(f"b_{name}", shape, dt))

        def sem(name):
            return ctx.enter_context(nc.semaphore(name))

        def bank(name, shape):
            return ctx.enter_context(nc.psum_tensor(f"b_{name}", shape, F32))

        X = sb["X"]
        stats = local("stats", [P, 3, TT, 6], F32)
        mv = local("mv", [P, 3, TT, 2], F32)
        var = local("var", [P, 3, TT], F32)
        rstd = local("rstd", [P, 3, TT], F32)
        xn = local("xn", [P, 3, TT, D], F32)
        aT_hi = local("aT_hi", [P, DH, S], FP16)
        aT_lo = local("aT_lo", [P, DH, S], FP16)
        zT_hi = local("zT_hi", [P, DH, S], FP16)
        zT_lo = local("zT_lo", [P, DH, S], FP16)
        sc = local("sc", [P, TT, T], F32)
        scm = local("scm", [P, TT, T], F32)
        smax = local("smax", [P, TT], F32)
        nbias = local("nbias", [P, TT], F32)
        expd = local("expd", [P, TT, T], F32)
        rsum = local("rsum", [P, TT], F32)
        rinv = local("rinv", [P, TT], F32)
        rval = local("rval", [P, TT], F32)
        prob = local("prob", [P, TT, T], F32)
        pT_hi = local("pT_hi", [T, S], BF16)
        pT_lo = local("pT_lo", [T, S], BF16)
        gel = local("gel", [P, 2, 2, S], F32)
        gT_hi = local("gT_hi", [P, FK, S], BF16)
        gT_lo = local("gT_lo", [P, FK, S], BF16)
        xb = local("xb", [P, TT, D], F32)

        p_t = [bank(f"p_t{i}", [P, DH, S]) for i in range(2)]
        p_h = [bank(f"p_h{i}", [P, 2, S]) for i in range(2)]
        p_s = bank("p_s", [P, TT, T])
        p_r = bank("p_r", [P, TT, D])
        p_y = bank("p_y", [P, TT, D])

        norm_stat, norm_rstd, norm_done = sem("norm_stat"), sem("norm_rstd"), sem("norm_done")
        turned = [sem(f"turned{n}") for n in range(3)]
        turn_hi = [sem(f"turn_hi{n}") for n in range(3)]
        turn_lo = [sem(f"turn_lo{n}") for n in range(3)]
        scored, max_done, bias_done, exp_done, prob_done = (sem(x) for x in (
            "scored", "max_done", "bias_done", "exp_done", "prob_done"))
        probs_turned, probs_hi, probs_lo, read_out, attn_added = (sem(x) for x in (
            "probs_turned", "probs_hi", "probs_lo", "read_out", "attn_added"))
        up_out, gelu_done, gelu_hi, gelu_lo, down_out, ffn_added, bias_added = (sem(x) for x in (
            "up_out", "gelu_done", "gelu_hi", "gelu_lo", "down_out", "ffn_added", "bias_added"))
        ld_w, mag_set = sem("ld_w"), sem("mag_set")
        attn_link, norm_link, search_link, mag_link, pool_link = (sem(x) for x in (
            "attn_link", "norm_link", "b_search_link", "mag_link", "b_pool_link"))
        pe_gate, dve_gate, pool_gate = sem("b_pe_gate"), sem("b_dve_gate"), sem("b_pool_gate")
        find = Search(nc, sb, sem, "b", 0)

        block = ctx.enter_context(nc.Block())

        STEPS = 8

        def unit_before(b, j, lag, ffn, tail):
            if j >= lag:
                return (b, j - lag) if ffn else None
            return (b - 1, j - lag + STEPS) if tail else None

        STAGES = (("head", 3), ("soft", 2), ("read", 1), ("ffn", 0), ("tail", -1))

        def over_batches(eng, body):
            def whole(b):
                body(b, *[0 <= b + ahead < NB for _, ahead in STAGES])

            for b in range(-3, 1):
                whole(b)
            with eng.Fori(1, NB - 3) as b:
                body(b, *[True] * len(STAGES))
            for b in range(NB - 3, NB + 1):
                whole(b)

        @block.sync
        def _(sp):
            sp.dma_start(sb["W"][:, 0, :].rearrange("p (k n) -> p k n", k=FK),
                         dr["w_fc"].rearrange("(k p) n -> p k n", p=P)).then_inc(ld_w, 16)
            sp.dma_start(sb["W"][:, 1, :].rearrange("p (h n) -> p h n", h=DH),
                         dr["w_proj"].rearrange("(h p) n -> p h n", p=P)).then_inc(ld_w, 16)
            sp.wait_ge(ld_w, 32)

        @block.tensor
        def _(pe):
            def turn(n, k, slot):
                for t in range(TT):
                    for h in range(DH):
                        last = nc.tensor.transpose(p_t[slot][:, h, t * P:(t + 1) * P],
                                                   xn[:, n, t, h * P:(h + 1) * P], sb["ident"][:])
                last.then_inc(turned[n], 1)

            def up(b, j):
                pe.wait_ge(turn_lo[1], b + 1)
                part(pe, gelu_done, 4 * b + j - 1)
                for i in range(2):
                    k = 2 * j + i
                    n = 0
                    for h in range(DH):
                        w = sb["w4"][:, 0, h * F + k * P:h * F + (k + 1) * P]
                        for z in (zT_hi, zT_lo):
                            last = nc.tensor.matmul(p_h[j % 2][:, i, :], w, z[:, h, :], start=n == 0,
                                                    stop=n == 2 * DH - 1)
                            n += 1
                last.then_inc(up_out, 1)

            def down(b, j):
                pe.wait_ge(gelu_lo, 4 * b + j + 1)
                if j == 0:
                    part(pe, ffn_added, b)
                for k in (2 * j, 2 * j + 1):
                    for t in range(TT):
                        for g in (gT_hi, gT_lo):
                            first = k == 0 and t == 0 and g is gT_hi
                            last = nc.tensor.matmul(p_y[:, t, :], g[:, k, t * P:(t + 1) * P],
                                                    sb["w4"][:, 1, k * D:(k + 1) * D], start=first,
                                                    stop=k == FK - 1, skip_group_check=True)
                last.then_inc(down_out, 1)

            def score(a):
                pe.wait_ge(turn_lo[0], a + 1)
                part(pe, max_done, a)
                for t in range(TT):
                    n = 0
                    for h in range(DH):
                        q = [z[:, h, t * P:(t + 1) * P] for z in (aT_hi, aT_lo)]
                        c = [sb[k][:, h, bass.ds(a * T, T)] for k in ("ctxT_hi", "ctxT_lo")]
                        for i, j in ((0, 0), (0, 1), (1, 0)):
                            last = nc.tensor.matmul(p_s[:, t, :], q[i], c[j], start=n == 0,
                                                    stop=n == 3 * DH - 1)
                            n += 1
                last.then_inc(scored, 1)

            def turn_probs(a):
                pe.wait_ge(prob_done, a + 1)
                part(pe, turn_lo[1], a)
                pe.sem_inc(pe_gate, 1)
                for t in range(TT):
                    last = nc.tensor.transpose(p_t[1][0:T, 0, t * P:(t + 1) * P], prob[:, t, :], sb["ident"][:])
                last.then_inc(probs_turned, 1)

            def readout(a):
                pe.wait_ge(probs_lo, a + 1)
                part(pe, attn_added, a)
                for t in range(TT):
                    p = [z[:, t * P:(t + 1) * P] for z in (pT_hi, pT_lo)]
                    v = [sb[k][:, bass.ds(a, 1), :].rearrange("k b d -> k (b d)") for k in ("ctx_hi", "ctx_lo")]
                    for n, (i, j) in enumerate(((0, 0), (0, 1), (1, 0))):
                        last = nc.tensor.matmul(p_r[:, t, :], p[i], v[j], start=n == 0, stop=n == 2)
                last.then_inc(read_out, 1)

            def body(b, head, soft, read, ffn, tail):
                for j in range(STEPS):
                    if j == 0 and read:
                        turn_probs(b + 1)
                    if j == 0 and soft:
                        score(b + 2)
                    if j % 2 == 0 and ffn:
                        up(b, j // 2)
                    if j == 1 and tail:
                        down(b - 1, 3)
                    if j >= 3 and j % 2 and ffn:
                        down(b, j // 2 - 1)
                    if j == 2 and read:
                        readout(b + 1)
                    if j == 6:
                        pe.wait_ge(norm_done, b + 4)
                    if j == 6 and head:
                        if tail:
                            part(pe, turn_lo[2], b - 1)
                        turn(0, b + 3, 0)
                    if j == 6 and read:
                        pe.wait_ge(probs_lo, b + 2)
                        turn(1, b + 1, 1)
                    if j == 7 and tail:
                        pe.wait_ge(turn_lo[0], b + 4 if head else NB)
                        turn(2, b - 1, 0)

            over_batches(pe, body)

        @block.scalar
        def _(act):
            def turn(n, k, slot, hi):
                act.wait_ge(turned[n], k + 1)
                nc.scalar.copy(hi, p_t[slot][:]).then_inc(turn_hi[n], 1)

            def gelu(b, j):
                act.wait_ge(up_out, 4 * b + j + 1)
                part(act, gelu_lo, 4 * b + j - 1)
                for i in range(2):
                    k = 2 * j + i
                    last = nc.scalar.activation(gel[:, j % 2, i, :], p_h[j % 2][:, i, :], ACT.Gelu_apprx_tanh,
                                                bias=sb["up_b"][:, k:k + 1])
                last.then_inc(gelu_done, 1)

            def gelu_part(b, j):
                act.wait_ge(gelu_done, 4 * b + j + 1)
                part(act, down_out, 4 * (b - 1) + j + 1)
                nc.scalar.copy(gT_hi[:, 2 * j:2 * j + 2, :], gel[:, j % 2]).then_inc(gelu_hi, 1)

            def exps(a):
                act.wait_ge(bias_done, a + 1)
                for t in range(TT):
                    last = nc.scalar.activation(expd[:, t, :], scm[:, t, :], ACT.Exp, bias=nbias[:, t:t + 1],
                                                scale=D ** -0.5, accum_out=rsum[:, t:t + 1])
                last.then_inc(exp_done, 1)

            def body(b, head, soft, read, ffn, tail):
                if ffn:
                    find.tick(act, b, 0)
                for j in range(STEPS):
                    if j == 0 and read:
                        act.wait_ge(probs_turned, b + 2)
                        nc.scalar.copy(pT_hi[:], p_t[1][0:T, 0, :]).then_inc(probs_hi, 1)
                    if j == 1 and soft:
                        exps(b + 2)
                    if j % 2 and ffn:
                        gelu(b, j // 2)
                    if ffn and j < STEPS - 1:
                        find.tick(act, b, j + 1)
                    if unit_before(b, j, 1, ffn, tail):
                        find.square(act, *unit_before(b, j, 1, ffn, tail))
                    if j % 2 and ffn:
                        gelu_part(b, j // 2)
                    if j == 6 and head:
                        turn(0, b + 3, 0, aT_hi[:])
                    if j == 7 and read:
                        turn(1, b + 1, 1, zT_hi[:])
                    if j == 7 and tail:
                        turn(2, b - 1, 0, sb["xT_hi"][:, bass.ds(b - 1, 1)].rearrange("p b h s -> p (b h) s"))

            over_batches(act, body)

        @block.gpsimd
        def _(pool):
            def body(b, head, soft, read, ffn, tail):
                if ffn:
                    if isinstance(b, int) and b == 0:
                        pool.wait_ge(mag_set, 8)
                    find.load(pool, b)
                elif tail:
                    find.load(pool, b, last=True)
                norms = [n for n, there in enumerate((head, read, tail)) if there]
                for j in range(STEPS):
                    if j == 0 and soft:
                        pool.wait_ge(max_done, b + 3)
                        pool.sem_inc(pool_gate, 1)
                        nc.gpsimd.tensor_scalar(nbias[:], smax[:], -D ** -0.5, 1.0, ALU.mult, ALU.mult
                                                ).then_inc(bias_done, 1)
                    if j == 4:
                        link = Link(pool, pool_link, b + 3)
                        pool.wait_ge(norm_stat, b + 4)
                        pool.sem_inc(pool_gate, 1)
                        at = slice(norms[0], norms[-1] + 1)
                        half = sb["neghalf"][:, 0:len(norms) * TT].rearrange("p (m t) -> p m t", t=TT)
                        link(nc.gpsimd.tensor_scalar(var[:, at], mv[:, at, :, 1], 1.0, LN_EPS, ALU.mult, ALU.add))
                        nc.gpsimd.tensor_tensor(rstd[:, at], var[:, at], half, ALU.pow).then_inc(norm_rstd, 1)
                    if ffn:
                        find.distance(pool, b, j)
                    if j == 5 and ffn:
                        part(pool, ffn_added, b)
                        pool.wait_ge(attn_added, b + 1)
                        nc.gpsimd.tensor_tensor(xb[:], X[:, bass.ds(b * TT, TT), :],
                                                sb["down_b"][:].unsqueeze(1).to_broadcast([P, TT, D]), ALU.add
                                                ).then_inc(bias_added, 1)

            over_batches(pool, body)

        @block.vector
        def _(dve):
            mags = Link(dve, mag_link)

            def magnitudes(j):
                size = 1024
                quarter = min(j % 5, 3)
                rows = slice(quarter * size, (quarter + 1) * size)
                at = slice(quarter * size // QBLK, (quarter + 1) * size // QBLK)
                blocks = sb["mag"][:, rows].rearrange("p (a b) -> p a b", b=QBLK)
                if j < 4:
                    dve.wait_ge(ld_w, 32)
                    mags(nc.vector.tensor_scalar(sb["mag"][:, rows].bitcast(U32),
                                                 sb["W"][:].rearrange("p m n -> p (m n)")[:, rows].bitcast(U32),
                                                 0x7FFFFFFF, None, ALU.bitwise_and))
                    nc.vector.tensor_reduce(sb["err"][:, at], blocks, AX, ALU.max).then_inc(mag_set, 1)
                elif j == 4:
                    dve.wait_ge(mag_set, 4)
                    mags(nc.vector.tensor_scalar(sb["base"][:], sb["err"][:], 1e-8, 1.0 / QMAX, ALU.max, ALU.mult))
                    nc.vector.memset(sb["best_err"][:], 3e38)
                    nc.vector.memset(sb["best"][:], 1.0)
                    mags(nc.vector.reciprocal(sb["upd"][:], sb["base"][:]))
                else:
                    nc.vector.tensor_tensor(blocks, blocks,
                                            sb["upd"][:, at].unsqueeze(2).to_broadcast([P, size // QBLK, QBLK]),
                                            ALU.mult).then_inc(mag_set, 1)
                    if j == 8:
                        dve.wait_ge(mag_set, 8)

            def stat(norms, link):
                at = [(n, t, b) for n, b in norms.items() for t in range(TT)]
                dve.sem_inc(dve_gate, 1)
                for n, t, b in at:
                    last = nc.vector.bn_stats(stats[:, n, t, :],
                                              X[:, bass.ds(b * TT + t, 1), :].rearrange("p a d -> p (a d)"))
                link(last)
                dve.sem_inc(dve_gate, 1)
                for n, t, b in at:
                    last = nc.vector.bn_aggr(mv[:, n, t, :], stats[:, n, t, :])
                last.then_inc(norm_stat, 1)

            def normed(norms):
                for n, b in norms.items():
                    for t in range(TT):
                        last = nc.vector.tensor_scalar(xn[:, n, t, :],
                                                       X[:, bass.ds(b * TT + t, 1), :].rearrange("p a d -> p (a d)"),
                                                       mv[:, n, t, 0:1], rstd[:, n, t:t + 1],
                                                       ALU.subtract, ALU.mult)
                last.then_inc(norm_done, 1)

            def turn(n, k, slot, lo, hi):
                dve.wait_ge(turn_hi[n], k + 1)
                nc.vector.tensor_tensor(lo, p_t[slot][:], hi, ALU.subtract).then_inc(turn_lo[n], 1)

            def gelu_rest(b, j):
                dve.wait_ge(gelu_hi, 4 * b + j + 1)
                nc.vector.tensor_tensor(gT_lo[:, 2 * j:2 * j + 2, :], gel[:, j % 2], gT_hi[:, 2 * j:2 * j + 2, :],
                                        ALU.subtract).then_inc(gelu_lo, 1)

            def body(b, head, soft, read, ffn, tail):
                wide = [P, TT, T]
                link = Link(dve, attn_link, 4 * (b + 2))
                norms = {n: b + ahead for n, (there, ahead) in enumerate(((head, 3), (read, 1), (tail, -1))) if there}
                for j in range(STEPS):
                    if j == 0 and soft:
                        a = b + 2
                        dve.wait_ge(scored, a + 1)
                        link(nc.vector.tensor_tensor(sc[:], p_s[:],
                                                     sb["keep"][:, bass.ds(a, 1), :].to_broadcast(wide), ALU.mult))
                        link(nc.vector.tensor_tensor(scm[:], sc[:],
                                                     sb["drop"][:, bass.ds(a, 1), :].to_broadcast(wide), ALU.add))
                        nc.vector.tensor_reduce(smax[:], scm[:], AX, ALU.max).then_inc(max_done, 1)
                    if j == 0 and read:
                        dve.wait_ge(probs_hi, b + 2)
                        nc.vector.tensor_tensor(pT_lo[:], p_t[1][0:T, 0, :], pT_hi[:], ALU.subtract
                                                ).then_inc(probs_lo, 1)
                    if j == 2 and soft:
                        a = b + 2
                        dve.wait_ge(exp_done, a + 1)
                        link(nc.vector.reciprocal(rinv[:], rsum[:]))
                        link(nc.vector.tensor_tensor(rval[:], rinv[:],
                                                     sb["valid"][:, bass.ds(a, 1)].to_broadcast([P, TT]), ALU.mult))
                        nc.vector.tensor_tensor(prob[:], expd[:], rval[:].unsqueeze(2).to_broadcast(wide), ALU.mult
                                                ).then_inc(prob_done, 1)
                    if ffn:
                        find.near(dve, b, j)
                    elif isinstance(b, int) and b in (-2, -1) and j < (5 if b == -2 else 4):
                        magnitudes(j if b == -2 else 5 + j)
                    if j == 0 and tail:
                        gelu_rest(b - 1, 3)
                    if j >= 2 and j % 2 == 0 and ffn:
                        gelu_rest(b, j // 2 - 1)
                    if j == 2 and tail:
                        dve.wait_ge(down_out, 4 * b)
                        dve.wait_ge(bias_added, b)
                        nc.vector.tensor_tensor(X[:, bass.ds((b - 1) * TT, TT), :], p_y[:], xb[:], ALU.add
                                                ).then_inc(ffn_added, 1)
                    at = unit_before(b, j, 2, ffn, tail)
                    if at:
                        find.total(dve, *at)
                        if at[1] == find.UNITS - 1:
                            find.choose(dve, at[0], Link(dve, search_link, find.LINKS * at[0]))
                    if j == 3 and read:
                        dve.wait_ge(read_out, b + 2)
                        here = X[:, bass.ds((b + 1) * TT, TT), :]
                        nc.vector.tensor_tensor(here, p_r[:], here, ALU.add).then_inc(attn_added, 1)
                    if j == 3:
                        if read:
                            dve.wait_ge(attn_added, b + 2)
                        if tail:
                            dve.wait_ge(ffn_added, b)
                        stat(norms, Link(dve, norm_link, b + 3))
                    if j == 5:
                        dve.wait_ge(norm_rstd, b + 4)
                        for n, a in norms.items():
                            part(dve, turned[n], a)
                        normed(norms)
                    if j == 7 and head:
                        turn(0, b + 3, 0, aT_lo[:], aT_hi[:])
                    if j == 7 and read:
                        turn(1, b + 1, 1, zT_lo[:], zT_hi[:])
                if tail:
                    xt = [sb[k][:, bass.ds(b - 1, 1)].rearrange("p b h s -> p (b h) s") for k in ("xT_lo", "xT_hi")]
                    turn(2, b - 1, 0, *xt)

            over_batches(dve, body)


def block_c(nc, sb):
    with ExitStack() as ctx:
        def local(name, shape, dt):
            return ctx.enter_context(nc.sbuf_tensor(f"c_{name}", shape, dt))

        def sem(name):
            return ctx.enter_context(nc.semaphore(name))

        def bank(name, shape):
            return ctx.enter_context(nc.psum_tensor(f"c_{name}", shape, F32))

        X = sb["X"]
        ROW = [T + P * (t + 1) for t in range(TT)]
        OFF = [0, ROW[0]]
        qT_hi = local("qT_hi", [P, NH, S], BF16)
        qT_lo = local("qT_lo", [P, NH, S], BF16)
        kT_hi = local("kT_hi", [P, NG, S], BF16)
        kT_lo = local("kT_lo", [P, NG, S], BF16)
        v_hi = local("v_hi", [P, TT, NG, HD], BF16)
        v_lo = local("v_lo", [P, TT, NG, HD], BF16)
        rc = local("rc", [P, REP + 1, HD], F32)
        rs = local("rs", [P, REP + 1, HD], F32)
        rot = local("rot", [P, 2, REP + 1, HD], F32)
        junk = local("junk", [P, REP, HD], BF16)
        ssq = local("ssq", [P, REP + 1], F32)
        mean = local("mean", [P, REP + 1], F32)
        rms = local("rms", [P, REP + 1], F32)
        qrms = local("qrms", [P, NH, TT], F32)
        smax = local("smax", [P, 2, TT], F32)
        nbias = local("nbias", [P, 2, 2, TT], F32)
        rsum = local("rsum", [P, 2, 2, TT], F32)
        rinv = local("rinv", [P, 2, 2, TT], F32)
        prob = local("prob", [P, 2, 2, sum(ROW)], F32)
        pT_hi = local("pT_hi", [P, 2, 3, 2 * S], BF16)
        pT_lo = local("pT_lo", [P, 2, 3, 2 * S], BF16)
        oT_hi = local("oT_hi", [P, 2, 2 * S], BF16)
        oT_lo = local("oT_lo", [P, 2, 2 * S], BF16)

        p_p = bank("p_p", [P, REP, HD])
        p_x = bank("p_x", [P, REP, P])
        p_s = [bank(f"p_s{i}", [P, 512]) for i in range(2)]
        p_t = [bank(f"p_t{i}", [P, 2 * S]) for i in range(2)]
        p_o = bank("p_o", [P, 2, S])
        p_y = bank("p_y", [P, TT, D])

        proj_out, proj_act, proj_dve, rot_done = (sem(x) for x in ("proj_out", "proj_act", "proj_dve", "rot_done"))
        x_out, x_hi, x_lo, q_scaled = (sem(x) for x in ("x_out", "x_hi", "x_lo", "q_scaled"))
        scored, bias_done, exp_done, inv_done, prob_done = (sem(x) for x in (
            "c_scored", "c_bias_done", "c_exp_done", "inv_done", "c_prob_done"))
        t_out, t_hi, t_lo, o_out, o_hi, o_lo = (sem(x) for x in ("t_out", "t_hi", "t_lo", "o_out", "o_hi", "o_lo"))
        wo_done, y_added = sem("wo_done"), sem("y_added")
        max_done, search_link, pool_link = sem("c_max_done"), sem("c_search_link"), sem("c_pool_link")
        pe_gate, pool_gate = sem("c_pe_gate"), sem("c_pool_gate")
        find = Search(nc, sb, sem, "c", NB)

        block = ctx.enter_context(nc.Block())

        LAG = 3

        def over_batches(eng, body):
            body(-1, False, True)
            body(0, True, True)
            with eng.Fori(1, NB - 1) as b:
                body(b, True, True)
            body(NB - 1, True, False)

        def made(b, j, attn, nxt):
            if j < 0:
                return (1, b) if attn else None
            if j < 4:
                return (2 + j // 2, b) if attn else None
            return ((j - 4) // 2, b + 1) if nxt and j < NP else None

        def steps(b, attn, nxt):
            for j in range(NP if nxt else NP + LAG):
                def pair(lag):
                    k = j - lag
                    if not attn or k >= NP or (k < 0 and isinstance(b, int) and b == 0):
                        return None
                    return (b, k) if k >= 0 else (b - 1, k + NP)

                ahead = (b, j + 1) if attn and j < NP - 1 else (b + 1, 0) if nxt and j == NP - 1 else None
                yield j, made(b, j, attn, nxt), made(b, j - 1, attn, nxt), pair, ahead

        @block.tensor
        def _(pe):
            def project(g, B, t, kv):
                n = 2 * (2 * (NG * B + g) + t) + kv
                part(pe, proj_act, n)
                part(pe, proj_dve, n)
                rows = [sb[k][:, bass.ds(B, 1)].rearrange("p b h s -> p (b h) s") for k in ("xT_hi", "xT_lo")]
                wide = 2 * HD if kv else REP * HD
                w = [sb[k][:, :, g * wide:(g + 1) * wide] for k in (("wkv_hi", "wkv_lo") if kv else ("wq_hi", "wq_lo"))]
                out = p_p[:].rearrange("p a d -> p (a d)")[:, 0:wide]
                i = 0
                for h in range(DH):
                    for a, c in ((0, 0), (0, 1), (1, 0)):
                        last = nc.tensor.matmul(out, rows[a][:, h, t * P:(t + 1) * P], w[c][:, h, :],
                                                start=i == 0, stop=i == 3 * DH - 1)
                        i += 1
                last.then_inc(proj_out, 1)

            def turn(g, B, t, kv):
                n = 2 * (2 * (NG * B + g) + t) + kv
                pe.wait_ge(rot_done, n + 1)
                part(pe, x_lo, n)
                for r in ([REP] if kv else range(REP)):
                    last = nc.tensor.transpose(p_x[:, r % REP, :], rot[:, t, r, :], sb["ident"][:])
                last.then_inc(x_out, 1)

            def score(b, j, i):
                g = j * 2 // REP
                h = 2 * j + i
                pe.wait_ge(x_lo, 4 * (NG * b + g) + 4)
                part(pe, exp_done, 2 * (NP * b + j - 1) + i + 1)
                for t in range(TT):
                    out = p_s[i][:, OFF[t]:OFF[t] + ROW[t]]
                    q = [z[:, h, t * P:(t + 1) * P] for z in (qT_hi, qT_lo)]
                    k = [z[:, g, 0:ROW[t] - T] for z in (kT_hi, kT_lo)]
                    kc = [sb[z][:, g, bass.ds(b * T, T)] for z in ("kcT_hi", "kcT_lo")]
                    for n, (x, y) in enumerate(((0, 0), (0, 1), (1, 0))):
                        nc.tensor.matmul(out[:, 0:T], q[x], kc[y], start=n == 0, stop=n == 2,
                                         skip_group_check=True)
                        last = nc.tensor.matmul(out[:, T:ROW[t]], q[x], k[y], start=False, stop=n == 2,
                                                skip_group_check=True)
                        if n == 0:
                            nc.tensor.matmul(out[:, ROW[t] - P:ROW[t]], sb["ident16"][:], sb["causal"][:],
                                             start=False, stop=False, skip_group_check=True)
                last.then_inc(scored, 1)

            def turn_probs(b, j, u):
                n = 3 * (NP * b + j) + u
                pe.wait_ge(prob_done, 2 * (NP * b + j) + 2)
                part(pe, t_lo, n - 1)
                if u == 0:
                    pe.sem_inc(pe_gate, 1)
                out = p_t[(j + u) % 2]
                for i in range(2):
                    for t in range(TT):
                        if u == 2 and t == 0:
                            continue
                        lo, wide = (0, T) if u == 0 else (T + (u - 1) * P, P)
                        col = i * P if u == 2 else i * S + t * P
                        last = nc.tensor.transpose(out[0:wide, col:col + P],
                                                   prob[:, j % 2, i, OFF[t] + lo:OFF[t] + lo + wide],
                                                   sb["ident"][:])
                last.then_inc(t_out, 1)

            def values(b, j):
                g = j * 2 // REP
                pe.wait_ge(t_lo, 3 * (NP * b + j) + 3)
                part(pe, o_lo, NP * b + j)
                out = p_o[:].rearrange("p i s -> p (i s)")
                own = [[z[:, u, g, :] for z in (v_hi, v_lo)] for u in range(TT)]
                con = [sb[z][:, bass.ds(b, 1), g, :].rearrange("k b d -> k (b d)") for z in ("vc_hi", "vc_lo")]
                for u, (rows, wide, v) in enumerate(((P, 2 * S, own[0]), (T, 2 * S, con), (P, S, own[1]))):
                    at = (1, 0, 2)[u]
                    p = [z[0:rows, j % 2, at, 0:wide] for z in (pT_hi, pT_lo)]
                    dst = out if u < 2 else p_o[:, :, P:S]
                    for n, (x, y) in enumerate(((0, 0), (0, 1), (1, 0))):
                        rhs = p[y] if u < 2 else p[y].rearrange("p (i s) -> p i s", i=2)
                        last = nc.tensor.matmul(dst, v[x], rhs, start=u == 0 and n == 0,
                                                stop=u == 2 and n == 2, skip_group_check=True)
                last.then_inc(o_out, 1)

            def finish(b, j):
                pe.wait_ge(o_lo, NP * b + j + 1)
                if j == 0:
                    part(pe, y_added, b)
                for i in range(2):
                    h = 2 * j + i
                    for t in range(TT):
                        at = slice(i * S + t * P, i * S + (t + 1) * P)
                        o = [z[:, j % 2, at] for z in (oT_hi, oT_lo)]
                        w = [sb[k][:, h, :] for k in ("wo_hi", "wo_lo")]
                        for n, (x, y) in enumerate(((0, 0), (0, 1), (1, 0))):
                            last = nc.tensor.matmul(p_y[:, t, :], o[x], w[y],
                                                    start=j == 0 and i == 0 and t == 0 and n == 0,
                                                    stop=h == NH - 1 and n == 2, skip_group_check=True)
                last.then_inc(wo_done, 1)

            def body(b, attn, nxt):
                for j, now, before, pair, ahead in steps(b, attn, nxt):
                    t = j % 2
                    if pair(1):
                        turn_probs(*pair(1), 0)
                    if now:
                        project(*now, t, 0)
                    if pair(1):
                        turn_probs(*pair(1), 1)
                    if before:
                        turn(*before, 1 - t, 0)
                    if ahead:
                        score(*ahead, 0)
                    if pair(3):
                        finish(*pair(3))
                    if now:
                        project(*now, t, 1)
                    if pair(1):
                        turn_probs(*pair(1), 2)
                    if ahead:
                        score(*ahead, 1)
                    if before:
                        turn(*before, 1 - t, 1)
                    if pair(2):
                        values(*pair(2))

            over_batches(pe, body)

        @block.scalar
        def _(act):
            def squares(g, B, t, kv):
                n = 2 * (NG * B + g) + t
                act.wait_ge(proj_out, 2 * n + kv + 1)
                part(act, q_scaled, n)
                for r in range(1 if kv else REP):
                    at = REP if kv else r
                    last = nc.scalar.activation(junk[:, r], p_p[:, r, :], ACT.Square, accum_out=ssq[:, at:at + 1])
                if kv:
                    part(act, o_out, NP * (B - 1) + 2 * g + 2)
                    last = nc.scalar.copy(v_hi[:, t, g, :], p_p[:, 1, :])
                last.then_inc(proj_act, 1)

            def turn(g, B, t, kv):
                act.wait_ge(x_out, 2 * (2 * (NG * B + g) + t) + kv + 1)
                part(act, scored, 2 * (NP * (B - 1) + 2 * g + 2))
                if kv:
                    ins = nc.scalar.copy(kT_hi[:, g, t * P:(t + 1) * P], p_x[:, 0, :])
                else:
                    ins = nc.scalar.copy(qT_hi[:, REP * g:REP * (g + 1), t * P:(t + 1) * P], p_x[:])
                ins.then_inc(x_hi, 1)

            def exps(b, j, i):
                n = NP * b + j
                act.wait_ge(bias_done, 2 * n + i + 1)
                part(act, t_out, 3 * (n - 1))
                for t in range(TT):
                    last = nc.scalar.activation(prob[:, j % 2, i, OFF[t]:OFF[t] + ROW[t]],
                                                p_s[i][:, OFF[t]:OFF[t] + ROW[t]], ACT.Exp,
                                                bias=nbias[:, j % 2, i, t:t + 1],
                                                scale=qrms[:, 2 * j + i, t:t + 1],
                                                accum_out=rsum[:, j % 2, i, t:t + 1])
                last.then_inc(exp_done, 1)

            def turn_probs(b, j, u):
                act.wait_ge(t_out, 3 * (NP * b + j) + u + 1)
                part(act, o_out, NP * b + j - 1)
                rows, wide = (T if u == 0 else P), (S if u == 2 else 2 * S)
                nc.scalar.copy(pT_hi[0:rows, j % 2, u, 0:wide], p_t[(j + u) % 2][0:rows, 0:wide]).then_inc(t_hi, 1)

            def values(b, j):
                act.wait_ge(o_out, NP * b + j + 1)
                part(act, wo_done, NP * b + j - 1)
                nc.scalar.copy(oT_hi[:, j % 2], p_o[:].rearrange("p i s -> p (i s)")).then_inc(o_hi, 1)

            def body(b, attn, nxt):
                for j, now, before, pair, ahead in steps(b, attn, nxt):
                    t = j % 2
                    if pair(0):
                        exps(*pair(0), 0)
                    if pair(3):
                        values(*pair(3))
                    if pair(1):
                        turn_probs(*pair(1), 0)
                    if pair(0):
                        exps(*pair(0), 1)
                    if now:
                        squares(*now, t, 0)
                    if pair(1):
                        turn_probs(*pair(1), 1)
                    if pair(0):
                        if j == 0:
                            find.tick(act, b, 0)
                        if j < NP - 1:
                            find.tick(act, b, j + 1)
                    if before:
                        turn(*before, 1 - t, 0)
                    if pair(1):
                        find.square(act, *pair(1))
                    if now:
                        squares(*now, t, 1)
                    if pair(1):
                        turn_probs(*pair(1), 2)
                    if before:
                        turn(*before, 1 - t, 1)

            over_batches(act, body)

        @block.gpsimd
        def _(pool):
            def rotate(g, B, t, kv):
                n = 2 * (NG * B + g) + t
                pool.wait_ge(proj_dve, 2 * n + kv + 1)
                part(pool, x_out, 2 * (n - 2) + kv + 1)
                if not kv:
                    nc.gpsimd.tensor_tensor(rot[:, t, 0:REP], rc[:, 0:REP], rs[:, 0:REP], ALU.add
                                            ).then_inc(rot_done, 1)
                    return
                link = Link(pool, pool_link, 3 * n)
                part(pool, exp_done, 2 * (NP * (B - 1) + 2 * g + 2))
                pool.sem_inc(pool_gate, 1)
                link(nc.gpsimd.tensor_scalar(mean[:], ssq[:], 1.0 / HD, RMS_EPS, ALU.mult, ALU.add))
                link(nc.gpsimd.tensor_tensor(rms[:], mean[:], sb["neghalf"][:, 0:REP + 1], ALU.pow))
                pool.sem_inc(pool_gate, 1)
                nc.gpsimd.tensor_scalar(qrms[:, REP * g:REP * (g + 1), t], rms[:, 0:REP], HD ** -0.5, 1.0,
                                        ALU.mult, ALU.mult).then_inc(q_scaled, 1)
                link(nc.gpsimd.tensor_tensor(rot[:, t, REP], rc[:, REP], rs[:, REP], ALU.add))
                pool.sem_inc(pool_gate, 1)
                nc.gpsimd.tensor_scalar(rot[:, t, REP], rot[:, t, REP], rms[:, REP:REP + 1], 1.0,
                                        ALU.mult, ALU.mult).then_inc(rot_done, 1)

            def normalise(b, j, i):
                pool.wait_ge(inv_done, 2 * (NP * b + j) + i + 1)
                pool.sem_inc(pool_gate, 1)
                for t in range(TT):
                    p = prob[:, j % 2, i, OFF[t]:OFF[t] + ROW[t]]
                    last = nc.gpsimd.tensor_scalar(p, p, rinv[:, j % 2, i, t:t + 1], 1.0, ALU.mult, ALU.mult)
                last.then_inc(prob_done, 1)

            def body(b, attn, nxt):
                if attn:
                    find.load(pool, b)
                for j, now, before, pair, ahead in steps(b, attn, nxt):
                    t = j % 2
                    if j == NP:
                        find.load(pool, NB, last=True)
                    if pair(0):
                        normalise(*pair(0), 0)
                        normalise(*pair(0), 1)
                        find.distance(pool, b, j)
                    if now:
                        rotate(*now, t, 0)
                        rotate(*now, t, 1)

            over_batches(pool, body)

        @block.vector
        def _(dve):
            def rope(g, B, t, kv):
                n = 2 * (NG * B + g) + t
                dve.wait_ge(proj_act, 2 * n + kv + 1)
                part(dve, rot_done, 2 * (n - 1) + kv + 1)
                heads, at = (1, slice(REP, REP + 1)) if kv else (REP, slice(0, REP))
                cosw = sb["cosw"][:, kv, t].unsqueeze(1).to_broadcast([P, heads, HD])
                nc.vector.tensor_tensor(rc[:, at], p_p[:, 0:heads], cosw, ALU.mult)
                src = p_p[:, 0:heads].rearrange("p r (h d) -> p r h d", h=2)[:, :, ::-1, :]
                sinw = sb["sinw"][:, kv, t].rearrange("p (a h d) -> p a h d", a=1, h=2
                                                      ).to_broadcast([P, heads, 2, HD // 2])
                last = nc.vector.tensor_tensor(rs[:, at].rearrange("p r (h d) -> p r h d", h=2), src, sinw, ALU.mult)
                if kv:
                    last = nc.vector.tensor_tensor(v_lo[:, t, g, :], p_p[:, 1, :], v_hi[:, t, g, :], ALU.subtract)
                last.then_inc(proj_dve, 1)

            def turn(g, B, t, kv):
                dve.wait_ge(x_hi, 2 * (2 * (NG * B + g) + t) + kv + 1)
                at = slice(t * P, (t + 1) * P)
                if kv:
                    ins = nc.vector.tensor_tensor(kT_lo[:, g, at], p_x[:, 0, :], kT_hi[:, g, at], ALU.subtract)
                else:
                    heads = slice(REP * g, REP * (g + 1))
                    ins = nc.vector.tensor_tensor(qT_lo[:, heads, at], p_x[:], qT_hi[:, heads, at], ALU.subtract)
                ins.then_inc(x_lo, 1)

            def maxima(b, j, i):
                dve.wait_ge(scored, 2 * (NP * b + j) + i + 1)
                for t in range(TT):
                    last = nc.vector.tensor_reduce(smax[:, i, t:t + 1], p_s[i][:, OFF[t]:OFF[t] + ROW[t]],
                                                   AX, ALU.max)
                last.then_inc(max_done, 1)

            def biases(b, j, i):
                n = 2 * (NP * b + j) + i
                dve.wait_ge(max_done, n + 1)
                dve.wait_ge(q_scaled, 2 * (NG * b + 2 * j // REP) + 2)
                nc.vector.scalar_tensor_tensor(nbias[:, j % 2, i], smax[:, i], -1.0, qrms[:, 2 * j + i],
                                               ALU.mult, ALU.mult).then_inc(bias_done, 1)

            def inverses(b, j, i):
                n = 2 * (NP * b + j) + i
                dve.wait_ge(exp_done, n + 1)
                nc.vector.reciprocal(rinv[:, j % 2, i], rsum[:, j % 2, i]).then_inc(inv_done, 1)

            def turn_probs(b, j, u):
                dve.wait_ge(t_hi, 3 * (NP * b + j) + u + 1)
                rows, wide = (T if u == 0 else P), (S if u == 2 else 2 * S)
                nc.vector.tensor_tensor(pT_lo[0:rows, j % 2, u, 0:wide], p_t[(j + u) % 2][0:rows, 0:wide],
                                        pT_hi[0:rows, j % 2, u, 0:wide], ALU.subtract).then_inc(t_lo, 1)

            def add(b):
                dve.wait_ge(wo_done, NP * (b + 1))
                here = X[:, bass.ds(b * TT, TT), :]
                nc.vector.tensor_tensor(here, p_y[:], here, ALU.add).then_inc(y_added, 1)

            def values(b, j):
                dve.wait_ge(o_hi, NP * b + j + 1)
                nc.vector.tensor_tensor(oT_lo[:, j % 2], p_o[:].rearrange("p i s -> p (i s)"), oT_hi[:, j % 2],
                                        ALU.subtract).then_inc(o_lo, 1)

            def body(b, attn, nxt):
                for j, now, before, pair, ahead in steps(b, attn, nxt):
                    t = j % 2
                    if pair(0):
                        find.near(dve, b, j)
                    if pair(3):
                        values(*pair(3))
                    if pair(1):
                        turn_probs(*pair(1), 0)
                    if pair(0):
                        inverses(*pair(0), 0)
                        inverses(*pair(0), 1)
                    if now:
                        rope(*now, t, 0)
                    if pair(1):
                        turn_probs(*pair(1), 1)
                    if before:
                        turn(*before, 1 - t, 0)
                    if ahead:
                        maxima(*ahead, 0)
                        biases(*ahead, 0)
                    if now:
                        rope(*now, t, 1)
                    if pair(2):
                        find.total(dve, *pair(2))
                    if pair(1):
                        turn_probs(*pair(1), 2)
                    if ahead:
                        maxima(*ahead, 1)
                        biases(*ahead, 1)
                    if before:
                        turn(*before, 1 - t, 1)
                    if j % NP == 2 and pair(3):
                        add(pair(3)[0])
                    if pair(2) and pair(2)[1] == NP - 1:
                        done = pair(2)[0]
                        find.choose(dve, done, Link(dve, search_link, find.LINKS * done))

            over_batches(dve, body)


def block_d(nc, sb, out):
    with ExitStack() as ctx:
        def local(name, shape, dt):
            return ctx.enter_context(nc.sbuf_tensor(f"d_{name}", shape, dt))

        def sem(name):
            return ctx.enter_context(nc.semaphore(name))

        def bank(name, shape):
            return ctx.enter_context(nc.psum_tensor(f"d_{name}", shape, F32))

        X = sb["X"]
        GT = 4
        NGR = NB * TT // GT
        GS = GT * P
        CH, CB = 512, 512 // QBLK
        NCH = 2 * 2048 // CH
        Wf = sb["W"][:].rearrange("p m n -> p (m n)")
        fc_hi = local("fc_hi", [P, DH, F], BF16)
        fc_lo = local("fc_lo", [P, DH, F], BF16)
        pj_hi = local("pj_hi", [P, FK, D], BF16)
        pj_lo = local("pj_lo", [P, FK, D], BF16)
        step = local("step", [P, NBLK], F32)
        step_inv = local("step_inv", [P, NBLK], F32)
        unit = local("unit", [P, 2, CH], F32)
        tick = local("tick", [P, 2, CH], F32)
        near = local("near", [P, 2, CH], F32)
        deq = local("deq", [P, 2, CH], F32)
        moved = local("moved", [P, 2, CH], F32)
        wq = local("wq", [P, 2, CH], F32)
        stats = local("stats", [P, GT, 6], F32)
        mv = local("mv", [P, GT, 2], F32)
        var = local("var", [P, GT], F32)
        rstd = local("rstd", [P, GT], F32)
        xn = local("xn", [P, GT, D], F32)
        zT_hi = local("zT_hi", [P, 2, DH, GS], FP16)
        zT_lo = local("zT_lo", [P, 2, DH, GS], FP16)
        sq = local("sq", [P, 2, GS], F32)
        rect = local("rect", [P, 2, GS], F32)
        gT_hi = local("gT_hi", [P, 2, GS], BF16)
        gT_lo = local("gT_lo", [P, 2, GS], BF16)

        p_t = [bank(f"p_t{h}", [P, GS]) for h in range(DH)]
        p_h = [bank(f"p_h{i}", [P, GS]) for i in range(2)]
        p_y = [bank(f"p_y{i}", [P, 2, D]) for i in range(2)]
        p_w = [bank(f"p_w{i}", [P, CH]) for i in range(2)]

        deq_done, wq_done, w_out, w_hi, w_lo = (sem(x) for x in ("deq_done", "wq_done", "w_out", "w_hi", "w_lo"))
        norm_stat, norm_rstd, norm_done, turned, z_hi, z_lo = (sem(x) for x in (
            "d_norm_stat", "d_norm_rstd", "d_norm_done", "d_turned", "z_hi", "z_lo"))
        up_out, rect_done, sq_done, g_hi, g_lo, down_out, y_added, stored = (sem(x) for x in (
            "d_up_out", "rect_done", "sq_done", "g_hi", "g_lo", "d_down_out", "d_y_added", "stored"))
        dve_link, pool_link = sem("d_dve_link"), sem("d_pool_link")

        block = ctx.enter_context(nc.Block())

        def over_groups(body):
            body(-1, 1, False, True)
            for i in range(NGR):
                body(i, i % 2, True, i + 1 < NGR)
            body(NGR, NGR % 2, False, False)

        MADE = (0, 1, 4, 6, 2, 3, 5, 7)

        def weight_view(c, w):
            if c < NCH // 2:
                return [w[:, i * D + h * P:i * D + (h + 1) * P] for h in range(DH) for i in range(2)]
            return [w[:, i * P:(i + 1) * P] for i in range(4)]

        def weight_place(c, fc, pj):
            if c < NCH // 2:
                return fc[:, :, 2 * c * P:(2 * c + 2) * P], [DH, 2 * P]
            c -= NCH // 2
            h, k = c // 2, 4 * (c % 2)
            return pj[:, k:k + 4, h * P:(h + 1) * P], [4, P]

        @block.tensor
        def _(pe):
            def weights(q):
                pe.wait_ge(wq_done, q + 1)
                part(pe, w_lo, q - 1)
                for n, tile in enumerate(weight_view(MADE[q], wq[:, q % 2])):
                    last = nc.tensor.transpose(p_w[q % 2][:, n * P:(n + 1) * P], tile, sb["ident"][:])
                last.then_inc(w_out, 1)

            def up(i, k, slot):
                n = FK * i + k
                if i == 0:
                    pe.wait_ge(w_lo, MADE.index(k // 2) + 1)
                part(pe, sq_done, n - 1)
                for m, (h, a, c) in enumerate([(h, a, c) for h in range(DH) for a, c in ((0, 0), (0, 1), (1, 0))]):
                    w = (fc_hi, fc_lo)[a][:, h, k * P:(k + 1) * P]
                    z = (zT_hi, zT_lo)[c][:, slot, h, :]
                    last = nc.tensor.matmul(p_h[k % 2][:], w, z, start=m == 0, stop=m == 3 * DH - 1)
                last.then_inc(up_out, 1)

            def down(i, k):
                pe.wait_ge(g_lo, FK * i + k + 1)
                if k == 0:
                    part(pe, y_added, i)
                if i == 0:
                    pe.wait_ge(w_lo, MADE.index(6 + k // 4) + 1)
                for t in range(GT):
                    for m, (a, c) in enumerate(((0, 0), (0, 1), (1, 0))):
                        g = (gT_hi, gT_lo)[a][:, k % 2, t * P:(t + 1) * P]
                        last = nc.tensor.matmul(p_y[t // 2][:, t % 2, :], g, (pj_hi, pj_lo)[c][:, k, :],
                                                start=k == 0 and t % 2 == 0 and m == 0,
                                                stop=k == FK - 1 and m == 2, skip_group_check=True)
                last.then_inc(down_out, 1)

            def turn(i):
                pe.wait_ge(norm_done, i + 1)
                part(pe, z_lo, DH * i)
                for h in range(DH):
                    for t in range(GT):
                        last = nc.tensor.transpose(p_t[h][:, t * P:(t + 1) * P], xn[:, t, h * P:(h + 1) * P],
                                                   sb["ident"][:])
                    last.then_inc(turned, 1)

            def body(i, slot, ffn, nxt):
                if i < 0:
                    turn(0)
                    weights(0)
                    return
                for k in range(FK):
                    if ffn:
                        if k == 0:
                            pe.wait_ge(z_lo, DH * (i + 1))
                        up(i, k, slot)
                    if i == 0 and k + 1 < NCH:
                        weights(k + 1)
                    m = FK * i + k - 2
                    if m >= 0 and m < FK * NGR:
                        down(m // FK, m % FK)
                    if nxt and k == 4:
                        turn(i + 1)

            over_groups(body)

        @block.scalar
        def _(act):
            def weights(q):
                act.wait_ge(w_out, q + 1)
                dst, (a, b) = weight_place(MADE[q], fc_hi, pj_hi)
                nc.scalar.copy(dst, p_w[q % 2][:].rearrange("p (a b) -> p a b", a=a)).then_inc(w_hi, 1)

            def turn(i, slot):
                for h in range(DH):
                    act.wait_ge(turned, DH * i + h + 1)
                    part(act, up_out, FK * (i - 1))
                    nc.scalar.copy(zT_hi[:, slot, h, :], p_t[h][:]).then_inc(z_hi, 1)

            def body(i, slot, ffn, nxt):
                if i < 0:
                    turn(0, 0)
                    weights(0)
                    return
                for k in range(FK):
                    if ffn:
                        n = FK * i + k
                        act.wait_ge(up_out, n + 1)
                        part(act, sq_done, n - 1)
                        nc.scalar.activation(rect[:, k % 2], p_h[k % 2][:], ACT.Relu).then_inc(rect_done, 1)
                        if i == 0 and k + 1 < NCH:
                            weights(k + 1)
                        act.wait_ge(sq_done, n + 1)
                        part(act, down_out, n - 1)
                        nc.scalar.copy(gT_hi[:, k % 2], sq[:, k % 2]).then_inc(g_hi, 1)
                    if nxt and k == 4:
                        turn(i + 1, 1 - slot)

            over_groups(body)

        @block.gpsimd
        def _(pool):
            link = Link(pool, pool_link)

            def body(i, slot, ffn, nxt):
                if nxt:
                    pool.wait_ge(norm_stat, i + 2)
                    link(nc.gpsimd.tensor_scalar(var[:], mv[:, :, 1], 1.0, LN_EPS, ALU.mult, ALU.add))
                    nc.gpsimd.tensor_tensor(rstd[:], var[:], sb["neghalf"][:, 0:GT], ALU.pow).then_inc(norm_rstd, 1)
                if i <= 0:
                    for q in range(3) if i < 0 else range(3, NCH):
                        c = MADE[q]
                        w = Wf[:, c * CH:(c + 1) * CH]
                        pool.wait_ge(deq_done, q + 1)
                        link(nc.gpsimd.tensor_tensor(moved[:, q % 2], deq[:, q % 2], w, ALU.subtract))
                        part(pool, w_out, q - 1)
                        nc.gpsimd.tensor_tensor(wq[:, q % 2], w, moved[:, q % 2], ALU.add).then_inc(wq_done, 1)

            over_groups(body)

        @block.vector
        def _(dve):
            link = Link(dve, dve_link)

            def dequantise(q):
                c = MADE[q]
                w = Wf[:, c * CH:(c + 1) * CH].rearrange("p (a b) -> p a b", b=QBLK)

                def wide(s):
                    return s[:, c * CB:(c + 1) * CB].unsqueeze(2).to_broadcast([P, CB, QBLK])

                def of(z):
                    return z[:, q % 2].rearrange("p (a b) -> p a b", b=QBLK)

                link(nc.vector.tensor_tensor(of(unit), w, wide(step_inv), ALU.mult))
                link(nc.vector.tensor_scalar(tick[:, q % 2], unit[:, q % 2], MAGIC, MAGIC - QMAX, ALU.add, ALU.max))
                link(nc.vector.tensor_scalar(near[:, q % 2], tick[:, q % 2], MAGIC + QMAX, -MAGIC, ALU.min, ALU.add))
                part(dve, wq_done, q - 1)
                nc.vector.tensor_tensor(of(deq), of(near), wide(step), ALU.mult).then_inc(deq_done, 1)

            def weights(q):
                dve.wait_ge(w_hi, q + 1)
                c = MADE[q]
                lo, (a, b) = weight_place(c, fc_lo, pj_lo)
                hi, _ = weight_place(c, fc_hi, pj_hi)
                nc.vector.tensor_tensor(lo, p_w[q % 2][:].rearrange("p (a b) -> p a b", a=a), hi, ALU.subtract
                                        ).then_inc(w_lo, 1)

            def stat(i):
                for t in range(GT):
                    last = nc.vector.bn_stats(stats[:, t, :], X[:, GT * i + t, :])
                link(last)
                for t in range(GT):
                    last = nc.vector.bn_aggr(mv[:, t, :], stats[:, t, :])
                last.then_inc(norm_stat, 1)

            def normed(i):
                dve.wait_ge(norm_rstd, i + 1)
                part(dve, turned, DH * i)
                for t in range(GT):
                    last = nc.vector.tensor_scalar(xn[:, t, :], X[:, GT * i + t, :], mv[:, t, 0:1], rstd[:, t:t + 1],
                                                   ALU.subtract, ALU.mult)
                last.then_inc(norm_done, 1)

            def turn(i, slot):
                for h in range(DH):
                    dve.wait_ge(z_hi, DH * i + h + 1)
                    nc.vector.tensor_tensor(zT_lo[:, slot, h, :], p_t[h][:], zT_hi[:, slot, h, :], ALU.subtract
                                            ).then_inc(z_lo, 1)

            def square(i, k):
                n = FK * i + k
                dve.wait_ge(rect_done, n + 1)
                part(dve, g_lo, n - 1)
                nc.vector.tensor_tensor(sq[:, k % 2], rect[:, k % 2], rect[:, k % 2], ALU.mult).then_inc(sq_done, 1)

            def rest(i, k):
                n = FK * i + k
                dve.wait_ge(g_hi, n + 1)
                nc.vector.tensor_tensor(gT_lo[:, k % 2], sq[:, k % 2], gT_hi[:, k % 2], ALU.subtract
                                        ).then_inc(g_lo, 1)

            def add(i):
                dve.wait_ge(down_out, FK * (i + 1))
                for s in range(2):
                    here = X[:, GT * i + 2 * s:GT * i + 2 * s + 2, :]
                    last = nc.vector.tensor_tensor(here, p_y[s][:], here, ALU.add)
                last.then_inc(y_added, 1)

            def body(i, slot, ffn, nxt):
                if i < 0:
                    stat(0)
                    link(nc.vector.tensor_tensor(step[:], sb["base"][:], sb["best"][:], ALU.mult))
                    link(nc.vector.reciprocal(step_inv[:], step[:]))
                    dequantise(0)
                    normed(0)
                    dequantise(1)
                    turn(0, 0)
                    weights(0)
                    dequantise(2)
                    return
                if nxt:
                    stat(i + 1)
                for k in range(FK):
                    if ffn:
                        square(i, k)
                        if nxt and k == 2:
                            normed(i + 1)
                        if i == 0 and k + 1 < NCH:
                            weights(k + 1)
                        if i == 0 and k + 3 < NCH:
                            dequantise(k + 3)
                        rest(i, k)
                    if i > 0 and k == 1:
                        add(i - 1)
                    if nxt and k == 4:
                        turn(i + 1, 1 - slot)

            over_groups(body)

        @block.sync
        def _(sp):
            for i in range(NGR):
                sp.wait_ge(y_added, i + 1)
                for s in range(GT // TT):
                    b = GT // TT * i + s
                    sp.dma_start(out[b].rearrange("(t p) d -> p t d", p=P), X[:, TT * b:TT * (b + 1), :]
                                 ).then_inc(stored, 16)
            sp.wait_ge(stored, 16 * NB)


def program(nc, out, **dr):
    with ExitStack() as ctx:
        sb = {}

        def keep(name, shape, dt, where=None):
            sb[name] = (where or ctx).enter_context(nc.sbuf_tensor(f"{name}", shape, dt))

        keep("X", [P, NB * TT, D], F32)
        keep("W", [P, 2, 2048], F32)
        keep("wq_hi", [P, DH, NH * HD], BF16)
        keep("wq_lo", [P, DH, NH * HD], BF16)
        keep("wkv_hi", [P, DH, NG * 2 * HD], BF16)
        keep("wkv_lo", [P, DH, NG * 2 * HD], BF16)
        keep("wo_hi", [P, NH, D], BF16)
        keep("wo_lo", [P, NH, D], BF16)
        keep("xT_hi", [P, NB, DH, S], FP16)
        keep("xT_lo", [P, NB, DH, S], FP16)
        keep("kcT_hi", [P, NG, NB * T], BF16)
        keep("kcT_lo", [P, NG, NB * T], BF16)
        keep("vc_hi", [T, NB, NG, HD], BF16)
        keep("vc_lo", [T, NB, NG, HD], BF16)
        keep("cosw", [P, 2, TT, HD], F32)
        keep("sinw", [P, 2, TT, HD], F32)
        keep("shrinks", [P, 2, NSHRINK], F32)
        keep("ident", [P, P], F32)
        keep("ident16", [P, P], BF16)
        keep("causal", [P, P], BF16)
        keep("neghalf", [P, 16], F32)
        keep("mag", [P, NBLK * QBLK], F32)
        keep("unit", [P, Search.RING, Search.CH], F32)
        keep("cur", [P, 2, 1], F32)
        keep("took", [P, 1], F32)
        for name in ("err", "best_err", "upd", "stay", "base", "best"):
            keep(name, [P, NBLK], F32)
        keep("magic", [P, 1], F32)
        with ExitStack() as early:
            keep("w4", [P, 2, 2048], BF16, early)
            keep("ctxT_hi", [P, DH, NB * T], BF16, early)
            keep("ctxT_lo", [P, DH, NB * T], BF16, early)
            keep("ctx_hi", [T, NB, D], BF16, early)
            keep("ctx_lo", [T, NB, D], BF16, early)
            keep("keep", [P, NB, T], F32, early)
            keep("drop", [P, NB, T], F32, early)
            keep("valid", [P, NB], F32, early)
            keep("rope", [P, 2, TT, HD], F32, early)
            keep("norms", [P, 2, HD], F32, early)
            keep("up_b", [P, FK], F32, early)
            keep("down_b", [P, D], F32, early)
            block_a(nc, dr, sb, ctx)
            block_b(nc, dr, sb)
        block_c(nc, sb)
        block_d(nc, sb, out)


_OUT = (NB, S, D)


def kernel(**inputs):
    import numpy as np
    import concourse.bacc as bacc
    from concourse.bass_utils import run_bass_kernel_spmd as run

    names = {
        "x": "x", "ctx": "ctx_2048", "mask": "mask_BxS2_bk0", "up": "L0_ffn_up_kernel", "up_b": "L0_ffn_up_bias",
        "down": "L0_ffn_down_kernel", "down_b": "L0_ffn_down_bias", "wq": "L1_xattn_wq", "wk": "L1_xattn_wk",
        "wv": "L1_xattn_wv", "wo": "L1_xattn_wo", "wk_ctx": "L1_xattn_wk_ctx", "wv_ctx": "L1_xattn_wv_ctx",
        "q_norm": "L1_xattn_q_norm_w", "k_norm": "L1_xattn_k_norm_w", "w_fc": "L1_ffn_w_fc",
        "w_proj": "L1_ffn_w_proj",
    }
    arrays = {k: np.ascontiguousarray(inputs[n]) for k, n in names.items()}
    freq = np.float32(1.0) / np.float32(10000.0) ** (np.arange(0, HD, 2, dtype=np.float32) / np.float32(HD))
    angle = np.outer(np.arange(S, dtype=np.float32), freq.astype(np.float32)).astype(np.float32)
    arrays["cos"] = np.concatenate([np.cos(angle)] * 2, -1).astype(np.float32)
    arrays["sin"] = np.concatenate([-np.sin(angle), np.sin(angle)], -1).astype(np.float32)
    shrinks = np.linspace(0.4, 1.0, NSHRINK).astype(np.float32)
    arrays["shrinks"] = np.stack([shrinks, np.float32(1.0) / shrinks]).astype(np.float32)
    arrays["ident"] = np.eye(P, dtype=np.float32)

    nc = bacc.Bacc("TRN2", target_bir_lowering=False, num_devices=1)
    given, aps = {}, {}
    for k, a in arrays.items():
        given[f"in_{k}"] = a
        aps[k] = nc.dram_tensor(f"in_{k}", a.shape, mybir.dt.from_np(a.dtype), kind="ExternalInput").ap()
    out = nc.dram_tensor("out", _OUT, F32, kind="ExternalOutput").ap()
    program(nc, out, **aps)
    return run(nc, [given], core_ids=[0]).results[0]["out"]
```
